# Optimizing a Trainium2 kernel written in Bass

```python
import numpy as np
import jax
import jax.numpy as jnp

def _softmax(x, axis=-1):
    return jax.nn.softmax(x, axis=axis)

def _gelu(x):
    return jax.nn.gelu(x, approximate=True)

def _silu(x):
    return jax.nn.silu(x)

def _sigmoid(x):
    return jax.nn.sigmoid(x)

def _layernorm(x, axis=-1, eps=1e-05):
    m = jnp.mean(x, axis=axis, keepdims=True)
    v = jnp.var(x, axis=axis, keepdims=True)
    return (x - m) / jnp.sqrt(v + eps)

def _scatter_add(tgt, idx, src, axis=0):
    return tgt.at[idx].add(src)

def _segment_sum(src, seg, n):
    return jax.ops.segment_sum(src, seg, n)
kernel_name = 'mk_xattn_ffn_d4_seqx_r8_e58278'

def setup_inputs(seed: int=0):
    np.random.seed(seed)
    _w = jnp.asarray

    def _rec_inputs():
        import jax
        import jax.numpy as jnp
        _rk = jax.random.key(seed)
        x = 7.22e-05 + 1 * jax.random.normal(jax.random.fold_in(_rk, 1), (8, 128, 512), jnp.float32)
        _lenS = 128 - jax.random.randint(jax.random.fold_in(_rk, 7), (8,), 0, max(1, 128 // 4) + 1, jnp.int32)
        _lenS2 = 128 - jax.random.randint(jax.random.fold_in(_rk, 8), (8,), 0, max(1, 128 // 4) + 1, jnp.int32)
        _ctx_4096P = jax.random.normal(jax.random.fold_in(_rk, 11), (8, 16, 512), jnp.float32)
        _ctx_4096c = jax.random.dirichlet(jax.random.fold_in(_rk, 511), 0.3 * jnp.ones((16,), jnp.float32), (8, 128))
        _ctx_4096t = jnp.einsum('bsk,bkd->bsd', _ctx_4096c, _ctx_4096P)
        _ctx_4096t = _ctx_4096t * jax.lax.rsqrt(jnp.mean(jnp.square(_ctx_4096t)) + 1e-12) * 0.953939
        ctx_4096 = 4.13588e-05 + 0.999923 * (_ctx_4096t + 0.3 * jax.random.normal(jax.random.fold_in(_rk, 611), (8, 128, 512), jnp.float32))
        _validS = jnp.arange(128)[None, :] < _lenS[:, None]
        _validS2 = jnp.arange(128)[None, :] < _lenS2[:, None]
        _causal = jnp.tril(jnp.ones((128, 128), dtype=bool))
        mask_1x1xSxS2_ff0 = jnp.where(jnp.ones((1, 1, 128, 128), dtype=bool), 0.0, -1000000000.0).astype(jnp.float32)
        return (x, ctx_4096, mask_1x1xSxS2_ff0)
    x, ctx_4096, mask_1x1xSxS2_ff0 = _rec_inputs()

    def _L0_xattn_setup():
        import jax, jax.numpy as jnp
        import numpy as np
        DIM = 512
        NUM_HEADS = 32
        NUM_KV_HEADS = 8
        HEAD_DIM = DIM // NUM_HEADS
        KV_DIM = DIM // (NUM_HEADS // NUM_KV_HEADS)
        B, S = (1, 256)
        key = jax.random.key(seed)
        ks = jax.random.split(key, 7)
        w_scale = DIM ** (-0.5)
        return {'query': jax.random.normal(ks[0], (B, S, DIM), jnp.float32), 'key': jax.random.normal(ks[1], (B, S, DIM), jnp.float32), 'value': jax.random.normal(ks[2], (B, S, DIM), jnp.float32), 'Wq': jax.random.normal(ks[3], (DIM, DIM), jnp.float32) * w_scale, 'Wk': jax.random.normal(ks[4], (DIM, KV_DIM), jnp.float32) * w_scale, 'Wv': jax.random.normal(ks[5], (DIM, KV_DIM), jnp.float32) * w_scale, 'Wo': jax.random.normal(ks[6], (DIM, DIM), jnp.float32) * w_scale}
    _L0_xattn_all = _L0_xattn_setup()
    _L0_xattn_in = {k: v for k, v in _L0_xattn_all.items() if k in ('Wq', 'Wk', 'Wv', 'Wo')}
    del _L0_xattn_all

    def _L0_ffn_setup():
        import jax, jax.numpy as jnp
        import numpy as np
        D_IN = 512
        D_OUT = 512
        RANK = 16
        NUM_EXPERTS = 8
        TOP_K = 2
        SCALING = 32.0 / RANK
        key = jax.random.key(seed)
        ks = jax.random.split(key, 6)
        x = jax.random.normal(ks[0], (4, 256, D_IN), dtype=jnp.float32)
        W_base = jax.random.normal(ks[1], (D_OUT, D_IN), dtype=jnp.float32) * (1.0 / np.sqrt(D_IN))
        b_base = jax.random.normal(ks[2], (D_OUT,), dtype=jnp.float32) * 0.01
        W_router = jax.random.normal(ks[3], (NUM_EXPERTS, D_IN), dtype=jnp.float32) * 0.01
        A_stack = jax.random.uniform(ks[4], (NUM_EXPERTS, RANK, D_IN), dtype=jnp.float32, minval=-1.0, maxval=1.0) * (1.0 / np.sqrt(D_IN))
        B_stack = jax.random.normal(ks[5], (NUM_EXPERTS, D_OUT, RANK), dtype=jnp.float32) * 0.02
        return {'x': x, 'W_base': W_base, 'b_base': b_base, 'W_router': W_router, 'A_stack': A_stack, 'B_stack': B_stack}
    _L0_ffn_all = _L0_ffn_setup()
    _L0_ffn_in = {k: v for k, v in _L0_ffn_all.items() if k in ('W_base', 'b_base', 'W_router', 'A_stack', 'B_stack')}
    del _L0_ffn_all

    def _L1_xattn_setup():
        import jax, jax.numpy as jnp
        import numpy as np
        import math
        D_MODEL = 128
        NHEAD = 16
        MAX_SUP = 4
        DK = D_MODEL // NHEAD
        DM = D_MODEL * MAX_SUP
        B, S = (2, 128)
        key = jax.random.key(seed)
        ks = jax.random.split(key, 12)
        std = 0.02
        inp = {'q': jax.random.normal(ks[0], (B, S, DM), jnp.float32), 'k': jax.random.normal(ks[1], (B, S, DM), jnp.float32), 'v': jax.random.normal(ks[2], (B, S, DM), jnp.float32), 'Wq': jax.random.normal(ks[3], (DM, DM), jnp.float32) * std, 'bq': jnp.zeros((DM,), jnp.float32), 'Wk': jax.random.normal(ks[4], (DM, DM), jnp.float32) * std, 'bk': jnp.zeros((DM,), jnp.float32), 'Wv': jax.random.normal(ks[5], (DM, DM), jnp.float32) * std, 'bv': jnp.zeros((DM,), jnp.float32), 'interference': jax.random.normal(ks[6], (NHEAD, MAX_SUP, MAX_SUP), jnp.float32), 'amp': jnp.ones((1,), jnp.float32), 'Wo': jax.random.normal(ks[7], (DM, DM), jnp.float32) * std, 'bo': jnp.zeros((DM,), jnp.float32)}
        return inp
    _L1_xattn_all = _L1_xattn_setup()
    _L1_xattn_in = {k: v for k, v in _L1_xattn_all.items() if k in ('Wq', 'bq', 'Wk', 'bk', 'Wv', 'bv', 'interference', 'amp', 'Wo', 'bo')}
    del _L1_xattn_all

    def _L1_ffn_setup():
        import jax, jax.numpy as jnp
        import numpy as np

        def sparsemax(z):
            E = z.shape[-1]
            z_sorted = -jnp.sort(-z, axis=-1)
            z_cum = jnp.cumsum(z_sorted, axis=-1)
            k = jnp.arange(1, E + 1, dtype=z.dtype)
            support = 1.0 + k * z_sorted > z_cum
            k_z = jnp.sum(support, axis=-1, keepdims=True)
            tau_sum = jnp.take_along_axis(z_cum, k_z.astype(jnp.int32) - 1, axis=-1)
            tau = (tau_sum - 1.0) / k_z.astype(z.dtype)
            return jnp.maximum(z - tau, 0.0)
        key = jax.random.key(seed)
        ks = jax.random.split(key, 6)
        B, S, D_IN, D_OUT, E, R = (8, 256, 512, 512, 8, 16)
        x = jax.random.normal(ks[0], (B, S, D_IN), dtype=jnp.float32)
        W_base = jax.random.normal(ks[1], (D_OUT, D_IN), dtype=jnp.float32) * D_IN ** (-0.5)
        b_base = jax.random.normal(ks[2], (D_OUT,), dtype=jnp.float32) * 0.01
        W_router = jax.random.normal(ks[3], (E, D_IN), dtype=jnp.float32) * D_IN ** (-0.5)
        b_router = jnp.zeros((E,), dtype=jnp.float32)
        lora_A = jax.random.normal(ks[4], (E, D_IN, R), dtype=jnp.float32) * D_IN ** (-0.5)
        lora_B = jnp.zeros((E, R, D_OUT), dtype=jnp.float32)
        return {'x': x, 'W_base': W_base, 'b_base': b_base, 'W_router': W_router, 'b_router': b_router, 'lora_A': lora_A, 'lora_B': lora_B}
    _L1_ffn_all = _L1_ffn_setup()
    _L1_ffn_in = {k: v for k, v in _L1_ffn_all.items() if k in ('W_base', 'b_base', 'W_router', 'b_router', 'lora_A', 'lora_B')}
    del _L1_ffn_all

    def _L2_xattn_setup():
        import jax, jax.numpy as jnp
        import numpy as np
        key = jax.random.key(seed)
        k1, k2 = jax.random.split(key)
        B, Lq, Lk, D = (16, 128, 256, 512)
        query = jax.random.normal(k1, (B, Lq, D), dtype=jnp.float32)
        key_t = jax.random.normal(k2, (B, Lk, D), dtype=jnp.float32)
        return {'query': query, 'key': key_t}
    _L2_xattn_all = _L2_xattn_setup()
    _L2_xattn_in = {k: v for k, v in _L2_xattn_all.items() if k in ()}
    del _L2_xattn_all

    def _L2_ffn_setup():
        import jax, jax.numpy as jnp
        import numpy as np
        GROUP = 64

        def dequant_q40(w, s, out_features, in_features):
            msb = w >> 4
            lsb = (w & 15 ^ 8) - 8
            g = jnp.concatenate([msb, lsb], axis=1).reshape(-1, GROUP)
            deq = g.astype(s.dtype) * s[:, None]
            return deq.reshape(out_features, in_features)
        key = jax.random.key(seed)
        ks = jax.random.split(key, 7)
        dim, hidden = (512, 1376)
        B, S = (2, 256)

        def packed(k, din, dout):
            return jax.random.randint(k, (din * dout // GROUP // 2, GROUP), -128, 128, dtype=jnp.int32)

        def scales(k, din, dout):
            return (jax.random.uniform(k, (din * dout // GROUP,), dtype=jnp.float32) + 0.5) * 0.01
        x = jax.random.normal(ks[0], (B, S, dim), dtype=jnp.float32)
        w1 = packed(ks[1], dim, hidden)
        s1 = scales(ks[2], dim, hidden)
        w2 = packed(ks[3], hidden, dim)
        s2 = scales(ks[4], hidden, dim)
        w3 = packed(ks[5], dim, hidden)
        s3 = scales(ks[6], dim, hidden)
        return {'x': x, 'w1': w1, 's1': s1, 'w2': w2, 's2': s2, 'w3': w3, 's3': s3}
    _L2_ffn_all = _L2_ffn_setup()
    _L2_ffn_in = {k: v for k, v in _L2_ffn_all.items() if k in ('w1', 's1', 'w2', 's2', 'w3', 's3')}
    del _L2_ffn_all

    def _L3_xattn_setup():
        import jax, jax.numpy as jnp
        import numpy as np
        NUM_HEADS = 32
        NUM_KV_HEADS = 8
        HEAD_DIM = 128
        HIDDEN = 512
        EPS = 1e-05

        def rmsnorm(x, w, eps=EPS):
            xf = x.astype(jnp.float32)
            var = jnp.mean(xf * xf, axis=-1, keepdims=True)
            return w * (xf * jax.lax.rsqrt(var + eps)).astype(x.dtype)
        key = jax.random.key(seed)
        ks = jax.random.split(key, 10)
        B, Q, KV = (1, 128, 6404)
        s = 1.0 / np.sqrt(HIDDEN)
        return {'hidden_states': jax.random.normal(ks[0], (B, Q, HIDDEN), jnp.float32), 'cross_attention_states': jax.random.normal(ks[1], (B, KV, HIDDEN), jnp.float32), 'attention_mask': jnp.zeros((B, 1, Q, KV), jnp.float32), 'q_proj_w': jax.random.normal(ks[2], (NUM_HEADS * HEAD_DIM, HIDDEN), jnp.float32) * s, 'k_proj_w': jax.random.normal(ks[3], (NUM_KV_HEADS * HEAD_DIM, HIDDEN), jnp.float32) * s, 'v_proj_w': jax.random.normal(ks[4], (NUM_KV_HEADS * HEAD_DIM, HIDDEN), jnp.float32) * s, 'o_proj_w': jax.random.normal(ks[5], (HIDDEN, NUM_HEADS * HEAD_DIM), jnp.float32) * s, 'q_norm_w': jnp.ones((HEAD_DIM,), jnp.float32), 'k_norm_w': jnp.ones((HEAD_DIM,), jnp.float32)}
    _L3_xattn_all = _L3_xattn_setup()
    _L3_xattn_in = {k: v for k, v in _L3_xattn_all.items() if k in ('q_proj_w', 'k_proj_w', 'v_proj_w', 'o_proj_w', 'q_norm_w', 'k_norm_w')}
    del _L3_xattn_all

    def _L3_ffn_setup():
        import jax, jax.numpy as jnp
        import numpy as np
        R = 16
        LORA_ALPHA = 16
        SCALING = LORA_ALPHA / R
        key = jax.random.key(seed)
        kx, kr, ka = jax.random.split(key, 3)
        B, S, D, DO, E = (4, 256, 512, 512, 8)
        x = jax.random.normal(kx, (B, S, D), dtype=jnp.float32)
        bound_r = 1.0 / np.sqrt(D)
        route_w = jax.random.uniform(kr, (E, D), jnp.float32, -bound_r, bound_r)
        bound_a = 1.0 / np.sqrt(D)
        A = jax.random.uniform(ka, (E, R, D), jnp.float32, -bound_a, bound_a)
        kb = jax.random.fold_in(key, 7)
        Bw = jax.random.normal(kb, (E, DO, R), dtype=jnp.float32) * 0.02
        return {'x': x, 'route_w': route_w, 'A': A, 'Bw': Bw}
    _L3_ffn_all = _L3_ffn_setup()
    _L3_ffn_in = {k: v for k, v in _L3_ffn_all.items() if k in ('route_w', 'A', 'Bw')}
    del _L3_ffn_all
    return {'x': x, 'ctx_4096': ctx_4096, 'mask_1x1xSxS2_ff0': mask_1x1xSxS2_ff0, 'L0_xattn_Wq': _L0_xattn_in['Wq'], 'L0_xattn_Wk': _L0_xattn_in['Wk'], 'L0_xattn_Wv': _L0_xattn_in['Wv'], 'L0_xattn_Wo': _L0_xattn_in['Wo'], 'L0_ffn_W_base': _L0_ffn_in['W_base'], 'L0_ffn_b_base': _L0_ffn_in['b_base'], 'L0_ffn_W_router': _L0_ffn_in['W_router'], 'L0_ffn_A_stack': _L0_ffn_in['A_stack'], 'L0_ffn_B_stack': _L0_ffn_in['B_stack'], 'L1_xattn_Wq': _L1_xattn_in['Wq'], 'L1_xattn_bq': _L1_xattn_in['bq'], 'L1_xattn_Wk': _L1_xattn_in['Wk'], 'L1_xattn_bk': _L1_xattn_in['bk'], 'L1_xattn_Wv': _L1_xattn_in['Wv'], 'L1_xattn_bv': _L1_xattn_in['bv'], 'L1_xattn_interference': _L1_xattn_in['interference'], 'L1_xattn_amp': _L1_xattn_in['amp'], 'L1_xattn_Wo': _L1_xattn_in['Wo'], 'L1_xattn_bo': _L1_xattn_in['bo'], 'L1_ffn_W_base': _L1_ffn_in['W_base'], 'L1_ffn_b_base': _L1_ffn_in['b_base'], 'L1_ffn_W_router': _L1_ffn_in['W_router'], 'L1_ffn_b_router': _L1_ffn_in['b_router'], 'L1_ffn_lora_A': _L1_ffn_in['lora_A'], 'L1_ffn_lora_B': _L1_ffn_in['lora_B'], 'L2_ffn_w1': _L2_ffn_in['w1'], 'L2_ffn_s1': _L2_ffn_in['s1'], 'L2_ffn_w2': _L2_ffn_in['w2'], 'L2_ffn_s2': _L2_ffn_in['s2'], 'L2_ffn_w3': _L2_ffn_in['w3'], 'L2_ffn_s3': _L2_ffn_in['s3'], 'L3_xattn_q_proj_w': _L3_xattn_in['q_proj_w'], 'L3_xattn_k_proj_w': _L3_xattn_in['k_proj_w'], 'L3_xattn_v_proj_w': _L3_xattn_in['v_proj_w'], 'L3_xattn_o_proj_w': _L3_xattn_in['o_proj_w'], 'L3_xattn_q_norm_w': _L3_xattn_in['q_norm_w'], 'L3_xattn_k_norm_w': _L3_xattn_in['k_norm_w'], 'L3_ffn_route_w': _L3_ffn_in['route_w'], 'L3_ffn_A': _L3_ffn_in['A'], 'L3_ffn_Bw': _L3_ffn_in['Bw']}

def reference(x, ctx_4096, mask_1x1xSxS2_ff0, L0_xattn_Wq, L0_xattn_Wk, L0_xattn_Wv, L0_xattn_Wo, L0_ffn_W_base, L0_ffn_b_base, L0_ffn_W_router, L0_ffn_A_stack, L0_ffn_B_stack, L1_xattn_Wq, L1_xattn_bq, L1_xattn_Wk, L1_xattn_bk, L1_xattn_Wv, L1_xattn_bv, L1_xattn_interference, L1_xattn_amp, L1_xattn_Wo, L1_xattn_bo, L1_ffn_W_base, L1_ffn_b_base, L1_ffn_W_router, L1_ffn_b_router, L1_ffn_lora_A, L1_ffn_lora_B, L2_ffn_w1, L2_ffn_s1, L2_ffn_w2, L2_ffn_s2, L2_ffn_w3, L2_ffn_s3, L3_xattn_q_proj_w, L3_xattn_k_proj_w, L3_xattn_v_proj_w, L3_xattn_o_proj_w, L3_xattn_q_norm_w, L3_xattn_k_norm_w, L3_ffn_route_w, L3_ffn_A, L3_ffn_Bw):
    import jax
    import jax.numpy as jnp

    def _L0_xattn_ref(query, key, value, Wq, Wk, Wv, Wo):
        import jax, jax.numpy as jnp
        import numpy as np
        DIM = 512
        NUM_HEADS = 32
        NUM_KV_HEADS = 8
        HEAD_DIM = DIM // NUM_HEADS
        KV_DIM = DIM // (NUM_HEADS // NUM_KV_HEADS)
        B, S = (1, 256)
        b, sq, _ = query.shape
        _, sk, _ = key.shape
        rep = NUM_HEADS // NUM_KV_HEADS
        q = (query @ Wq).reshape(b, sq, NUM_HEADS, HEAD_DIM).transpose(0, 2, 1, 3)
        k = (key @ Wk).reshape(b, sk, NUM_KV_HEADS, HEAD_DIM).transpose(0, 2, 1, 3)
        v = (value @ Wv).reshape(b, sk, NUM_KV_HEADS, HEAD_DIM).transpose(0, 2, 1, 3)
        k = jnp.repeat(k, rep, axis=1)
        v = jnp.repeat(v, rep, axis=1)
        scale = HEAD_DIM ** (-0.5)
        scores = jnp.einsum('bhqd,bhkd->bhqk', q, k) * scale
        probs = jax.nn.softmax(scores, axis=-1)
        out = jnp.einsum('bhqk,bhkd->bhqd', probs, v)
        out = out.transpose(0, 2, 1, 3).reshape(b, sq, DIM)
        return out @ Wo

    def _L0_ffn_ref(x, W_base, b_base, W_router, A_stack, B_stack):
        import jax, jax.numpy as jnp
        import numpy as np
        D_IN = 512
        D_OUT = 512
        RANK = 16
        NUM_EXPERTS = 8
        TOP_K = 2
        SCALING = 32.0 / RANK
        orig_shape = x.shape
        xf = x.reshape(-1, D_IN)
        logits = xf @ W_router.T
        probs = jax.nn.softmax(logits, axis=-1)
        topk_p, topk_i = jax.lax.top_k(probs, TOP_K)
        topk_p = topk_p / jnp.sum(topk_p, axis=-1, keepdims=True)
        combine = jnp.sum(jax.nn.one_hot(topk_i, NUM_EXPERTS, dtype=xf.dtype) * topk_p[..., None], axis=1)
        h = jnp.einsum('nd,erd->ner', xf, A_stack)
        h = h * combine[..., None]
        lora_out = jnp.einsum('ner,eor->no', h, B_stack) * SCALING
        base_out = xf @ W_base.T + b_base
        out = base_out + lora_out
        return out.reshape(orig_shape[:-1] + (D_OUT,))

    def _L1_xattn_ref(q, k, v, Wq, bq, Wk, bk, Wv, bv, interference, amp, Wo, bo):
        import jax, jax.numpy as jnp
        import numpy as np
        import math
        D_MODEL = 128
        NHEAD = 16
        MAX_SUP = 4
        DK = D_MODEL // NHEAD
        DM = D_MODEL * MAX_SUP
        B, S = (2, 128)
        b, s, dm = q.shape
        H, M = (interference.shape[0], interference.shape[1])
        dk = dm // (H * M)

        def proj(x, W, bias):
            y = x @ W.T + bias
            y = y.reshape(b, s, H, dk, M)
            return jnp.transpose(y, (0, 2, 1, 3, 4))
        qh = proj(q, Wq, bq)
        kh = proj(k, Wk, bk)
        vh = proj(v, Wv, bv)

        def interfere(x):
            return x + 0.1 * amp[0] * jnp.einsum('bhsdi,hij->bhsdj', x, interference)
        qh, kh, vh = (interfere(qh), interfere(kh), interfere(vh))
        scores = jnp.einsum('bhqdm,bhkdm->bhqkm', qh, kh) / math.sqrt(dk)
        weights = jax.nn.softmax(scores, axis=3)
        out = jnp.einsum('bhqkm,bhkdm->bhqdm', weights, vh)
        out = jnp.transpose(out, (0, 2, 1, 3, 4)).reshape(b, s, dm)
        return out @ Wo.T + bo

    def _L1_ffn_ref(x, W_base, b_base, W_router, b_router, lora_A, lora_B):
        import jax, jax.numpy as jnp
        import numpy as np

        def sparsemax(z):
            E = z.shape[-1]
            z_sorted = -jnp.sort(-z, axis=-1)
            z_cum = jnp.cumsum(z_sorted, axis=-1)
            k = jnp.arange(1, E + 1, dtype=z.dtype)
            support = 1.0 + k * z_sorted > z_cum
            k_z = jnp.sum(support, axis=-1, keepdims=True)
            tau_sum = jnp.take_along_axis(z_cum, k_z.astype(jnp.int32) - 1, axis=-1)
            tau = (tau_sum - 1.0) / k_z.astype(z.dtype)
            return jnp.maximum(z - tau, 0.0)
        base_out = jnp.einsum('bsd,od->bso', x, W_base) + b_base
        logits = jnp.einsum('bsd,ed->bse', x, W_router) + b_router
        weights = sparsemax(logits)
        h = jnp.einsum('bsd,edr->bser', x, lora_A)
        expert_out = jnp.einsum('bser,bse,ero->bso', h, weights, lora_B)
        return base_out + expert_out

    def _L2_xattn_ref(query, key):
        import jax, jax.numpy as jnp
        import numpy as np
        a = jnp.einsum('bqd,bkd->bqk', query, key)
        e = jax.nn.softmax(a, axis=-1)
        c = jnp.einsum('bqk,bkd->bqd', e, key)
        return c

    def _L2_ffn_ref(x, w1, s1, w2, s2, w3, s3):
        import jax, jax.numpy as jnp
        import numpy as np
        GROUP = 64

        def dequant_q40(w, s, out_features, in_features):
            msb = w >> 4
            lsb = (w & 15 ^ 8) - 8
            g = jnp.concatenate([msb, lsb], axis=1).reshape(-1, GROUP)
            deq = g.astype(s.dtype) * s[:, None]
            return deq.reshape(out_features, in_features)
        dim = x.shape[-1]
        hidden = w1.shape[0] * w1.shape[1] * 2 // dim
        W1 = dequant_q40(w1, s1, hidden, dim)
        W3 = dequant_q40(w3, s3, hidden, dim)
        W2 = dequant_q40(w2, s2, dim, hidden)
        a = jnp.einsum('bsd,hd->bsh', x, W1)
        b = jnp.einsum('bsd,hd->bsh', x, W3)
        h = jax.nn.silu(a) * b
        return jnp.einsum('bsh,dh->bsd', h, W2)

    def _L3_xattn_ref(hidden_states, cross_attention_states, attention_mask, q_proj_w, k_proj_w, v_proj_w, o_proj_w, q_norm_w, k_norm_w):
        import jax, jax.numpy as jnp
        import numpy as np
        NUM_HEADS = 32
        NUM_KV_HEADS = 8
        HEAD_DIM = 128
        HIDDEN = 512
        EPS = 1e-05

        def rmsnorm(x, w, eps=EPS):
            xf = x.astype(jnp.float32)
            var = jnp.mean(xf * xf, axis=-1, keepdims=True)
            return w * (xf * jax.lax.rsqrt(var + eps)).astype(x.dtype)
        B, Q, _ = hidden_states.shape
        KV = cross_attention_states.shape[1]
        n_rep = NUM_HEADS // NUM_KV_HEADS
        q = (hidden_states @ q_proj_w.T).reshape(B, Q, NUM_HEADS, HEAD_DIM).transpose(0, 2, 1, 3)
        k = (cross_attention_states @ k_proj_w.T).reshape(B, KV, NUM_KV_HEADS, HEAD_DIM).transpose(0, 2, 1, 3)
        v = (cross_attention_states @ v_proj_w.T).reshape(B, KV, NUM_KV_HEADS, HEAD_DIM).transpose(0, 2, 1, 3)
        q = rmsnorm(q, q_norm_w)
        k = jnp.repeat(k, n_rep, axis=1)
        v = jnp.repeat(v, n_rep, axis=1)
        k = rmsnorm(k, k_norm_w)
        scale = 1.0 / np.sqrt(HEAD_DIM)
        scores = jnp.einsum('bhqd,bhkd->bhqk', q, k) * scale + attention_mask
        attn = jax.nn.softmax(scores.astype(jnp.float32), axis=-1).astype(q.dtype)
        out = jnp.einsum('bhqk,bhkd->bhqd', attn, v)
        out = out.transpose(0, 2, 1, 3).reshape(B, Q, NUM_HEADS * HEAD_DIM)
        return out @ o_proj_w.T

    def _L3_ffn_ref(x, route_w, A, Bw):
        import jax, jax.numpy as jnp
        import numpy as np
        R = 16
        LORA_ALPHA = 16
        SCALING = LORA_ALPHA / R
        logits = jnp.einsum('bsd,ed->bse', x, route_w)
        topk_v, topk_idx = jax.lax.top_k(logits, 1)
        E = logits.shape[-1]
        route_weight = jax.nn.one_hot(topk_idx[..., 0], E, dtype=logits.dtype) * topk_v
        h = jnp.einsum('bsd,erd->bser', x, A)
        wh = route_weight[..., None] * h
        out = jnp.einsum('bser,eor->bso', wh, Bw) * SCALING
        return out
    x = x + _L0_xattn_ref(_layernorm(x, axis=-1), ctx_4096, ctx_4096, L0_xattn_Wq, L0_xattn_Wk, L0_xattn_Wv, L0_xattn_Wo)
    x = x + _L0_ffn_ref(_layernorm(x, axis=-1), L0_ffn_W_base, L0_ffn_b_base, L0_ffn_W_router, L0_ffn_A_stack, L0_ffn_B_stack)
    x = x + _L1_xattn_ref(_layernorm(x, axis=-1), ctx_4096, ctx_4096, L1_xattn_Wq, L1_xattn_bq, L1_xattn_Wk, L1_xattn_bk, L1_xattn_Wv, L1_xattn_bv, L1_xattn_interference, L1_xattn_amp, L1_xattn_Wo, L1_xattn_bo)
    x = x + _L1_ffn_ref(_layernorm(x, axis=-1), L1_ffn_W_base, L1_ffn_b_base, L1_ffn_W_router, L1_ffn_b_router, L1_ffn_lora_A, L1_ffn_lora_B)
    x = x + _L2_xattn_ref(_layernorm(x, axis=-1), ctx_4096)
    x = x + _L2_ffn_ref(_layernorm(x, axis=-1), L2_ffn_w1, L2_ffn_s1, L2_ffn_w2, L2_ffn_s2, L2_ffn_w3, L2_ffn_s3)
    x = x + _L3_xattn_ref(_layernorm(x, axis=-1), ctx_4096, mask_1x1xSxS2_ff0, L3_xattn_q_proj_w, L3_xattn_k_proj_w, L3_xattn_v_proj_w, L3_xattn_o_proj_w, L3_xattn_q_norm_w, L3_xattn_k_norm_w)
    x = x + _L3_ffn_ref(_layernorm(x, axis=-1), L3_ffn_route_w, L3_ffn_A, L3_ffn_Bw)
    return x

_drawn_inputs = setup_inputs


def setup_inputs(seed=0):
    import zlib

    import numpy as np

    out = dict(_drawn_inputs(seed))
    spreads = {'L1_xattn_bq': (0.0, 0.8),
     'L1_xattn_bk': (0.0, 0.8),
     'L1_xattn_bv': (0.0, 0.1),
     'L1_xattn_bo': (0.0, 0.1),
     'L1_ffn_b_router': (0.0, 0.287),
     'L1_ffn_lora_B': (0.0, 0.1),
     'L3_xattn_q_norm_w': (1.0, 0.2),
     'L3_xattn_k_norm_w': (1.0, 0.2)}
    factors = {'L0_ffn_b_base': 6.591,
     'L1_xattn_Wq': 7.467,
     'L1_xattn_Wk': 7.636,
     'L1_xattn_interference': 2.846,
     'L1_ffn_b_base': 7.645,
     'L3_ffn_route_w': 4.77,
     'L3_ffn_A': 4.391,
     'L3_ffn_Bw': 4.313}
    for name, (base, spread) in spreads.items():
        noise = np.random.default_rng([zlib.crc32(name.encode()), seed]).standard_normal(out[name].shape)
        drawn = base * np.exp(spread * noise) if base else spread * noise
        out[name] = jnp.asarray(drawn.astype(out[name].dtype))
    for name, factor in factors.items():
        out[name] = (out[name] * factor).astype(out[name].dtype)
    return out
```

```python
from contextlib import ExitStack

import numpy as np

import concourse.bass as bass
from concourse import mybir
from concourse.alu_op_type import AluOpType as ALU

ACT = mybir.ActivationFunctionType
AX = mybir.AxisListType
F32 = mybir.dt.float32
F32R = mybir.dt.float32r
F16 = mybir.dt.float16
BF16 = mybir.dt.bfloat16
I32 = mybir.dt.int32
U32 = mybir.dt.uint32

P = 128
B = 8
D = 512
KC = D // P
TOK = B * P
HALF = TOK // 2
HB = B // 2
EPS = 1e-5
EXPERTS, RANK = 8, 16
LR = EXPERTS * RANK
HIDDEN = 1376
HCH = -(-HIDDEN // P)
PASSES = ((0, 0), (0, 1), (1, 0))


class Chip:
    pass


def split_passes(nc, out, stationary, moving, first, last):
    for n, (s, m) in enumerate(PASSES):
        ins = nc.tensor.matmul(out, stationary[s], moving[m], start=first and n == 0, stop=last and n == 2)
    return ins


def fp(ap):
    return ap.bitcast(F32)


def load_inputs(nc, c, d):
    with ExitStack() as ctx:
        raw = ctx.enter_context(nc.sbuf_tensor("ctx_raw", [P, KC, TOK], F32))
        loaded = c.sem("in_loaded")
        ctx_loaded = c.sem("ctx_loaded")
        high = c.sem("ctx_high")
        low = c.sem("ctx_low")
        block = ctx.enter_context(nc.Block())

        @block.sync
        def _(sp):
            for k in range(KC):
                sp.dma_start(raw[:, k, :], d["ctxT"][:, k, :]).then_inc(ctx_loaded, 16)
            sp.dma_start(c.x[:, :, :], d["x"].rearrange("b p n -> p b n")).then_inc(loaded, 16)
            sp.dma_start(c.consts[:, :], d["consts"]).then_inc(loaded, 16)
            sp.wait_ge(loaded, 32)

        @block.gpsimd
        def _(pool):
            nc.gpsimd.memset(c.ones[:, :], 1.0)
            nc.gpsimd.memset(c.minus_half[:, :], -0.5)

        @block.scalar
        def _(act):
            act.wait_ge(ctx_loaded, 16 * KC)
            for k in range(KC):
                nc.scalar.copy(c.ctxT[0][:, k, :], raw[:, k, :]).then_inc(high, 1)

        @block.vector
        def _(dve):
            for k in range(KC):
                dve.wait_ge(high, k + 1)
                nc.vector.tensor_tensor(c.ctxT[1][:, k, :], raw[:, k, :], fp(c.ctxT[0][:, k, :]), ALU.subtract).then_inc(low, 1)


def layernorm_steps(nc, c, t, ctx, width):
    n = Chip()
    n.stats = ctx.enter_context(nc.sbuf_tensor(t + "stats", [P, width, 6], F32))
    n.mv = ctx.enter_context(nc.sbuf_tensor(t + "mv", [P, width, 2], F32))
    n.ve = ctx.enter_context(nc.sbuf_tensor(t + "ve", [P, width], F32))
    n.rstd = ctx.enter_context(nc.sbuf_tensor(t + "rstd", [P, width], F32))
    n.xn = ctx.enter_context(nc.sbuf_tensor(t + "xn", [P, width, D], F32))
    n.stats_done, n.mv_done, n.var_ready = c.sem(t + "stats_done"), c.sem(t + "mv_done"), c.sem(t + "var_ready")
    n.rstd_ready = c.sem(t + "rstd_ready")
    n.xn_ready = c.sem(t + "xn_ready")
    n.xnT_full = c.sem(t + "xnT_full")
    n.xnT_high, n.xnT_low = c.sem(t + "xnT_high"), c.sem(t + "xnT_low")
    return n


def norm_on_vector(nc, dve, n, c, it, width, x_of):
    for u in range(width):
        nc.vector.bn_stats(n.stats[:, u, :], x_of(u)).then_inc(n.stats_done, 1)
    dve.wait_ge(n.stats_done, it * width + width)
    nc.vector.tensor_copy(c.scratch[:, :], c.ones[:, 0:1])
    for u in range(width):
        nc.vector.bn_aggr(n.mv[:, u, :], n.stats[:, u, :]).then_inc(n.mv_done, 1)
    dve.wait_ge(n.mv_done, it * width + width)
    nc.vector.tensor_scalar(n.ve[:, :], n.mv[:, :, 1], EPS, None, ALU.add).then_inc(n.var_ready, 1)
    dve.wait_ge(n.rstd_ready, it + 1)
    for u in range(width):
        nc.vector.tensor_scalar(n.xn[:, u, :], x_of(u), n.mv[:, u, 0:1], n.rstd[:, u:u + 1],
                                ALU.subtract, ALU.mult).then_inc(n.xn_ready, 1)


def rstd_on_pool(nc, pool, n, c, it, width):
    pool.wait_ge(n.var_ready, it + 1)
    nc.gpsimd.tensor_tensor(n.rstd[:, :], n.ve[:, :], c.minus_half[:, 0:width], ALU.pow).then_inc(n.rstd_ready, 1)


def norm_transpose(nc, c, d, t, xnT, bias=None):
    W = HB
    with ExitStack() as ctx:
        n = layernorm_steps(nc, c, t, ctx, W)
        if bias:
            bias_sb = ctx.enter_context(nc.sbuf_tensor(t + "bias", [P, D], F32))
            bias_loaded = c.sem(t + "bias_loaded")
        block = ctx.enter_context(nc.Block())

        @block.sync
        def _(sp):
            if bias:
                sp.dma_start(bias_sb[:, :], d[bias].partition_broadcast(P).rearrange("p a n -> p (a n)")).then_inc(bias_loaded, 16)

        @block.vector
        def _(dve):
            with dve.Fori(0, B // W) as it:
                norm_on_vector(nc, dve, n, c, it, W, lambda u: c.x[:, bass.ds(it * W + u, 1), :].rearrange("p a n -> p (a n)"))
                for u in range(W):
                    dve.wait_ge(n.xnT_high, it * W + u + 1)
                    cols = bass.ds((it * W + u) * P, P)
                    nc.vector.tensor_tensor(xnT[1][:, :, cols], c.bank[u][:, :].rearrange("p (k t) -> p k t", k=KC),
                                            fp(xnT[0][:, :, cols]), ALU.subtract).then_inc(n.xnT_low, 1)

        @block.gpsimd
        def _(pool):
            if bias:
                pool.wait_ge(bias_loaded, 16)
            with pool.Fori(0, B // W) as it:
                rstd_on_pool(nc, pool, n, c, it, W)
                if bias:
                    for u in range(W):
                        pool.wait_ge(n.xn_ready, it * W + u + 1)
                        xb = c.x[:, bass.ds(it * W + u, 1), :].rearrange("p a n -> p (a n)")
                        nc.gpsimd.tensor_tensor(xb, xb, bias_sb[:, :], ALU.add)

        @block.tensor
        def _(pe):
            with pe.Fori(0, B // W) as it:
                for u in range(W):
                    pe.wait_ge(n.xn_ready, it * W + u + 1)
                    for k in range(KC):
                        last = nc.tensor.transpose(c.bank[u][:, k * P:(k + 1) * P], n.xn[:, u, k * P:(k + 1) * P], c.ident)
                    last.then_inc(n.xnT_full, 1)

        @block.scalar
        def _(act):
            with act.Fori(0, B // W) as it:
                for u in range(W):
                    act.wait_ge(n.xnT_full, it * W + u + 1)
                    nc.scalar.copy(xnT[0][:, :, bass.ds((it * W + u) * P, P)],
                                   c.bank[u][:, :].rearrange("p (k t) -> p k t", k=KC)).then_inc(n.xnT_high, 1)


def store_output(nc, c, d):
    with ExitStack() as ctx:
        stored = c.sem("out_stored")
        block = ctx.enter_context(nc.Block())

        @block.sync
        def _(sp):
            sp.dma_start(d["out"].rearrange("b p n -> p b n"), c.x[:, :, :]).then_inc(stored, 16)
            sp.wait_ge(stored, 16)


IDENT, MASK16, MASKM, MASKG, BLOCK4, IOTA, TRI, RECK = 0, 128, 136, 140, 144, 272, 280, 344
CONSTS = 352


def constants():
    p = np.arange(P)
    a = np.zeros((P, CONSTS), np.float32)
    a[:, IDENT:IDENT + P] = np.eye(P)
    a[:, MASK16:MASK16 + 8] = p[:, None] // 16 == np.arange(8)
    a[:, MASKM:MASKM + 4] = p[:, None] % 4 == np.arange(4)
    a[:, MASKG:MASKG + 4] = p[:, None] // 32 == np.arange(4)
    a[:, BLOCK4:BLOCK4 + P] = p[:, None] // 4 == p // 4
    a[:, IOTA:IOTA + 8] = np.arange(8)
    a[:, TRI:TRI + 64] = np.tril(np.ones((8, 8))).reshape(-1)
    a[:, RECK:RECK + 8] = 1.0 / np.arange(1, 9)
    return a



def small_head_attention(nc, c, d, layer, xnT):
    own_kv = layer == 1
    SG = 4 if own_kv else 2
    HEADS = 4 * SG
    DV = P // HEADS
    VW = 3 * DV + 1
    MASKS = 4 if own_kv else 8
    SCALE = (8 if own_kv else 16) ** -0.5
    N = B * SG
    t = f"a{layer}_"
    with ExitStack() as ctx:
        def sb(name, shape, dt=F32):
            return ctx.enter_context(nc.sbuf_tensor(t + name, shape, dt))

        def pair(name, shape, dt=F32R):
            return sb(name + "_hi", shape, dt), sb(name + "_lo", shape, dt)

        def sem(name):
            return c.sem(t + name)

        kTm = pair("kTm", [P, MASKS, TOK])
        qT = pair("qT", [P, 4 if own_kv else 1, TOK])
        wq, wk, wv, wo = pair("wq", [P, KC, P]), pair("wk", [P, KC, P]), pair("wv", [P, KC, P]), pair("wo", [P, D])
        temp = pair("temp", [P, 2, HALF])
        wo_raw = sb("wo_raw", [P, D])
        if own_kv:
            w_nat = sb("w_nat", [P, 3, D])
            inter_raw, inter = sb("inter_raw", [P, KC, 4]), sb("inter", [P, KC, 4])
            amp = sb("amp", [P, 1])
            bias_raw, bias = sb("bias_raw", [P, KC, 3]), sb("bias", [P, 3])
            fold = sb("fold", [P, P])
        else:
            wkv_raw = sb("wkv_raw", [P, 2 * KC, P])
            wq_raw = wkv_raw[:, 0:KC, :]
        v_aug = sb("v_aug", [P, B, HEADS, VW], BF16)
        v_rest = sb("v_rest", [P, B, P])
        row_max = sb("row_max", [P, 2, 4])
        prob = sb("prob", [P, 2, HALF])
        pT = pair("pT", [P, 2, HALF], F16)
        o_raw, o_inv, o_sb = sb("o_raw", [P, 2, P]), sb("o_inv", [P, 2, HEADS]), sb("o_sb", [P, 2, P])
        oT = pair("oT", [P, 2, P])

        once_loaded = sem("once_loaded")
        wq_loaded = sem("wq_loaded")
        wo_loaded = sem("wo_loaded")
        split_high = sem("split_high")
        kv_split = sem("kv_split")
        wq_split, wo_split = sem("wq_split"), sem("wo_split")
        ones_set = sem("ones_set")
        inter_ready = sem("inter_ready")
        fold_step, folded = sem("fold_step"), sem("folded")
        m_full = sem("m_full")
        m_high = sem("m_high")
        m_free = sem("m_free")
        mask_high, mask_low = sem("mask_high"), sem("mask_low")
        v2_ready, v3_ready = sem("v2_ready"), sem("v3_ready")
        s_full = sem("s_full")
        max_ready = sem("max_ready")
        s_free = sem("s_free")
        p_ready = sem("p_ready")
        pT_full = sem("pT_full")
        pT_high = sem("pT_high")
        pT_low = sem("pT_low")
        pv_done = sem("pv_done")
        o_step = sem("o_step")
        o_free = sem("o_free")

        S, PT, OB, M = c.bank[0:2], c.bank[2:4], c.bank[4:6], c.bank[6:8]

        def ends(n):
            return n // SG if 0 <= n < N and n % SG == SG - 1 else None

        ahead = [] if own_kv else ["k0", "k1", "v0", "v1"]
        order = (["fq", "fk", "fv", "fb"] if own_kv else []) + ["q0", "q1"] + (["k0", "k1", "v0", "v1"] if own_kv else [])
        for n in range(N + 5):
            order += [f"t{ends(n - 3)}"] if ends(n - 3) is not None else []
            order += [f"o{ends(n - 4)}"] if ends(n - 4) is not None else []
        by_act = [x for x in order if x[0] != "o" and x != "fb"]
        assert len(ahead) % 2 == 0 and len(order) % 2 == 0

        def tile(g, name):
            return ahead.index(name) if name in ahead else g * len(order) + (len(ahead) + order.index(name))

        def high(g, name):
            return ahead.index(name) if name in ahead else g * len(by_act) + (len(ahead) + by_act.index(name))

        def bank_of(name):
            return M[(ahead.index(name) if name in ahead else order.index(name)) % 2]

        def temp_of(name):
            return (ahead.index(name) if name in ahead else order.index(name)) % 2

        block = ctx.enter_context(nc.Block())

        @block.sync
        def _(sp):
            def load_wq(g):
                if own_kv:
                    sp.dma_start(w_nat[:, :, :], d["L1_wqkv"][bass.ds(g, 1)].rearrange("a p w n -> (a p) w n")).then_inc(wq_loaded, 16)
                else:
                    sp.dma_start(wq_raw, d["L0_wq"][bass.ds(g, 1)].rearrange("a p k n -> (a p) k n")).then_inc(wq_loaded, 16)

            def load_wo(g):
                sp.dma_start(wo_raw[:, :], d[f"L{layer}_wo"][bass.ds(g, 1)].rearrange("a p n -> (a p) n")).then_inc(wo_loaded, 16)

            if own_kv:
                sp.dma_start(inter_raw[:, :, :], d["L1_inter"]).then_inc(once_loaded, 16)
                sp.dma_start(amp[:, :], d["L1_amp"]).then_inc(once_loaded, 16)
                sp.dma_start(bias_raw[:, :, :], d["L1_bias"]).then_inc(once_loaded, 16)
            else:
                sp.dma_start(wkv_raw[:, :, :], d["L0_wkv"]).then_inc(once_loaded, 16)
                sp.wait_ge(kv_split, 1)
            load_wq(0)
            load_wo(0)
            with sp.Fori(1, KC) as g:
                if own_kv:
                    sp.wait_ge(m_free, tile(g - 1, "fb") + 3)
                else:
                    sp.wait_ge(wq_split, g)
                load_wq(g)
                sp.wait_ge(wo_split, g)
                load_wo(g)

        @block.gpsimd
        def _(pool):
            def split(raw, parts, highs, done):
                one = c.ones[:, 0:1].broadcast_to([P, raw.shape[1]]) if raw.ndim == 2 else \
                    c.ones[:, 0:1].unsqueeze(2).broadcast_to([P, raw.shape[1], raw.shape[2]])
                nc.gpsimd.tensor_tensor(parts[0], raw, one, ALU.mult).then_inc(split_high, 1)
                pool.wait_ge(split_high, highs + 1)
                nc.gpsimd.tensor_tensor(parts[1], raw, fp(parts[0]), ALU.subtract).then_inc(done, 1)

            def value_parts(g, half):
                pool.wait_ge(m_free, tile(g, f"v{half}") + 3)
                for u in range(HB):
                    b = half * HB + u
                    rest = v_rest[:, b, :].rearrange("p (h e) -> p h e", h=HEADS)
                    one = c.ones[:, 0:1].unsqueeze(2).broadcast_to([P, HEADS, DV])
                    nc.gpsimd.tensor_tensor(v_aug[:, b, :, DV:2 * DV], rest, one, ALU.mult).then_inc(v2_ready, 1)
                for u in range(HB):
                    b = half * HB + u
                    rest = v_rest[:, b, :].rearrange("p (h e) -> p h e", h=HEADS)
                    pool.wait_ge(v2_ready, (g if own_kv else 0) * B + (b + 1))
                    nc.gpsimd.tensor_tensor(v_aug[:, b, :, 2 * DV:3 * DV], rest, v_aug[:, b, :, DV:2 * DV],
                                            ALU.subtract).then_inc(v3_ready, 1)

            def whole(w):
                return [x[:, :, :] for x in w]

            nc.gpsimd.memset(v_aug[:, :, :, VW - 1:VW], 1.0).then_inc(ones_set, 1)
            if not own_kv:
                pool.wait_ge(once_loaded, 16)
                split(wkv_raw[:, 0:KC, :], whole(wk), 0, kv_split)
                split(wkv_raw[:, KC:2 * KC, :], whole(wv), 1, kv_split)
                pool.wait_ge(wq_loaded, 16)
                split(wq_raw, whole(wq), 2, wq_split)
            pool.wait_ge(wo_loaded, 16)
            split(wo_raw[:, :], [x[:, :] for x in wo], 0 if own_kv else 3, wo_split)
            value_parts(0, 0)
            value_parts(0, 1)
            with pool.Fori(1, KC) as g:
                if not own_kv:
                    pool.wait_ge(wq_loaded, g * 16 + 16)
                    pool.wait_ge(m_free, tile(g - 1, "q1") + 3)
                    split(wq_raw, whole(wq), g * 2 + 2, wq_split)
                pool.wait_ge(wo_loaded, g * 16 + 16)
                pool.wait_ge(m_free, tile(g - 1, f"o{B - 1}") + 3)
                split(wo_raw[:, :], [x[:, :] for x in wo], g if own_kv else g * 2 + 3, wo_split)
                if own_kv:
                    value_parts(g, 0)
                    value_parts(g, 1)

        @block.tensor
        def _(pe):
            def take(g, name):
                pe.wait_ge(m_free, tile(g, name) + 1)
                return bank_of(name)

            def transposed(g, name, w, rhs, half):
                bank = take(g, name)
                for k in range(KC):
                    ins = split_passes(nc, bank[:, :], [x[:, k, :] for x in w],
                                       [x[:, k, half * HALF:(half + 1) * HALF] for x in rhs], k == 0, k == KC - 1)
                ins.then_inc(m_full, 1)

            def keys(g):
                for half in range(2):
                    transposed(g, f"k{half}", wk, c.ctxT, half)

            def values(g):
                for half in range(2):
                    bank = take(g, f"v{half}")
                    for u in range(HB):
                        cols = slice((half * HB + u) * P, (half * HB + u + 1) * P)
                        for k in range(KC):
                            ins = split_passes(nc, bank[:, u * P:(u + 1) * P], [x[:, k, cols] for x in c.ctxT],
                                               [x[:, k, :] for x in wv], k == 0, k == KC - 1)
                    ins.then_inc(m_full, 1)

            if not own_kv:
                pe.wait_ge(kv_split, 2)
                keys(0)
                values(0)
            with pe.Fori(0, KC) as g:
                if own_kv:
                    pe.wait_ge(folded, g + 1)
                    pe.wait_ge(wq_loaded, g * 16 + 16)
                    for n, name in enumerate(("fq", "fk", "fv")):
                        bank = take(g, name)
                        for k in range(KC):
                            ins = nc.tensor.matmul(bank[:, k * P:(k + 1) * P], w_nat[:, n, k * P:(k + 1) * P], fold[:, :],
                                                   start=True, stop=True)
                        ins.then_inc(m_full, 1)
                    bank = take(g, "fb")
                    pe.wait_ge(once_loaded, 48)
                    nc.tensor.matmul(bank[:, 0:3], fold[:, :], bias_raw[:, bass.ds(g, 1), :].rearrange("p a n -> p (a n)"),
                                     start=True, stop=True).then_inc(m_full, 1)
                    pe.wait_ge(m_free, tile(g, "fq") + 3)
                else:
                    pe.wait_ge(wq_split, g + 1)
                transposed(g, "q0", wq, xnT, 0)
                transposed(g, "q1", wq, xnT, 1)
                if own_kv:
                    pe.wait_ge(m_free, tile(g, "fk") + 3)
                    keys(g)
                    pe.wait_ge(m_free, tile(g, "fv") + 3)
                    values(g)
                for n in range(N + 5):
                    if n < N:
                        b, s = n // SG, n % SG
                        if n == 0:
                            tiles = g * 4 + 4 if own_kv else 2
                            pe.wait_ge(mask_high, tiles)
                            pe.wait_ge(mask_low, tiles)
                            pe.wait_ge(m_free, tile(g, "q1") + 3)
                        pe.wait_ge(s_free, g * N + (n + 1))
                        tok = slice(b * P, (b + 1) * P)
                        keys_of = slice(0, 4) if own_kv else slice(4 * s, 4 * s + 4)
                        split_passes(nc, S[n % 2][:, :].rearrange("p (a t) -> p a t", a=4),
                                     [x[:, s if own_kv else 0, tok] for x in qT], [x[:, keys_of, tok] for x in kTm],
                                     True, True).then_inc(s_full, 1)
                    if 0 <= n - 1 < N:
                        i = n - 1
                        pe.wait_ge(p_ready, g * N + (i + 1))
                        pe.wait_ge(pT_low, g * N + (i + 1))
                        for h in range(4):
                            ins = nc.tensor.transpose(PT[i % 2][:, h * P:(h + 1) * P], prob[:, i % 2, h * P:(h + 1) * P], c.ident)
                        ins.then_inc(pT_full, 1)
                    if 0 <= n - 2 < N:
                        i = n - 2
                        b, s = i // SG, i % SG
                        pe.wait_ge(pT_low, g * N + (i + 3))
                        if s == 0:
                            pe.wait_ge(o_free, g * B + (b + 1))
                        if i == 0:
                            pe.wait_ge(v3_ready, g * B + B if own_kv else B)
                            pe.wait_ge(ones_set, 1)
                        for h in range(4):
                            head = 4 * s + h
                            out = OB[b % 2][:, head * VW:(head + 1) * VW]
                            nc.tensor.matmul(out, pT[0][:, i % 2, h * P:(h + 1) * P], v_aug[:, b, head, :], start=True, stop=False)
                            ins = nc.tensor.matmul(out, pT[1][:, i % 2, h * P:(h + 1) * P], v_aug[:, b, head, :],
                                                   start=False, stop=True)
                        ins.then_inc(pv_done, 1)
                    if ends(n - 3) is not None:
                        b = ends(n - 3)
                        bank = take(g, f"t{b}")
                        pe.wait_ge(o_free, g * B + (b + 3))
                        nc.tensor.transpose(bank[:, 0:P], o_sb[:, b % 2, :], c.ident).then_inc(m_full, 1)
                    if ends(n - 4) is not None:
                        b = ends(n - 4)
                        bank = take(g, f"o{b}")
                        if b == 0:
                            pe.wait_ge(wo_split, g + 1)
                        pe.wait_ge(m_free, tile(g, f"t{b}") + 3)
                        split_passes(nc, bank[:, :], [x[:, b % 2, :] for x in oT], [x[:, :] for x in wo],
                                     True, True).then_inc(m_full, 1)

        @block.scalar
        def _(act):
            def masked(g, name, out, masks, col):
                r, half = temp_of(name), int(name[1])
                act.wait_ge(m_full, tile(g, name) + 1)
                if own_kv:
                    act.wait_ge(m_free, tile(g, "fb") + 3)
                    nc.scalar.activation(temp[0][:, r, :], bank_of(name)[:, :], ACT.Identity,
                                         bias=bias[:, col:col + 1]).then_inc(m_high, 1)
                else:
                    nc.scalar.copy(temp[0][:, r, :], bank_of(name)[:, :]).then_inc(m_high, 1)
                act.wait_ge(m_high, high(g, name) + 1)
                for m in range(out[0].shape[1]):
                    ins = nc.scalar.activation(out[0][:, m, half * HALF:(half + 1) * HALF], fp(temp[0][:, r, :]), ACT.Copy,
                                               scale=c.consts[:, masks + m:masks + m + 1])
                ins.then_inc(mask_high, 1)

            def values(g, half):
                act.wait_ge(m_full, tile(g, f"v{half}") + 1)
                for u in range(HB):
                    src = bank_of(f"v{half}")[:, u * P:(u + 1) * P]
                    out = v_aug[:, half * HB + u, :, 0:DV]
                    if own_kv:
                        src = src.rearrange("p (h e m) -> p h m e", h=4, m=4)
                        out = out.rearrange("p (h m) e -> p h m e", h=4)
                    else:
                        src = src.rearrange("p (h e) -> p h e", h=HEADS)
                    ins = nc.scalar.copy(out, src)
                ins.then_inc(m_high, 1)

            if not own_kv:
                masked(0, "k0", kTm, MASK16, None)
                masked(0, "k1", kTm, MASK16, None)
                values(0, 0)
                values(0, 1)
            with act.Fori(0, KC) as g:
                if own_kv:
                    for name, w in (("fq", wq), ("fk", wk), ("fv", wv)):
                        act.wait_ge(m_full, tile(g, name) + 1)
                        nc.scalar.copy(w[0][:, :, :], bank_of(name)[:, :].rearrange("p (k n) -> p k n", k=KC)).then_inc(m_high, 1)
                    masked(g, "q0", qT, MASKG, 0)
                    masked(g, "q1", qT, MASKG, 0)
                    masked(g, "k0", kTm, MASKM, 1)
                    masked(g, "k1", kTm, MASKM, 1)
                    values(g, 0)
                    values(g, 1)
                else:
                    for half in range(2):
                        act.wait_ge(m_full, tile(g, f"q{half}") + 1)
                        nc.scalar.copy(qT[0][:, 0, half * HALF:(half + 1) * HALF], bank_of(f"q{half}")[:, :]).then_inc(m_high, 1)
                for n in range(N + 5):
                    if n < N:
                        act.wait_ge(s_free, g * N + (n + 3))
                        nc.scalar.activation(prob[:, n % 2, :], prob[:, n % 2, :], ACT.Exp, scale=SCALE).then_inc(p_ready, 1)
                    if 0 <= n - 1 < N:
                        act.wait_ge(pT_full, g * N + n)
                        nc.scalar.copy(pT[0][:, (n - 1) % 2, :], PT[(n - 1) % 2][:, :]).then_inc(pT_high, 1)
                    if ends(n - 3) is not None:
                        b = ends(n - 3)
                        act.wait_ge(m_full, tile(g, f"t{b}") + 1)
                        src = bank_of(f"t{b}")[:, 0:P]
                        if own_kv:
                            nc.scalar.activation(oT[0][:, b % 2, :], src, ACT.Identity, bias=bias[:, 2:3]).then_inc(m_high, 1)
                        else:
                            nc.scalar.copy(oT[0][:, b % 2, :], src).then_inc(m_high, 1)

        @block.vector
        def _(dve):
            def masked(g, name, out, masks, col):
                r, half = temp_of(name), int(name[1])
                dve.wait_ge(m_high, high(g, name) + 1)
                if own_kv:
                    nc.vector.scalar_tensor_tensor(temp[1][:, r, :], bank_of(name)[:, :], bias[:, col:col + 1],
                                                   fp(temp[0][:, r, :]), ALU.add, ALU.subtract).then_inc(m_free, 1)
                else:
                    nc.vector.tensor_tensor(temp[1][:, r, :], bank_of(name)[:, :], fp(temp[0][:, r, :]), ALU.subtract).then_inc(m_free, 1)
                dve.wait_ge(m_free, tile(g, name) + 3)
                for m in range(out[1].shape[1]):
                    ins = nc.vector.tensor_scalar(out[1][:, m, half * HALF:(half + 1) * HALF], fp(temp[1][:, r, :]),
                                                  c.consts[:, masks + m:masks + m + 1], None, ALU.mult)
                ins.then_inc(mask_low, 1)

            def values(g, half):
                dve.wait_ge(m_high, high(g, f"v{half}") + 1)
                for u in range(HB):
                    b = half * HB + u
                    src = bank_of(f"v{half}")[:, u * P:(u + 1) * P]
                    first, out = v_aug[:, b, :, 0:DV], v_rest[:, b, :]
                    if own_kv:
                        src = src.rearrange("p (h e m) -> p h m e", h=4, m=4)
                        first = first.rearrange("p (h m) e -> p h m e", h=4)
                        out = out.rearrange("p (h m e) -> p h m e", h=4, m=4)
                    else:
                        src = src.rearrange("p (h e) -> p h e", h=HEADS)
                        out = out.rearrange("p (h e) -> p h e", h=HEADS)
                    ins = nc.vector.tensor_tensor(out, src, first, ALU.subtract)
                ins.then_inc(m_free, 1)

            dve.sem_inc(m_free, 2)
            dve.sem_inc(s_free, 2)
            dve.sem_inc(pT_low, 2)
            dve.sem_inc(o_free, 2)
            if own_kv:
                dve.wait_ge(once_loaded, 48)
                nc.vector.tensor_scalar(inter[:, :, :], inter_raw[:, :, :], amp[:, 0:1], 0.1, ALU.mult, ALU.mult).then_inc(inter_ready, 1)
                dve.wait_ge(inter_ready, 1)
            else:
                masked(0, "k0", kTm, MASK16, None)
                masked(0, "k1", kTm, MASK16, None)
                values(0, 0)
                values(0, 1)
            with dve.Fori(0, KC) as g:
                if own_kv:
                    nc.vector.tensor_tensor(fold[:, :].rearrange("p (e j) -> p e j", j=4),
                                            c.consts[:, BLOCK4:BLOCK4 + P].rearrange("p (e j) -> p e j", j=4),
                                            inter[:, bass.ds(g, 1), :].broadcast_to([P, P // 4, 4]), ALU.mult).then_inc(fold_step, 1)
                    dve.wait_ge(fold_step, g + 1)
                    nc.vector.tensor_tensor(fold[:, :], fold[:, :], c.ident, ALU.add).then_inc(folded, 1)
                    for name, w in (("fq", wq), ("fk", wk), ("fv", wv)):
                        dve.wait_ge(m_high, high(g, name) + 1)
                        nc.vector.tensor_tensor(w[1][:, :, :], bank_of(name)[:, :].rearrange("p (k n) -> p k n", k=KC),
                                                fp(w[0][:, :, :]), ALU.subtract).then_inc(m_free, 1)
                    dve.wait_ge(m_full, tile(g, "fb") + 1)
                    nc.vector.tensor_copy(bias[:, :], bank_of("fb")[:, 0:3]).then_inc(m_free, 1)
                    dve.wait_ge(m_free, tile(g, "fb") + 3)
                    masked(g, "q0", qT, MASKG, 0)
                    masked(g, "q1", qT, MASKG, 0)
                    masked(g, "k0", kTm, MASKM, 1)
                    masked(g, "k1", kTm, MASKM, 1)
                    values(g, 0)
                    values(g, 1)
                else:
                    for half in range(2):
                        dve.wait_ge(m_high, high(g, f"q{half}") + 1)
                        cols = slice(half * HALF, (half + 1) * HALF)
                        nc.vector.tensor_tensor(qT[1][:, 0, cols], bank_of(f"q{half}")[:, :], fp(qT[0][:, 0, cols]),
                                                ALU.subtract).then_inc(m_free, 1)
                for n in range(N + 5):
                    if n < N:
                        dve.wait_ge(s_full, g * N + (n + 1))
                        scores = S[n % 2][:, :].rearrange("p (a t) -> p a t", a=4)
                        nc.vector.tensor_reduce(row_max[:, n % 2, :], scores, AX.X, ALU.max).then_inc(max_ready, 1)
                        dve.wait_ge(max_ready, g * N + (n + 1))
                        nc.vector.tensor_tensor(prob[:, n % 2, :].rearrange("p (a t) -> p a t", a=4), scores,
                                                row_max[:, n % 2, :].unsqueeze(2).broadcast_to([P, 4, P]), ALU.subtract).then_inc(s_free, 1)
                    if 0 <= n - 1 < N:
                        i = n - 1
                        dve.wait_ge(pT_high, g * N + (i + 1))
                        nc.vector.tensor_tensor(pT[1][:, i % 2, :], PT[i % 2][:, :], pT[0][:, i % 2, :], ALU.subtract).then_inc(pT_low, 1)
                    if ends(n - 2) is not None:
                        b = ends(n - 2)
                        r = b % 2
                        dve.wait_ge(pv_done, g * N + (n - 1))
                        sums = OB[r][:, 0:HEADS * VW].rearrange("p (h w) -> p h w", w=VW)
                        nc.vector.tensor_reduce(o_raw[:, r, :].rearrange("p (h e) -> p h e", h=HEADS),
                                                sums[:, :, 0:3 * DV].rearrange("p h (s e) -> p h e s", s=3), AX.X, ALU.add).then_inc(o_step, 1)
                        nc.vector.reciprocal(o_inv[:, r, :].unsqueeze(2), sums[:, :, 3 * DV:VW]).then_inc(o_step, 1)
                        dve.wait_ge(o_step, g * 2 * B + (2 * b + 2))
                        if own_kv:
                            out = o_sb[:, r, :].rearrange("p (h e m) -> p h m e", h=4, m=4)
                            raw = o_raw[:, r, :].rearrange("p (h m e) -> p h m e", h=4, m=4)
                            inv = o_inv[:, r, :].rearrange("p (h m) -> p h m", h=4).unsqueeze(3).broadcast_to([P, 4, 4, DV])
                        else:
                            out = o_sb[:, r, :].rearrange("p (h e) -> p h e", h=HEADS)
                            raw = o_raw[:, r, :].rearrange("p (h e) -> p h e", h=HEADS)
                            inv = o_inv[:, r, :].unsqueeze(2).broadcast_to([P, HEADS, DV])
                        nc.vector.tensor_tensor(out, raw, inv, ALU.mult).then_inc(o_free, 1)
                    if ends(n - 3) is not None:
                        b = ends(n - 3)
                        dve.wait_ge(m_high, high(g, f"t{b}") + 1)
                        src, hi, lo = bank_of(f"t{b}")[:, 0:P], fp(oT[0][:, b % 2, :]), oT[1][:, b % 2, :]
                        if own_kv:
                            nc.vector.scalar_tensor_tensor(lo, src, bias[:, 2:3], hi, ALU.add, ALU.subtract).then_inc(m_free, 1)
                        else:
                            nc.vector.tensor_tensor(lo, src, hi, ALU.subtract).then_inc(m_free, 1)
                    if ends(n - 4) is not None:
                        b = ends(n - 4)
                        dve.wait_ge(m_full, tile(g, f"o{b}") + 1)
                        nc.vector.tensor_tensor(c.x[:, b, :], bank_of(f"o{b}")[:, :], c.x[:, b, :], ALU.add).then_inc(m_free, 1)

class Chain:

    def __init__(self, eng, sem, base):
        self.eng, self.sem, self.base, self.n = eng, sem, base, 0

    def __call__(self, ins):
        ins.then_inc(self.sem, 1)
        self.n += 1
        self.eng.wait_ge(self.sem, self.base + self.n)


def moe_ffn(nc, c, d, layer):
    W = HB
    base = layer != 3
    t = f"f{layer}_"
    NA = LR + EXPERTS
    STEPS = {0: 12, 1: 9, 3: 6}[layer]
    with ExitStack() as ctx:
        def sb(name, shape, dt=F32):
            return ctx.enter_context(nc.sbuf_tensor(t + name, shape, dt))

        def pair(name, shape, dt=F32R):
            return sb(name + "_hi", shape, dt), sb(name + "_lo", shape, dt)

        def sem(name):
            return c.sem(t + name)

        n = layernorm_steps(nc, c, t, ctx, W)
        xnT = pair("xnT", [P, W, KC, P])
        wa_raw, wb_raw = sb("wa_raw", [P, KC, NA]), sb("wb_raw", [P, D])
        wa, wb = pair("wa", [P, KC, NA]), pair("wb", [P, D])
        raws, parts = [wa_raw[:, :, :], wb_raw[:, :]], [[x[:, :, :] for x in wa], [x[:, :] for x in wb]]
        if base:
            w0_raw, w0 = sb("w0_raw", [P, KC, D]), pair("w0", [P, KC, D])
            raws.append(w0_raw[:, :, :])
            parts.append([x[:, :, :] for x in w0])
            bias = sb("bias", [P, D])
        router_bias = sb("router_bias", [P, EXPERTS])
        logits, top, comb = sb("logits", [P, W, EXPERTS]), sb("top", [P, W, EXPERTS]), sb("comb", [P, W, EXPERTS])
        index, index_f = sb("index", [P, W, EXPERTS], U32), sb("index_f", [P, W, EXPERTS])
        chosen = sb("chosen", [P, W, EXPERTS])
        cum_terms, cum = sb("cum_terms", [P, W, EXPERTS, EXPERTS]), sb("cum", [P, W, EXPERTS])
        small = sb("small", [P, 5, W])
        hs = sb("hs", [P, W, LR])
        hT = pair("hT", [P, W, P])

        w_loaded = [sem(f"w{i}_loaded") for i in range(len(raws))]
        bias_loaded = sem("bias_loaded")
        w_high, w_low = sem("w_high"), sem("w_low")
        bias_added = sem("bias_added")
        h_full = sem("h_full")
        logits_done = sem("logits_done")
        step = sem("step")
        gap_ready, exp_ready = sem("gap_ready"), sem("exp_ready")
        hs_ready = sem("hs_ready")
        hT_full, hT_high, hT_low = sem("hT_full"), sem("hT_high"), sem("hT_low")
        out_full = sem("out_full")
        added = sem("added")

        block = ctx.enter_context(nc.Block())

        @block.sync
        def _(sp):
            sp.dma_start(wa_raw[:, :, :], d[f"L{layer}_wa"]).then_inc(w_loaded[0], 16)
            sp.dma_start(wb_raw[:, :], d[f"L{layer}_wb"]).then_inc(w_loaded[1], 16)
            if base:
                sp.dma_start(w0_raw[:, :, :], d[f"L{layer}_w0"]).then_inc(w_loaded[2], 16)
                sp.dma_start(bias[:, :], d[f"L{layer}_b0"].partition_broadcast(P).rearrange("p a n -> p (a n)")).then_inc(bias_loaded, 16)
            if layer == 1:
                sp.dma_start(router_bias[:, :], d["L1_br"].partition_broadcast(P).rearrange("p a n -> p (a n)")).then_inc(bias_loaded, 16)

        @block.gpsimd
        def _(pool):
            if base:
                pool.wait_ge(bias_loaded, 32 if layer == 1 else 16)
            with pool.Fori(0, B // W) as it:
                rstd_on_pool(nc, pool, n, c, it, W)
                if base:
                    for u in range(W):
                        pool.wait_ge(n.xn_ready, it * W + (u + 1))
                        xb = c.x[:, bass.ds(it * W + u, 1), :].rearrange("p a n -> p (a n)")
                        nc.gpsimd.tensor_tensor(xb, xb, bias[:, :], ALU.add).then_inc(bias_added, 1)

        @block.tensor
        def _(pe):
            with pe.Fori(0, B // W) as it:
                for u in range(W):
                    pe.wait_ge(n.xn_ready, it * W + (u + 1))
                    for k in range(KC):
                        ins = nc.tensor.transpose(c.bank[u][:, k * P:(k + 1) * P], n.xn[:, u, k * P:(k + 1) * P], c.ident)
                    ins.then_inc(n.xnT_full, 1)
                pe.wait_ge(w_low, len(raws))
                for u in range(W):
                    pe.wait_ge(n.xnT_low, it * W + (u + 1))
                    for k in range(KC):
                        ins = split_passes(nc, c.bank[u][:, 0:NA], [x[:, u, k, :] for x in xnT], [x[:, k, :] for x in wa],
                                           k == 0, k == KC - 1)
                    ins.then_inc(h_full, 1)
                if base:
                    for u in range(W):
                        for k in range(KC):
                            split_passes(nc, c.bank[4 + u][:, :], [x[:, u, k, :] for x in xnT], [x[:, k, :] for x in w0],
                                         k == 0, False)
                for u in range(W):
                    pe.wait_ge(hs_ready, it * W + (u + 1))
                    nc.tensor.transpose(c.bank[u][:, 0:P], hs[:, u, :], c.ident).then_inc(hT_full, 1)
                for u in range(W):
                    pe.wait_ge(hT_low, it * W + (u + 1))
                    split_passes(nc, c.bank[4 + u][:, :], [x[:, u, :] for x in hT], [x[:, :] for x in wb],
                                 not base, True).then_inc(out_full, 1)

        @block.scalar
        def _(act):
            for i, (raw, part) in enumerate(zip(raws, parts)):
                act.wait_ge(w_loaded[i], 16)
                nc.scalar.copy(part[0], raw).then_inc(w_high, 1)
            with act.Fori(0, B // W) as it:
                for u in range(W):
                    act.wait_ge(n.xnT_full, it * W + (u + 1))
                    nc.scalar.copy(xnT[0][:, u, :, :], c.bank[u][:, :].rearrange("p (k t) -> p k t", k=KC)).then_inc(n.xnT_high, 1)
                if layer == 0:
                    act.wait_ge(gap_ready, it + 1)
                    nc.scalar.activation(small[:, 1, :], small[:, 0, :], ACT.Exp).then_inc(exp_ready, 1)
                for u in range(W):
                    act.wait_ge(hT_full, it * W + (u + 1))
                    nc.scalar.copy(hT[0][:, u, :], c.bank[u][:, 0:P]).then_inc(hT_high, 1)

        @block.vector
        def _(dve):
            def each(x):
                return x.unsqueeze(2).broadcast_to([P, W, EXPERTS])

            def hot(i):
                return nc.vector.tensor_tensor(chosen[:, :, :], iota, each(index_f[:, :, i]), ALU.is_equal)

            iota = c.consts[:, IOTA:IOTA + EXPERTS].unsqueeze(1).broadcast_to([P, W, EXPERTS])
            for i, (raw, part) in enumerate(zip(raws, parts)):
                dve.wait_ge(w_high, i + 1)
                nc.vector.tensor_tensor(part[1], raw, fp(part[0]), ALU.subtract).then_inc(w_low, 1)
            if layer == 1:
                dve.wait_ge(bias_loaded, 32)
            with dve.Fori(0, B // W) as it:
                link = Chain(dve, step, it * STEPS)
                norm_on_vector(nc, dve, n, c, it, W, lambda u: c.x[:, bass.ds(it * W + u, 1), :].rearrange("p a n -> p (a n)"))
                for u in range(W):
                    dve.wait_ge(n.xnT_high, it * W + (u + 1))
                    nc.vector.tensor_tensor(xnT[1][:, u, :, :], c.bank[u][:, :].rearrange("p (k t) -> p k t", k=KC),
                                            fp(xnT[0][:, u, :, :]), ALU.subtract).then_inc(n.xnT_low, 1)
                for u in range(W):
                    dve.wait_ge(h_full, it * W + (u + 1))
                    if layer == 1:
                        ins = nc.vector.tensor_tensor(logits[:, u, :], c.bank[u][:, LR:NA], router_bias[:, :], ALU.add)
                    else:
                        ins = nc.vector.tensor_copy(logits[:, u, :], c.bank[u][:, LR:NA])
                link(ins)
                nc.vector.tensor_copy(c.scratch[:, :], c.ones[:, 0:1])
                for u in range(W):
                    ins = nc.vector.max(top[:, u, :], logits[:, u, :])
                link(ins)
                if layer == 1:
                    link(nc.vector.tensor_tensor(cum_terms[:, :, :, :], top[:, :, :].unsqueeze(2).broadcast_to([P, W, EXPERTS, EXPERTS]),
                                                 c.consts[:, TRI:TRI + 64].rearrange("p (k j) -> p k j", k=8).unsqueeze(1)
                                                 .broadcast_to([P, W, EXPERTS, EXPERTS]), ALU.mult))
                    link(nc.vector.tensor_reduce(cum[:, :, :], cum_terms[:, :, :, :], AX.X, ALU.add))
                    link(nc.vector.tensor_scalar(cum[:, :, :], cum[:, :, :], 1.0, None, ALU.subtract))
                    link(nc.vector.tensor_tensor(cum[:, :, :], cum[:, :, :], c.consts[:, RECK:RECK + 8].unsqueeze(1)
                                                 .broadcast_to([P, W, EXPERTS]), ALU.mult))
                    link(nc.vector.tensor_reduce(small[:, 0, :], cum[:, :, :], AX.X, ALU.max))
                    link(nc.vector.tensor_tensor(comb[:, :, :], logits[:, :, :], each(small[:, 0, :]), ALU.subtract))
                    link(nc.vector.tensor_scalar(comb[:, :, :], comb[:, :, :], 0.0, None, ALU.max))
                else:
                    nc.vector.tensor_copy(c.scratch[:, :], c.ones[:, 0:1])
                    for u in range(W):
                        ins = nc.vector.max_index(index[:, u, :], top[:, u, :], logits[:, u, :])
                    link(ins)
                    link(nc.vector.tensor_copy(index_f[:, :, :], index[:, :, :]))
                    if layer == 0:
                        nc.vector.tensor_tensor(small[:, 0, :], top[:, :, 1], top[:, :, 0], ALU.subtract).then_inc(gap_ready, 1)
                        link(hot(0))
                        dve.wait_ge(exp_ready, it + 1)
                        link(nc.vector.tensor_scalar(small[:, 2, :], small[:, 1, :], 1.0, 0.5, ALU.add, ALU.mult))
                        link(nc.vector.reciprocal(small[:, 3, :], small[:, 2, :]))
                        link(nc.vector.tensor_tensor(small[:, 4, :], small[:, 1, :], small[:, 3, :], ALU.mult))
                        link(nc.vector.tensor_tensor(comb[:, :, :], chosen[:, :, :], each(small[:, 3, :]), ALU.mult))
                        link(hot(1))
                        link(nc.vector.tensor_tensor(cum[:, :, :], chosen[:, :, :], each(small[:, 4, :]), ALU.mult))
                        link(nc.vector.tensor_tensor(comb[:, :, :], comb[:, :, :], cum[:, :, :], ALU.add))
                    else:
                        link(hot(0))
                        link(nc.vector.tensor_tensor(comb[:, :, :], chosen[:, :, :], each(top[:, :, 0]), ALU.mult))
                for u in range(W):
                    ins = nc.vector.tensor_tensor(hs[:, u, :].rearrange("p (e r) -> p e r", e=EXPERTS),
                                                  c.bank[u][:, 0:LR].rearrange("p (e r) -> p e r", e=EXPERTS),
                                                  comb[:, u, :].unsqueeze(2).broadcast_to([P, EXPERTS, RANK]), ALU.mult)
                    ins.then_inc(hs_ready, 1)
                for u in range(W):
                    dve.wait_ge(hT_high, it * W + (u + 1))
                    nc.vector.tensor_tensor(hT[1][:, u, :], c.bank[u][:, 0:P], fp(hT[0][:, u, :]), ALU.subtract).then_inc(hT_low, 1)
                for u in range(W):
                    dve.wait_ge(out_full, it * W + (u + 1))
                    if base:
                        dve.wait_ge(bias_added, it * W + (u + 1))
                    xb = c.x[:, bass.ds(it * W + u, 1), :].rearrange("p a n -> p (a n)")
                    nc.vector.tensor_tensor(xb, c.bank[4 + u][:, :], xb, ALU.add).then_inc(added, 1)
                assert link.n == STEPS, link.n


def context_attention(nc, c, d):
    W = HB
    t = "a2_"
    with ExitStack() as ctx:
        def sb(name, shape, dt=F32):
            return ctx.enter_context(nc.sbuf_tensor(t + name, shape, dt))

        def pair(name, shape, dt=F32R):
            return sb(name + "_hi", shape, dt), sb(name + "_lo", shape, dt)

        def sem(name):
            return c.sem(t + name)

        n = layernorm_steps(nc, c, t, ctx, W)
        xnT = pair("xnT", [P, W, KC, P])
        raw = sb("raw", [P, W, D])
        cx = pair("cx", [P, W, D])
        minus_max, sums, inv = sb("minus_max", [P, W]), sb("sums", [P, W]), sb("inv", [P, W])
        prob = sb("prob", [P, W, P])
        pT = pair("pT", [P, W, P])
        loaded = [sem(f"loaded{u}") for u in range(W)]
        cx_high, cx_low = sem("cx_high"), sem("cx_low")
        s_full, max_ready, p_ready, inv_ready = sem("s_full"), sem("max_ready"), sem("p_ready"), sem("inv_ready")
        pT_full, pT_high, pT_low = sem("pT_full"), sem("pT_high"), sem("pT_low")
        out_full, added = sem("out_full"), sem("added")
        block = ctx.enter_context(nc.Block())

        @block.sync
        def _(sp):
            for u in range(W):
                sp.dma_start(raw[:, u, :], d["ctx"][u]).then_inc(loaded[u], 16)
            for u in range(W):
                sp.wait_ge(cx_low, u + 1)
                sp.dma_start(raw[:, u, :], d["ctx"][W + u]).then_inc(loaded[u], 16)

        @block.gpsimd
        def _(pool):
            with pool.Fori(0, B // W) as it:
                rstd_on_pool(nc, pool, n, c, it, W)

        @block.tensor
        def _(pe):
            with pe.Fori(0, B // W) as it:
                for u in range(W):
                    pe.wait_ge(n.xn_ready, it * W + (u + 1))
                    for k in range(KC):
                        ins = nc.tensor.transpose(c.bank[u][:, k * P:(k + 1) * P], n.xn[:, u, k * P:(k + 1) * P], c.ident)
                    ins.then_inc(n.xnT_full, 1)
                for u in range(W):
                    pe.wait_ge(n.xnT_low, it * W + (u + 1))
                    for k in range(KC):
                        ins = split_passes(nc, c.bank[4 + u][:, 0:P], [x[:, u, k, :] for x in xnT],
                                           [x[:, k, bass.ds((it * W + u) * P, P)] for x in c.ctxT], k == 0, k == KC - 1)
                    ins.then_inc(s_full, 1)
                for u in range(W):
                    pe.wait_ge(p_ready, it * W + (u + 1))
                    nc.tensor.transpose(c.bank[4 + u][:, P:2 * P], prob[:, u, :], c.ident).then_inc(pT_full, 1)
                for u in range(W):
                    pe.wait_ge(pT_low, it * W + (u + 1))
                    pe.wait_ge(cx_low, it * W + (u + 1))
                    split_passes(nc, c.bank[u][:, :], [x[:, u, :] for x in pT], [x[:, u, :] for x in cx],
                                 True, True).then_inc(out_full, 1)

        @block.scalar
        def _(act):
            with act.Fori(0, B // W) as it:
                for u in range(W):
                    act.wait_ge(loaded[u], it * 16 + 16)
                    act.wait_ge(added, it * W + (u + 1))
                    nc.scalar.copy(cx[0][:, u, :], raw[:, u, :]).then_inc(cx_high, 1)
                for u in range(W):
                    act.wait_ge(n.xnT_full, it * W + (u + 1))
                    nc.scalar.copy(xnT[0][:, u, :, :], c.bank[u][:, :].rearrange("p (k t) -> p k t", k=KC)).then_inc(n.xnT_high, 1)
                for u in range(W):
                    act.wait_ge(max_ready, it * W + (u + 1))
                    nc.scalar.activation(prob[:, u, :], c.bank[4 + u][:, 0:P], ACT.Exp, bias=minus_max[:, u:u + 1],
                                         accum_out=sums[:, u:u + 1]).then_inc(p_ready, 1)
                for u in range(W):
                    act.wait_ge(pT_full, it * W + (u + 1))
                    nc.scalar.copy(pT[0][:, u, :], c.bank[4 + u][:, P:2 * P]).then_inc(pT_high, 1)

        @block.vector
        def _(dve):
            dve.sem_inc(added, W)
            with dve.Fori(0, B // W) as it:
                for u in range(W):
                    dve.wait_ge(cx_high, it * W + (u + 1))
                    nc.vector.tensor_tensor(cx[1][:, u, :], raw[:, u, :], fp(cx[0][:, u, :]), ALU.subtract).then_inc(cx_low, 1)
                norm_on_vector(nc, dve, n, c, it, W, lambda u: c.x[:, bass.ds(it * W + u, 1), :].rearrange("p a n -> p (a n)"))
                for u in range(W):
                    dve.wait_ge(n.xnT_high, it * W + (u + 1))
                    nc.vector.tensor_tensor(xnT[1][:, u, :, :], c.bank[u][:, :].rearrange("p (k t) -> p k t", k=KC),
                                            fp(xnT[0][:, u, :, :]), ALU.subtract).then_inc(n.xnT_low, 1)
                for u in range(W):
                    dve.wait_ge(s_full, it * W + (u + 1))
                    nc.vector.tensor_reduce(minus_max[:, u:u + 1], c.bank[4 + u][:, 0:P], AX.X, ALU.max, negate=True).then_inc(max_ready, 1)
                for u in range(W):
                    dve.wait_ge(p_ready, it * W + (u + 1))
                    nc.vector.reciprocal(inv[:, u:u + 1], sums[:, u:u + 1]).then_inc(inv_ready, 1)
                for u in range(W):
                    dve.wait_ge(pT_high, it * W + (u + 1))
                    nc.vector.tensor_tensor(pT[1][:, u, :], c.bank[4 + u][:, P:2 * P], fp(pT[0][:, u, :]), ALU.subtract).then_inc(pT_low, 1)
                dve.wait_ge(inv_ready, it * W + W)
                for u in range(W):
                    dve.wait_ge(out_full, it * W + (u + 1))
                    xb = c.x[:, bass.ds(it * W + u, 1), :].rearrange("p a n -> p (a n)")
                    nc.vector.scalar_tensor_tensor(xb, c.bank[u][:, :], inv[:, u:u + 1], xb, ALU.mult, ALU.add).then_inc(added, 1)


def gated_ffn(nc, c, d, xnT):
    t = "f2_"
    with ExitStack() as ctx:
        def sb(name, shape, dt=F32):
            return ctx.enter_context(nc.sbuf_tensor(t + name, shape, dt))

        def pair(name, shape, dt=F32R):
            return sb(name + "_hi", shape, dt), sb(name + "_lo", shape, dt)

        def sem(name):
            return c.sem(t + name)

        packed = sb("packed", [P, 3, D], I32)
        scales = sb("scales", [P, 3, D])
        shifts = sb("shifts", [P, 1 + D], I32)
        weight = sb("weight", [P, 3, D])
        parts = [pair(f"w{i}", [P, D]) for i in (1, 3, 2)]
        gate, hidden = sb("gate", [P, 2, HALF]), sb("hidden", [P, 2, HALF])
        hT = pair("hT", [P, TOK])
        shifts_loaded = sem("shifts_loaded")
        packed_loaded, scales_loaded = sem("packed_loaded"), sem("scales_loaded")
        shifted, unpacked = sem("shifted"), sem("unpacked")
        as_float = sem("as_float")
        weight_ready = sem("weight_ready")
        w_high, w_low = sem("w_high"), sem("w_low")
        w2_high, w2_low = sem("w2_high"), sem("w2_low")
        up_full = sem("up_full")
        gate_ready, hidden_ready, h_high, h_low = sem("gate_ready"), sem("hidden_ready"), sem("h_high"), sem("h_low")
        out_full, added = sem("out_full"), sem("added")
        UP, OUT = c.bank[0:4], c.bank[4:8]
        LAST = HCH - 1
        block = ctx.enter_context(nc.Block())

        @block.sync
        def _(sp):
            sp.dma_start(shifts[:, :], d["shifts"]).then_inc(shifts_loaded, 16)

            def load_packed(ch):
                sp.dma_start(packed[:, :, :], d["L2_packed"][bass.ds(ch, 1)].rearrange("a p w n -> (a p) w n")).then_inc(packed_loaded, 16)

            def load_scales(ch):
                for half in range(2):
                    src = d["L2_s13"][bass.ds(ch, 1), half:half + 1].rearrange("a h w n -> (a h) w n")
                    sp.dma_start(scales[64 * half:64 * half + 64, 0:2, :],
                                 src.partition_broadcast(64).rearrange("p a w n -> p (a w) n")).then_inc(scales_loaded, 16)
                for q in range(4):
                    src = d["L2_s2"][bass.ds(ch, 1), q:q + 1].rearrange("a q n -> (a q) n")
                    sp.dma_start(scales[32 * q:32 * q + 32, 2, :],
                                 src.partition_broadcast(32).rearrange("p a n -> p (a n)")).then_inc(scales_loaded, 16)

            load_packed(0)
            load_scales(0)
            with sp.Fori(1, HCH) as ch:
                sp.wait_ge(weight_ready, ch * 3)
                load_packed(ch)
                load_scales(ch)

        @block.gpsimd
        def _(pool):
            def scale(ch):
                pool.wait_ge(scales_loaded, ch * 96 + 96)
                for w in range(3):
                    pool.wait_ge(as_float, ch * 3 + (w + 1))
                    nc.gpsimd.tensor_tensor(weight[:, w, :], weight[:, w, :], scales[:, w, :], ALU.mult).then_inc(weight_ready, 1)

            def low(ch):
                for w in range(3):
                    if w < 2:
                        pool.wait_ge(w_high, ch * 2 + (w + 1))
                    else:
                        pool.wait_ge(w2_high, ch + 1)
                    nc.gpsimd.tensor_tensor(parts[w][1][:, :], weight[:, w, :], fp(parts[w][0][:, :]),
                                            ALU.subtract).then_inc(w_low if w < 2 else w2_low, 1)

            with pool.Fori(0, HCH) as ch:
                scale(ch)
                low(ch)

        @block.tensor
        def _(pe):
            def chunk(ch):
                pe.wait_ge(w_low, ch * 2 + 2)
                for half in range(2):
                    pe.wait_ge(hidden_ready, ch * 2 + (half + 1))
                    for w in range(2):
                        for k in range(KC):
                            ins = split_passes(nc, UP[2 * half + w][:, :], [x[:, k * P:(k + 1) * P] for x in parts[w]],
                                               [x[:, k, half * HALF:(half + 1) * HALF] for x in xnT], k == 0, k == KC - 1)
                        ins.then_inc(up_full, 1)
                pe.wait_ge(w2_low, ch + 1)
                for b in range(B):
                    if b % HB == 0:
                        pe.wait_ge(h_low, ch * 2 + (b // HB + 1))
                    pe.wait_ge(added, ch * B + (b + 1))
                    split_passes(nc, OUT[b % 4][:, :], [x[:, b * P:(b + 1) * P] for x in hT], [x[:, :] for x in parts[2]],
                                 True, True).then_inc(out_full, 1)

            with pe.Fori(0, HCH) as ch:
                chunk(ch)

        @block.scalar
        def _(act):
            def high(ch, w):
                act.wait_ge(weight_ready, ch * 3 + (w + 1))
                nc.scalar.copy(parts[w][0][:, :], weight[:, w, :]).then_inc(w_high if w < 2 else w2_high, 1)

            def to_float(ch):
                for w in range(3):
                    act.wait_ge(unpacked, ch * 3 + (w + 1))
                    nc.scalar.copy(weight[:, w, :], packed[:, w, :]).then_inc(as_float, 1)

            def chunk(ch, more):
                if more:
                    act.wait_ge(w_low, ch * 2 + 2)
                    act.wait_ge(w2_low, ch + 1)
                    to_float(ch + 1)
                for half in range(2):
                    act.wait_ge(up_full, ch * 4 + (2 * half + 1))
                    nc.scalar.activation(gate[:, half, :], UP[2 * half][:, :], ACT.Silu).then_inc(gate_ready, 1)
                    act.wait_ge(hidden_ready, ch * 2 + (half + 3))
                    nc.scalar.copy(hT[0][:, half * HALF:(half + 1) * HALF], hidden[:, half, :]).then_inc(h_high, 1)
                if more:
                    act.wait_ge(up_full, ch * 4 + 4)
                    high(ch + 1, 0)
                    high(ch + 1, 1)
                    act.wait_ge(out_full, ch * B + B)
                    high(ch + 1, 2)

            to_float(0)
            high(0, 0)
            high(0, 1)
            high(0, 2)
            with act.Fori(0, LAST) as ch:
                chunk(ch, True)
            chunk(LAST, False)

        @block.vector
        def _(dve):
            def unpack(ch):
                dve.wait_ge(packed_loaded, ch * 16 + 16)
                for w in range(3):
                    by = shifts[:, 0:1].broadcast_to([P, D]) if w < 2 else shifts[:, 1:1 + D]
                    nc.vector.tensor_tensor(packed[:, w, :], packed[:, w, :], by, ALU.logical_shift_left).then_inc(shifted, 1)
                for w in range(3):
                    dve.wait_ge(shifted, ch * 3 + (w + 1))
                    nc.vector.tensor_scalar(packed[:, w, :], packed[:, w, :], 28, None, ALU.arith_shift_right).then_inc(unpacked, 1)

            def chunk(ch, more):
                if more:
                    unpack(ch + 1)
                for half in range(2):
                    dve.wait_ge(up_full, ch * 4 + (2 * half + 2))
                    dve.wait_ge(gate_ready, ch * 2 + (half + 1))
                    nc.vector.tensor_tensor(hidden[:, half, :], UP[2 * half + 1][:, :], gate[:, half, :], ALU.mult).then_inc(hidden_ready, 1)
                    dve.wait_ge(h_high, ch * 2 + (half + 1))
                    cols = slice(half * HALF, (half + 1) * HALF)
                    nc.vector.tensor_tensor(hT[1][:, cols], hidden[:, half, :], fp(hT[0][:, cols]), ALU.subtract).then_inc(h_low, 1)
                for b in range(B):
                    dve.wait_ge(out_full, ch * B + (b + 1))
                    nc.vector.tensor_tensor(c.x[:, b, :], OUT[b % 4][:, :], c.x[:, b, :], ALU.add).then_inc(added, 1)
            dve.sem_inc(hidden_ready, 2)
            dve.sem_inc(added, 4)
            dve.wait_ge(shifts_loaded, 16)
            unpack(0)
            with dve.Fori(0, LAST) as ch:
                chunk(ch, True)
            chunk(LAST, False)


def wide_head_attention(nc, c, d, xnT):
    G, H = 8, 4
    t = "a3_"
    SCALE = P ** -0.5
    N = B
    LAGS = 5
    with ExitStack() as ctx:
        def sb(name, shape, dt=F32):
            return ctx.enter_context(nc.sbuf_tensor(t + name, shape, dt))

        def pair(name, shape, dt=F32R):
            return sb(name + "_hi", shape, dt), sb(name + "_lo", shape, dt)

        def sem(name):
            return c.sem(t + name)

        raw = sb("raw", [P, 4 * D])
        wq, wo = pair("wq", [P, KC, H * P]), pair("wo", [P, H, D])
        wkv = pair("wkv", [P, 2 * KC, P])
        norms = sb("norms", [P, 2])
        mask = sb("mask", [P, P])
        square = sb("square", [P, 2, HALF])
        qT = pair("qT", [P, H, TOK])
        kT = pair("kT", [P, TOK])
        v = pair("v", [P, B, P])
        held = sb("held", [P, TOK])
        diag = sb("diag", [P, HB, P])
        var_q, rq = sb("var_q", [P, B, H]), sb("rq", [P, B, H])
        var_k, rk = sb("var_k", [P, B]), sb("rk", [P, B])
        minus_max, sums, inv = sb("minus_max", [P, 3, H]), sb("sums", [P, 3, H]), sb("inv", [P, 3, H])
        prob = sb("prob", [P, 3, H, P])
        pT = pair("pT", [P, HALF])
        oT = pair("oT", [P, H, P])

        once_loaded = sem("once_loaded")
        raw_loaded = sem("raw_loaded")
        raw_high = sem("raw_high")
        raw_split = sem("raw_split")
        m_full, m_high = sem("m_full"), sem("m_high")
        m_free = sem("m_free")
        ss_done = sem("ss_done")
        var_ready = sem("var_ready")
        rms_ready = sem("rms_ready")
        rq_ready, diag_ready = sem("rq_ready"), sem("diag_ready")
        k_high, k_low = sem("k_high"), sem("k_low")
        s_full = sem("s_full")
        s_free = sem("s_free")
        max_ready, exp_ready, inv_ready = sem("max_ready"), sem("exp_ready"), sem("inv_ready")
        p_ready = sem("p_ready")
        pT_full, pT_high, pT_low = sem("pT_full"), sem("pT_high"), sem("pT_low")
        o_full, o_high, o_low = sem("o_full"), sem("o_high"), sem("o_low")
        S, PT, OB, M = c.bank[0:2], c.bank[2:4], c.bank[4:6], c.bank[6:8]

        order = ["v0", "v1", "w0", "w1", "k0", "k1"] + [f"q{h}{a}" for h in range(2) for a in range(H)] + ["r0", "r1"]
        order += [f"o{b}" for b in range(B)]
        by_act = [x for x in order if x[0] in "wkq"]
        squares = [x for x in order if x[0] in "kq"]
        USES = 2 + N
        assert len(order) % 2 == 0 and len(squares) % 2 == 0

        def tile(g, name):
            return g * len(order) + order.index(name)

        def high(g, name):
            return g * len(by_act) + by_act.index(name)

        def squared(g, name):
            return g * len(squares) + squares.index(name)

        def bank_of(name):
            return M[order.index(name) % 2]

        block = ctx.enter_context(nc.Block())

        @block.sync
        def _(sp):
            sp.dma_start(norms[:, :], d["L3_norms"]).then_inc(once_loaded, 16)
            sp.dma_start(mask[:, :], d["mask"]).then_inc(once_loaded, 16)

            def load(g, name, width):
                sp.dma_start(raw[:, 0:width], d[name][bass.ds(g, 1)].rearrange("a p n -> (a p) n")).then_inc(raw_loaded, 16)

            load(0, "L3_wkv", 2 * D)
            sp.wait_ge(raw_split, 1)
            load(0, "L3_wq", 4 * D)
            sp.wait_ge(raw_split, 2)
            load(0, "L3_wo", 4 * D)
            with sp.Fori(1, G) as g:
                sp.wait_ge(raw_split, g * 3)
                load(g, "L3_wkv", 2 * D)
                sp.wait_ge(raw_split, g * 3 + 1)
                load(g, "L3_wq", 4 * D)
                sp.wait_ge(raw_split, g * 3 + 2)
                load(g, "L3_wo", 4 * D)

        @block.gpsimd
        def _(pool):
            def split(g, n, w, width):
                pool.wait_ge(raw_loaded, g * 48 + (n * 16 + 16))
                nc.gpsimd.tensor_tensor(w[0], raw[:, 0:width], c.ones[:, 0:1].broadcast_to([P, width]), ALU.mult).then_inc(raw_high, 1)
                pool.wait_ge(raw_high, g * 3 + (n + 1))
                nc.gpsimd.tensor_tensor(w[1], raw[:, 0:width], fp(w[0]), ALU.subtract).then_inc(raw_split, 1)

            def flat(w):
                return [x[:, :, :].rearrange("p a n -> p (a n)") for x in w]

            def split_kv_q(g):
                split(g, 0, flat(wkv), 2 * D)
                split(g, 1, flat(wq), 4 * D)

            def group(g):
                split(g, 2, flat(wo), 4 * D)
                pool.wait_ge(var_ready, g * 2 + 1)
                nc.gpsimd.tensor_tensor(rk[:, :], var_k[:, :], c.minus_half[:, 0:B], ALU.pow).then_inc(rms_ready, 1)
                pool.wait_ge(var_ready, g * 2 + 2)
                nc.gpsimd.tensor_tensor(rq[:, :, :].rearrange("p b h -> p (b h)"), var_q[:, :, :].rearrange("p b h -> p (b h)"),
                                        c.minus_half[:, 0:B * H], ALU.pow).then_inc(rms_ready, 1)
                for b in range(B):
                    pool.wait_ge(inv_ready, g * N + (b + 1))
                    pool.wait_ge(exp_ready, g * N + (b + 1))
                    nc.gpsimd.tensor_tensor(prob[:, b % 3, :, :], prob[:, b % 3, :, :],
                                            inv[:, b % 3, :].unsqueeze(2).broadcast_to([P, H, P]), ALU.mult).then_inc(p_ready, 1)

            split_kv_q(0)
            group(0)
            with pool.Fori(1, G) as g:
                pool.wait_ge(m_free, tile(g - 1, f"o{B - 1}") + 3)
                split_kv_q(g)
                group(g)

        @block.tensor
        def _(pe):
            def take(g, name):
                pe.wait_ge(m_free, tile(g, name) + 1)
                return bank_of(name)

            def transposed(g, name, w, rhs, half):
                bank = take(g, name)
                for k in range(KC):
                    ins = split_passes(nc, bank[:, :], [x[k] for x in w], [x[:, k, half * HALF:(half + 1) * HALF] for x in rhs],
                                       k == 0, k == KC - 1)
                ins.then_inc(m_full, 1)

            def sums_of_squares(g, name):
                half = int(name[1])
                pe.wait_ge(m_high, high(g, name) + 1)
                for u in range(HB):
                    b = half * HB + u
                    out = S[0][:, b:b + 1] if name[0] == "k" else S[1][:, b * H + int(name[2]):b * H + int(name[2]) + 1]
                    ins = nc.tensor.matmul(out, square[:, squares.index(name) % 2, u * P:(u + 1) * P], c.ones[:, 0:1],
                                           start=True, stop=True)
                ins.then_inc(ss_done, 1)

            pe.wait_ge(once_loaded, 32)
            with pe.Fori(0, G) as g:
                pe.wait_ge(raw_split, g * 3 + 1)
                for half in range(2):
                    transposed(g, f"v{half}", [[x[:, KC + k, :] for k in range(KC)] for x in wkv], c.ctxT, half)
                for half in range(2):
                    bank = take(g, f"w{half}")
                    pe.wait_ge(m_free, tile(g, f"v{half}") + 3)
                    for u in range(HB):
                        b = half * HB + u
                        ins = nc.tensor.transpose(bank[:, u * P:(u + 1) * P], held[:, b * P:(b + 1) * P], c.ident)
                    ins.then_inc(m_full, 1)
                for half in range(2):
                    transposed(g, f"k{half}", [[x[:, k, :] for k in range(KC)] for x in wkv], c.ctxT, half)
                pe.wait_ge(raw_split, g * 3 + 2)
                pe.wait_ge(s_free, g * USES + 1)
                before = ["k0", "k1"]
                for half in range(2):
                    for a in range(H):
                        transposed(g, f"q{half}{a}", [[x[:, k, a * P:(a + 1) * P] for k in range(KC)] for x in wq], xnT, half)
                        name = before.pop(0)
                        sums_of_squares(g, name)
                        before.append(f"q{half}{a}")
                for name in before:
                    sums_of_squares(g, name)
                for half in range(2):
                    bank = take(g, f"r{half}")
                    pe.wait_ge(diag_ready, g * 2 + (half + 1))
                    nc.tensor.matmul(bank[:, :], c.ones[:, :], diag[:, :, :].rearrange("p a n -> p (a n)"),
                                     start=True, stop=True).then_inc(m_full, 1)
                for n in range(N + LAGS):
                    if n < N:
                        if n == 0:
                            pe.wait_ge(k_low, g * 2 + 2)
                            pe.wait_ge(m_free, tile(g, "q13") + 3)
                        pe.wait_ge(s_free, g * USES + (n + 3))
                        tok = slice(n * P, (n + 1) * P)
                        for h in range(H):
                            ins = split_passes(nc, S[n % 2][:, h * P:(h + 1) * P], [x[:, h, tok] for x in qT], [x[:, tok] for x in kT],
                                               True, True)
                        ins.then_inc(s_full, 1)
                    if 0 <= n - 4 < N:
                        b = n - 4
                        if b == 0:
                            pe.wait_ge(raw_split, g * 3 + 3)
                        bank = take(g, f"o{b}")
                        pe.wait_ge(o_low, g * N + (b + 1))
                        for h in range(H):
                            ins = split_passes(nc, bank[:, :], [x[:, h, :] for x in oT], [x[:, h, :] for x in wo], h == 0, h == H - 1)
                        ins.then_inc(m_full, 1)
                    if 0 <= n - 3 < N:
                        b = n - 3
                        pe.wait_ge(pT_low, g * N + (b + 1))
                        split_passes(nc, OB[b % 2][:, :], [x[:, b, :] for x in v], [x[:, :] for x in pT], True, True).then_inc(o_full, 1)
                    if 0 <= n - 2 < N:
                        b = n - 2
                        pe.wait_ge(p_ready, g * N + (b + 1))
                        for h in range(H):
                            ins = nc.tensor.transpose(PT[b % 2][:, h * P:(h + 1) * P], prob[:, b % 3, h, :], c.ident)
                        ins.then_inc(pT_full, 1)

        @block.scalar
        def _(act):
            def copy_and_square(g, name, out, factor):
                half = int(name[1])
                act.wait_ge(m_full, tile(g, name) + 1)
                if out is not None:
                    nc.scalar.activation(out, bank_of(name)[:, :], ACT.Copy, scale=factor)
                act.wait_ge(ss_done, squared(g, name) + 1)
                nc.scalar.activation(square[:, squares.index(name) % 2, :], bank_of(name)[:, :], ACT.Square).then_inc(m_high, 1)

            act.sem_inc(ss_done, 2)
            act.wait_ge(once_loaded, 32)
            with act.Fori(0, G) as g:
                for half in range(2):
                    act.wait_ge(m_full, tile(g, f"w{half}") + 1)
                    nc.scalar.copy(v[0][:, half * HB:(half + 1) * HB, :], bank_of(f"w{half}")[:, :]
                                   .rearrange("p (b n) -> p b n", b=HB)).then_inc(m_high, 1)
                for half in range(2):
                    copy_and_square(g, f"k{half}", None, None)
                for half in range(2):
                    for a in range(H):
                        copy_and_square(g, f"q{half}{a}", qT[0][:, a, half * HALF:(half + 1) * HALF], norms[:, 0:1])
                for half in range(2):
                    act.wait_ge(m_free, tile(g, f"r{half}") + 3)
                    cols = slice(half * HALF, (half + 1) * HALF)
                    nc.scalar.copy(kT[0][:, cols], held[:, cols]).then_inc(k_high, 1)
                for n in range(N + LAGS):
                    if n < N:
                        act.wait_ge(max_ready, g * N + (n + 1))
                        for h in range(H):
                            ins = nc.scalar.activation(prob[:, n % 3, h, :], prob[:, n % 3, h, :], ACT.Exp,
                                                       bias=minus_max[:, n % 3, h:h + 1], accum_out=sums[:, n % 3, h:h + 1])
                        ins.then_inc(exp_ready, 1)
                    if 0 <= n - 2 < N:
                        b = n - 2
                        act.wait_ge(pT_full, g * N + (b + 1))
                        nc.scalar.copy(pT[0][:, :], PT[b % 2][:, :]).then_inc(pT_high, 1)
                    if 0 <= n - 3 < N:
                        b = n - 3
                        act.wait_ge(o_full, g * N + (b + 1))
                        nc.scalar.copy(oT[0][:, :, :], OB[b % 2][:, :].rearrange("p (h t) -> p h t", h=H)).then_inc(o_high, 1)

        @block.vector
        def _(dve):
            dve.sem_inc(m_free, 2)
            dve.sem_inc(s_free, 2)
            dve.wait_ge(once_loaded, 32)
            with dve.Fori(0, G) as g:
                for half in range(2):
                    dve.wait_ge(m_full, tile(g, f"v{half}") + 1)
                    nc.vector.tensor_copy(held[:, half * HALF:(half + 1) * HALF], bank_of(f"v{half}")[:, :]).then_inc(m_free, 1)
                for half in range(2):
                    dve.wait_ge(m_high, high(g, f"w{half}") + 1)
                    part = slice(half * HB, (half + 1) * HB)
                    nc.vector.tensor_tensor(v[1][:, part, :], bank_of(f"w{half}")[:, :].rearrange("p (b n) -> p b n", b=HB),
                                            fp(v[0][:, part, :]), ALU.subtract).then_inc(m_free, 1)
                for half in range(2):
                    dve.wait_ge(m_high, high(g, f"k{half}") + 1)
                    nc.vector.tensor_scalar(held[:, half * HALF:(half + 1) * HALF], bank_of(f"k{half}")[:, :], norms[:, 1:2], None,
                                            ALU.mult).then_inc(m_free, 1)
                for half in range(2):
                    for a in range(H):
                        name = f"q{half}{a}"
                        cols = slice(half * HALF, (half + 1) * HALF)
                        dve.wait_ge(m_high, high(g, name) + 1)
                        nc.vector.scalar_tensor_tensor(qT[1][:, a, cols], bank_of(name)[:, :], norms[:, 0:1], fp(qT[0][:, a, cols]),
                                                       ALU.mult, ALU.subtract).then_inc(m_free, 1)
                        if name == "q01":
                            dve.wait_ge(ss_done, squared(g, "k1") + 3)
                            nc.vector.tensor_scalar(var_k[:, :], S[0][:, 0:B], 1.0 / P, EPS, ALU.mult, ALU.add).then_inc(var_ready, 1)
                        if name == "q10":
                            dve.wait_ge(rms_ready, g * 2 + 1)
                            nc.vector.tensor_tensor(diag[:, :, :], c.ident.unsqueeze(1).broadcast_to([P, HB, P]),
                                                    rk[:, 0:HB].unsqueeze(2).broadcast_to([P, HB, P]), ALU.mult).then_inc(diag_ready, 1)
                dve.wait_ge(ss_done, squared(g, "q13") + 3)
                nc.vector.tensor_scalar(var_q[:, :, :].rearrange("p b h -> p (b h)"), S[1][:, 0:B * H], 1.0 / P, EPS,
                                        ALU.mult, ALU.add).then_inc(var_ready, 1)
                dve.wait_ge(var_ready, g * 2 + 2)
                dve.sem_inc(s_free, 2)
                for half in range(2):
                    dve.wait_ge(m_full, tile(g, f"r{half}") + 1)
                    if half == 0:
                        nc.vector.tensor_tensor(diag[:, :, :], c.ident.unsqueeze(1).broadcast_to([P, HB, P]),
                                                rk[:, HB:B].unsqueeze(2).broadcast_to([P, HB, P]), ALU.mult).then_inc(diag_ready, 1)
                    cols = slice(half * HALF, (half + 1) * HALF)
                    nc.vector.tensor_tensor(held[:, cols], bank_of(f"r{half}")[:, :], held[:, cols], ALU.mult).then_inc(m_free, 1)
                for half in range(2):
                    cols = slice(half * HALF, (half + 1) * HALF)
                    dve.wait_ge(k_high, g * 2 + (half + 1))
                    nc.vector.tensor_tensor(kT[1][:, cols], held[:, cols], fp(kT[0][:, cols]), ALU.subtract).then_inc(k_low, 1)
                dve.wait_ge(rms_ready, g * 2 + 2)
                nc.vector.tensor_scalar(rq[:, :, :], rq[:, :, :], SCALE, None, ALU.mult).then_inc(rq_ready, 1)
                dve.wait_ge(rq_ready, g + 1)
                for n in range(N + LAGS):
                    if n < N:
                        r = n % 3
                        dve.wait_ge(s_full, g * N + (n + 1))
                        for h in range(H):
                            ins = nc.vector.scalar_tensor_tensor(prob[:, r, h, :], S[n % 2][:, h * P:(h + 1) * P], rq[:, n, h:h + 1],
                                                                 mask[:, :], ALU.mult, ALU.add)
                        ins.then_inc(s_free, 1)
                        dve.wait_ge(s_free, g * USES + (n + 5))
                        nc.vector.tensor_reduce(minus_max[:, r, :], prob[:, r, :, :], AX.X, ALU.max, negate=True).then_inc(max_ready, 1)
                    if 0 <= n - 1 < N:
                        r = (n - 1) % 3
                        dve.wait_ge(exp_ready, g * N + n)
                        nc.vector.reciprocal(inv[:, r, :], sums[:, r, :]).then_inc(inv_ready, 1)
                    if 0 <= n - 2 < N:
                        b = n - 2
                        dve.wait_ge(pT_high, g * N + (b + 1))
                        nc.vector.tensor_tensor(pT[1][:, :], PT[b % 2][:, :], fp(pT[0][:, :]), ALU.subtract).then_inc(pT_low, 1)
                    if 0 <= n - 3 < N:
                        b = n - 3
                        dve.wait_ge(o_high, g * N + (b + 1))
                        nc.vector.tensor_tensor(oT[1][:, :, :], OB[b % 2][:, :].rearrange("p (h t) -> p h t", h=H),
                                                fp(oT[0][:, :, :]), ALU.subtract).then_inc(o_low, 1)
                    if 0 <= n - 4 < N:
                        b = n - 4
                        dve.wait_ge(m_full, tile(g, f"o{b}") + 1)
                        nc.vector.tensor_tensor(c.x[:, b, :], bank_of(f"o{b}")[:, :], c.x[:, b, :], ALU.add).then_inc(m_free, 1)

def build(nc, d, upto=range(8)):
    with ExitStack() as ctx:
        c = Chip()
        in_use = []

        def new_semaphore(name):
            in_use.append(nc.alloc_semaphore(name))
            return in_use[-1]

        def clear_semaphores():
            nc.clear_and_free_semaphores(in_use)
            in_use.clear()
            nc.all_engine_barrier()

        c.sem = new_semaphore
        c.x = ctx.enter_context(nc.sbuf_tensor("x", [P, B, D], F32))
        c.ctxT = [ctx.enter_context(nc.sbuf_tensor(f"ctxT_{n}", [P, KC, TOK], F32R)) for n in ("hi", "lo")]
        c.consts = ctx.enter_context(nc.sbuf_tensor("consts_sb", [P, CONSTS], F32))
        c.ones = ctx.enter_context(nc.sbuf_tensor("ones", [P, P], F32))
        c.scratch = ctx.enter_context(nc.sbuf_tensor("scratch", [P, 1], F32))
        c.minus_half = ctx.enter_context(nc.sbuf_tensor("minus_half", [P, 40], F32))
        c.ident = c.consts[:, IDENT:IDENT + P]
        c.bank = [ctx.enter_context(nc.psum_tensor(f"bank{n}", [P, HALF], F32)) for n in range(8)]
        load_inputs(nc, c, d)

        def with_xnT(t, body, bias=None):
            with ExitStack() as inner:
                xnT = [inner.enter_context(nc.sbuf_tensor(f"{t}_{n}", [P, KC, TOK], F32R)) for n in ("xnT_hi", "xnT_lo")]
                norm_transpose(nc, c, d, t + "_", xnT, bias)
                body(xnT)

        steps = [
            lambda: with_xnT("n0", lambda xnT: small_head_attention(nc, c, d, 0, xnT)),
            lambda: moe_ffn(nc, c, d, 0),
            lambda: with_xnT("n1", lambda xnT: small_head_attention(nc, c, d, 1, xnT), "L1_bo"),
            lambda: moe_ffn(nc, c, d, 1),
            lambda: context_attention(nc, c, d),
            lambda: with_xnT("n2", lambda xnT: gated_ffn(nc, c, d, xnT)),
            lambda: with_xnT("n3", lambda xnT: wide_head_attention(nc, c, d, xnT)),
            lambda: moe_ffn(nc, c, d, 3),
        ]
        for n, step in enumerate(steps):
            if n in upto:
                step()
                clear_semaphores()
        store_output(nc, c, d)


def layouts(a):
    f = {n: np.asarray(v) for n, v in a.items()}
    o = {"x": f["x"], "consts": constants()}

    def rows(w, n=KC):
        return w.reshape(n, P, -1).transpose(1, 0, 2)

    ctx = f["ctx_4096"]
    o["ctxT"] = rows(ctx.transpose(2, 0, 1).reshape(D, TOK))
    o["ctx"] = ctx
    o["mask"] = f["mask_1x1xSxS2_ff0"].reshape(P, P)
    o["L0_wq"] = f["L0_xattn_Wq"].reshape(KC, P, 8, 4, 16).transpose(3, 1, 0, 2, 4).reshape(4, P, KC, P)
    o["L0_wkv"] = np.concatenate([rows(f["L0_xattn_Wk"]), rows(f["L0_xattn_Wv"])], 1)
    o["L0_wo"] = f["L0_xattn_Wo"].reshape(8, 4, 16, D).transpose(1, 0, 2, 3).reshape(4, P, D)
    o["L1_wqkv"] = np.stack([f[f"L1_xattn_W{n}"].reshape(KC, P, D) for n in "qkv"], 2)
    o["L1_wo"] = f["L1_xattn_Wo"].T.reshape(KC, P, D)
    o["L1_bias"] = np.stack([f[f"L1_xattn_b{n}"].reshape(KC, P).T for n in "qkv"], 2)
    o["L1_bo"] = f["L1_xattn_bo"].reshape(1, D)
    inter = np.broadcast_to(f["L1_xattn_interference"].reshape(KC, 4, 1, 4, 4), (KC, 4, 8, 4, 4))
    o["L1_inter"] = inter.reshape(KC, P, 4).transpose(1, 0, 2)
    o["L1_amp"] = np.broadcast_to(f["L1_xattn_amp"].reshape(1, 1), (P, 1))
    for n, a, r, bb in ((0, f["L0_ffn_A_stack"], "L0_ffn_W_router", f["L0_ffn_B_stack"].transpose(0, 2, 1)),
                        (1, f["L1_ffn_lora_A"].transpose(0, 2, 1), "L1_ffn_W_router", f["L1_ffn_lora_B"]),
                        (3, f["L3_ffn_A"], "L3_ffn_route_w", f["L3_ffn_Bw"].transpose(0, 2, 1))):
        o[f"L{n}_wa"] = rows(np.concatenate([a.reshape(LR, D), f[r]]).T)
        o[f"L{n}_wb"] = bb.reshape(LR, D)
        if n != 3:
            o[f"L{n}_w0"] = rows(f[f"L{n}_ffn_W_base"].T)
            o[f"L{n}_b0"] = f[f"L{n}_ffn_b_base"].reshape(1, D)
    o["L1_br"] = f["L1_ffn_b_router"].reshape(1, EXPERTS)

    pad = HCH * P - HIDDEN
    w13 = []
    for n in (1, 3):
        w = f[f"L2_ffn_w{n}"].reshape(HIDDEN, KC, 64).transpose(2, 1, 0)
        w = np.concatenate([w, w])
        w13.append(np.pad(w, ((0, 0), (0, 0), (0, pad))).reshape(P, KC, HCH, P).transpose(2, 0, 1, 3).reshape(HCH, P, D))
    blocks = HIDDEN // 32
    u = blocks * np.arange(D)[None, :] + np.arange(blocks)[:, None]
    w2 = f["L2_ffn_w2"].reshape(-1, 2, 32)[u // 4, u % 2]
    w2 = np.pad(w2.transpose(0, 2, 1).reshape(HIDDEN, D), ((0, pad), (0, 0))).reshape(HCH, P, D)
    o["L2_packed"] = np.stack([*w13, w2], 2)
    s13 = []
    for n in (1, 3):
        s = np.pad(f[f"L2_ffn_s{n}"].reshape(HIDDEN, KC, 2), ((0, pad), (0, 0), (0, 0)))
        s13.append(s.reshape(HCH, P, KC, 2).transpose(0, 3, 2, 1).reshape(HCH, 2, D))
    o["L2_s13"] = np.stack(s13, 2)
    o["L2_s2"] = np.pad(f["L2_ffn_s2"][u // 2], ((0, pad // 32), (0, 0))).reshape(HCH, 4, D)
    upper13 = np.arange(P)[:, None] < 64
    upper2 = (blocks * np.arange(D)[None, :] + np.arange(P)[:, None] // 32) % 4 < 2
    o["shifts"] = np.where(np.concatenate([upper13, upper2], 1), 24, 28).astype(np.int32)

    wq = f["L3_xattn_q_proj_w"].reshape(8, 4 * P, KC, P).transpose(0, 3, 2, 1)
    o["L3_wq"] = wq.reshape(8, P, 4 * D)
    wkv = [f[f"L3_xattn_{n}_proj_w"].reshape(8, P, KC, P).transpose(0, 3, 2, 1).reshape(8, P, D) for n in "kv"]
    o["L3_wkv"] = np.concatenate(wkv, 2)
    o["L3_wo"] = f["L3_xattn_o_proj_w"].reshape(D, 8, 4, P).transpose(1, 3, 2, 0).reshape(8, P, 4 * D)
    o["L3_norms"] = np.stack([f["L3_xattn_q_norm_w"], f["L3_xattn_k_norm_w"]], 1)
    return {n: np.ascontiguousarray(v) for n, v in o.items()}


def kernel(**inputs):
    import concourse.bacc as bacc
    from concourse.bass_utils import run_bass_kernel_spmd

    arrays = layouts(inputs)
    nc = bacc.Bacc("TRN2", target_bir_lowering=False, num_devices=1)
    d = {n: nc.dram_tensor(f"in_{n}", v.shape, mybir.dt.from_np(v.dtype), kind="ExternalInput").ap() for n, v in arrays.items()}
    d["out"] = nc.dram_tensor("out_x", (B, P, D), F32, kind="ExternalOutput").ap()
    build(nc, d)
    r = run_bass_kernel_spmd(nc, [{f"in_{n}": v for n, v in arrays.items()}], core_ids=[0])
    return r.results[0]["out_x"]
```

```python
from contextlib import ExitStack

import numpy as np

import concourse.bass as bass
from concourse import mybir
from concourse.alu_op_type import AluOpType as ALU

ACT = mybir.ActivationFunctionType
AX = mybir.AxisListType
F32 = mybir.dt.float32
F32R = mybir.dt.float32r
F16 = mybir.dt.float16
BF16 = mybir.dt.bfloat16
I32 = mybir.dt.int32
U32 = mybir.dt.uint32

P = 128
B = 8
D = 512
KC = D // P
TOK = B * P
HALF = TOK // 2
HB = B // 2
EPS = 1e-5
EXPERTS, RANK = 8, 16
LR = EXPERTS * RANK
HIDDEN = 1376
HCH = -(-HIDDEN // P)
PASSES = ((0, 0), (0, 1), (1, 0))


class Chip:
    pass


def split_passes(nc, out, stationary, moving, first, last):
    for n, (s, m) in enumerate(PASSES):
        ins = nc.tensor.matmul(out, stationary[s], moving[m], start=first and n == 0, stop=last and n == 2)
    return ins


def fp(ap):
    return ap.bitcast(F32)


def load_inputs(nc, c, d):
    with ExitStack() as ctx:
        raw = ctx.enter_context(nc.sbuf_tensor("ctx_raw", [P, KC, TOK], F32))
        loaded = c.sem("in_loaded")
        ctx_loaded = c.sem("ctx_loaded")
        high = c.sem("ctx_high")
        low = c.sem("ctx_low")
        block = ctx.enter_context(nc.Block())

        @block.sync
        def _(sp):
            for k in range(KC):
                sp.dma_start(raw[:, k, :], d["ctxT"][:, k, :]).then_inc(ctx_loaded, 16)
            sp.dma_start(c.x[:, :, :], d["x"].rearrange("b p n -> p b n")).then_inc(loaded, 16)
            sp.dma_start(c.consts[:, :], d["consts"]).then_inc(loaded, 16)
            sp.wait_ge(loaded, 32)

        @block.gpsimd
        def _(pool):
            nc.gpsimd.memset(c.ones[:, :], 1.0)
            nc.gpsimd.memset(c.minus_half[:, :], -0.5)

        @block.scalar
        def _(act):
            act.wait_ge(ctx_loaded, 16 * KC)
            for k in range(KC):
                nc.scalar.copy(c.ctxT[0][:, k, :], raw[:, k, :]).then_inc(high, 1)

        @block.vector
        def _(dve):
            for k in range(KC):
                dve.wait_ge(high, k + 1)
                nc.vector.tensor_tensor(c.ctxT[1][:, k, :], raw[:, k, :], fp(c.ctxT[0][:, k, :]), ALU.subtract).then_inc(low, 1)


def layernorm_steps(nc, c, t, ctx, width):
    n = Chip()
    n.stats = ctx.enter_context(nc.sbuf_tensor(t + "stats", [P, width, 6], F32))
    n.mv = ctx.enter_context(nc.sbuf_tensor(t + "mv", [P, width, 2], F32))
    n.ve = ctx.enter_context(nc.sbuf_tensor(t + "ve", [P, width], F32))
    n.rstd = ctx.enter_context(nc.sbuf_tensor(t + "rstd", [P, width], F32))
    n.xn = ctx.enter_context(nc.sbuf_tensor(t + "xn", [P, width, D], F32))
    n.stats_done, n.mv_done, n.var_ready = c.sem(t + "stats_done"), c.sem(t + "mv_done"), c.sem(t + "var_ready")
    n.rstd_ready = c.sem(t + "rstd_ready")
    n.xn_ready = c.sem(t + "xn_ready")
    n.xnT_full = c.sem(t + "xnT_full")
    n.xnT_high, n.xnT_low = c.sem(t + "xnT_high"), c.sem(t + "xnT_low")
    return n


def norm_on_vector(nc, dve, n, c, it, width, x_of):
    for u in range(width):
        nc.vector.bn_stats(n.stats[:, u, :], x_of(u)).then_inc(n.stats_done, 1)
    dve.wait_ge(n.stats_done, it * width + width)
    nc.vector.tensor_copy(c.scratch[:, :], c.ones[:, 0:1])
    for u in range(width):
        nc.vector.bn_aggr(n.mv[:, u, :], n.stats[:, u, :]).then_inc(n.mv_done, 1)
    dve.wait_ge(n.mv_done, it * width + width)
    nc.vector.tensor_scalar(n.ve[:, :], n.mv[:, :, 1], EPS, None, ALU.add).then_inc(n.var_ready, 1)
    dve.wait_ge(n.rstd_ready, it + 1)
    for u in range(width):
        nc.vector.tensor_scalar(n.xn[:, u, :], x_of(u), n.mv[:, u, 0:1], n.rstd[:, u:u + 1],
                                ALU.subtract, ALU.mult).then_inc(n.xn_ready, 1)


def rstd_on_pool(nc, pool, n, c, it, width):
    pool.wait_ge(n.var_ready, it + 1)
    nc.gpsimd.tensor_tensor(n.rstd[:, :], n.ve[:, :], c.minus_half[:, 0:width], ALU.pow).then_inc(n.rstd_ready, 1)


def norm_transpose(nc, c, d, t, xnT, bias=None):
    W = HB
    with ExitStack() as ctx:
        n = layernorm_steps(nc, c, t, ctx, W)
        if bias:
            bias_sb = ctx.enter_context(nc.sbuf_tensor(t + "bias", [P, D], F32))
            bias_loaded = c.sem(t + "bias_loaded")
        block = ctx.enter_context(nc.Block())

        @block.sync
        def _(sp):
            if bias:
                sp.dma_start(bias_sb[:, :], d[bias].partition_broadcast(P).rearrange("p a n -> p (a n)")).then_inc(bias_loaded, 16)

        @block.vector
        def _(dve):
            with dve.Fori(0, B // W) as it:
                norm_on_vector(nc, dve, n, c, it, W, lambda u: c.x[:, bass.ds(it * W + u, 1), :].rearrange("p a n -> p (a n)"))
                for u in range(W):
                    dve.wait_ge(n.xnT_high, it * W + u + 1)
                    cols = bass.ds((it * W + u) * P, P)
                    nc.vector.tensor_tensor(xnT[1][:, :, cols], c.bank[u][:, :].rearrange("p (k t) -> p k t", k=KC),
                                            fp(xnT[0][:, :, cols]), ALU.subtract).then_inc(n.xnT_low, 1)

        @block.gpsimd
        def _(pool):
            if bias:
                pool.wait_ge(bias_loaded, 16)
            with pool.Fori(0, B // W) as it:
                rstd_on_pool(nc, pool, n, c, it, W)
                if bias:
                    for u in range(W):
                        pool.wait_ge(n.xn_ready, it * W + u + 1)
                        xb = c.x[:, bass.ds(it * W + u, 1), :].rearrange("p a n -> p (a n)")
                        nc.gpsimd.tensor_tensor(xb, xb, bias_sb[:, :], ALU.add)

        @block.tensor
        def _(pe):
            with pe.Fori(0, B // W) as it:
                for u in range(W):
                    pe.wait_ge(n.xn_ready, it * W + u + 1)
                    for k in range(KC):
                        last = nc.tensor.transpose(c.bank[u][:, k * P:(k + 1) * P], n.xn[:, u, k * P:(k + 1) * P], c.ident)
                    last.then_inc(n.xnT_full, 1)

        @block.scalar
        def _(act):
            with act.Fori(0, B // W) as it:
                for u in range(W):
                    act.wait_ge(n.xnT_full, it * W + u + 1)
                    nc.scalar.copy(xnT[0][:, :, bass.ds((it * W + u) * P, P)],
                                   c.bank[u][:, :].rearrange("p (k t) -> p k t", k=KC)).then_inc(n.xnT_high, 1)


def store_output(nc, c, d):
    with ExitStack() as ctx:
        stored = c.sem("out_stored")
        block = ctx.enter_context(nc.Block())

        @block.sync
        def _(sp):
            sp.dma_start(d["out"].rearrange("b p n -> p b n"), c.x[:, :, :]).then_inc(stored, 16)
            sp.wait_ge(stored, 16)


IDENT, MASK16, MASKM, MASKG, BLOCK4, IOTA, TRI, RECK = 0, 128, 136, 140, 144, 272, 280, 344
CONSTS = 352


def constants():
    p = np.arange(P)
    a = np.zeros((P, CONSTS), np.float32)
    a[:, IDENT:IDENT + P] = np.eye(P)
    a[:, MASK16:MASK16 + 8] = p[:, None] // 16 == np.arange(8)
    a[:, MASKM:MASKM + 4] = p[:, None] % 4 == np.arange(4)
    a[:, MASKG:MASKG + 4] = p[:, None] // 32 == np.arange(4)
    a[:, BLOCK4:BLOCK4 + P] = p[:, None] // 4 == p // 4
    a[:, IOTA:IOTA + 8] = np.arange(8)
    a[:, TRI:TRI + 64] = np.tril(np.ones((8, 8))).reshape(-1)
    a[:, RECK:RECK + 8] = 1.0 / np.arange(1, 9)
    return a



def small_head_attention(nc, c, d, layer, xnT):
    own_kv = layer == 1
    SG = 4 if own_kv else 2
    HEADS = 4 * SG
    DV = P // HEADS
    VW = 3 * DV + 1
    MASKS = 4 if own_kv else 8
    SCALE = (8 if own_kv else 16) ** -0.5
    N = B * SG
    TICKS = N + 7
    t = f"a{layer}_"
    with ExitStack() as ctx:
        def sb(name, shape, dt=F32):
            return ctx.enter_context(nc.sbuf_tensor(t + name, shape, dt))

        def pair(name, shape, dt=F32R):
            return sb(name + "_hi", shape, dt), sb(name + "_lo", shape, dt)

        def sem(name):
            return c.sem(t + name)

        kTm = pair("kTm", [P, MASKS, TOK])
        qT = pair("qT", [P, 4 if own_kv else 1, TOK])
        wq, wk, wv, wo = pair("wq", [P, KC, P]), pair("wk", [P, KC, P]), pair("wv", [P, KC, P]), pair("wo", [P, D])
        temp = pair("temp", [P, 2, HALF])
        if own_kv:
            wo_raw = sb("wo_raw", [P, D])
            w_nat = sb("w_nat", [P, 3, D])
            inter_raw, inter = sb("inter_raw", [P, KC, 4]), sb("inter", [P, KC, 4])
            amp = sb("amp", [P, 1])
            bias_raw, bias = sb("bias_raw", [P, KC, 3]), sb("bias", [P, 3])
            fold = sb("fold", [P, P])
        else:
            wkv_raw = sb("wkv_raw", [P, 2 * KC, P])
            wq_raw, wo_raw = wkv_raw[:, 0:KC, :], wkv_raw[:, KC:2 * KC, :].rearrange("p k n -> p (k n)")
        v_aug = sb("v_aug", [P, B, HEADS, VW], BF16)
        v_rest = sb("v_rest", [P, B, P])
        minus_max = sb("minus_max", [P, 3, 4])
        prob = sb("prob", [P, 3, HALF])
        pT = pair("pT", [P, 2, HALF], F16)
        o_raw, o_inv, o_sb = sb("o_raw", [P, 2, P]), sb("o_inv", [P, 2, HEADS]), sb("o_sb", [P, 2, P])
        oT = pair("oT", [P, 2, P])

        once_loaded = sem("once_loaded")
        wq_loaded = sem("wq_loaded")
        wo_loaded = sem("wo_loaded")
        split_high = sem("split_high")
        kv_split = sem("kv_split")
        wq_split, wo_split = sem("wq_split"), sem("wo_split")
        ones_set = sem("ones_set")
        inter_ready = sem("inter_ready")
        fold_step, folded = sem("fold_step"), sem("folded")
        bias_scaled = sem("bias_scaled")
        m_full = sem("m_full")
        m_high = sem("m_high")
        m_free = sem("m_free")
        mask_high, mask_low = sem("mask_high"), sem("mask_low")
        v2_ready, v3_ready = sem("v2_ready"), sem("v3_ready")
        s_full = sem("s_full")
        max_ready = sem("max_ready")
        p_ready = sem("p_ready")
        pT_full = sem("pT_full")
        pT_high = sem("pT_high")
        pT_low = sem("pT_low")
        pv_done = sem("pv_done")
        o_step = sem("o_step")
        o_free = sem("o_free")

        S, PT, OB, M = c.bank[0:2], c.bank[2:4], c.bank[4:6], c.bank[6:8]

        def ends(n):
            return n // SG if 0 <= n < N and n % SG == SG - 1 else None

        ahead = [] if own_kv else ["k0", "k1", "v0", "v1"]
        order = (["fq", "fk", "fv", "fb"] if own_kv else []) + ["q0", "q1"] + (["k0", "k1", "v0", "v1"] if own_kv else [])
        for n in range(TICKS):
            order += [f"t{ends(n - 5)}"] if ends(n - 5) is not None else []
            order += [f"o{ends(n - 6)}"] if ends(n - 6) is not None else []
        by_act = [x for x in order if x[0] != "o" and x != "fb"]
        assert len(ahead) % 2 == 0 and len(order) % 2 == 0

        def tile(g, name):
            return ahead.index(name) if name in ahead else g * len(order) + (len(ahead) + order.index(name))

        def high(g, name):
            return ahead.index(name) if name in ahead else g * len(by_act) + (len(ahead) + by_act.index(name))

        def bank_of(name):
            return M[(ahead.index(name) if name in ahead else order.index(name)) % 2]

        def temp_of(name):
            return (ahead.index(name) if name in ahead else order.index(name)) % 2

        block = ctx.enter_context(nc.Block())

        @block.sync
        def _(sp):
            def load_wq(g):
                if own_kv:
                    sp.dma_start(w_nat[:, :, :], d["L1_wqkv"][bass.ds(g, 1)].rearrange("a p w n -> (a p) w n")).then_inc(wq_loaded, 16)
                else:
                    sp.dma_start(wq_raw, d["L0_wq"][bass.ds(g, 1)].rearrange("a p k n -> (a p) k n")).then_inc(wq_loaded, 16)

            def load_wo(g):
                sp.dma_start(wo_raw[:, :], d[f"L{layer}_wo"][bass.ds(g, 1)].rearrange("a p n -> (a p) n")).then_inc(wo_loaded, 16)

            if own_kv:
                sp.dma_start(inter_raw[:, :, :], d["L1_inter"]).then_inc(once_loaded, 16)
                sp.dma_start(amp[:, :], d["L1_amp"]).then_inc(once_loaded, 16)
                sp.dma_start(bias_raw[:, :, :], d["L1_bias"]).then_inc(once_loaded, 16)
            else:
                sp.dma_start(wkv_raw[:, :, :], d["L0_wkv"]).then_inc(once_loaded, 16)
                sp.wait_ge(kv_split, 1)
            load_wq(0)
            if not own_kv:
                sp.wait_ge(kv_split, 2)
            load_wo(0)
            with sp.Fori(1, KC) as g:
                if own_kv:
                    sp.wait_ge(m_free, tile(g - 1, "fb") + 3)
                else:
                    sp.wait_ge(wq_split, g)
                load_wq(g)
                sp.wait_ge(wo_split, g)
                load_wo(g)

        @block.gpsimd
        def _(pool):
            def split(raw, parts, highs, done):
                one = c.ones[:, 0:1].broadcast_to([P, raw.shape[1]]) if raw.ndim == 2 else \
                    c.ones[:, 0:1].unsqueeze(2).broadcast_to([P, raw.shape[1], raw.shape[2]])
                nc.gpsimd.tensor_tensor(parts[0], raw, one, ALU.mult).then_inc(split_high, 1)
                pool.wait_ge(split_high, highs + 1)
                nc.gpsimd.tensor_tensor(parts[1], raw, fp(parts[0]), ALU.subtract).then_inc(done, 1)

            def value_parts(g, half):
                pool.wait_ge(m_free, tile(g, f"v{half}") + 3)
                for u in range(HB):
                    b = half * HB + u
                    rest = v_rest[:, b, :].rearrange("p (h e) -> p h e", h=HEADS)
                    one = c.ones[:, 0:1].unsqueeze(2).broadcast_to([P, HEADS, DV])
                    nc.gpsimd.tensor_tensor(v_aug[:, b, :, DV:2 * DV], rest, one, ALU.mult).then_inc(v2_ready, 1)
                for u in range(HB):
                    b = half * HB + u
                    rest = v_rest[:, b, :].rearrange("p (h e) -> p h e", h=HEADS)
                    pool.wait_ge(v2_ready, (g if own_kv else 0) * B + (b + 1))
                    nc.gpsimd.tensor_tensor(v_aug[:, b, :, 2 * DV:3 * DV], rest, v_aug[:, b, :, DV:2 * DV],
                                            ALU.subtract).then_inc(v3_ready, 1)

            def whole(w):
                return [x[:, :, :] for x in w]

            nc.gpsimd.memset(v_aug[:, :, :, VW - 1:VW], 1.0).then_inc(ones_set, 1)
            if not own_kv:
                pool.wait_ge(once_loaded, 16)
                split(wkv_raw[:, 0:KC, :], whole(wk), 0, kv_split)
                split(wkv_raw[:, KC:2 * KC, :], whole(wv), 1, kv_split)
                pool.wait_ge(wq_loaded, 16)
                split(wq_raw, whole(wq), 2, wq_split)
            pool.wait_ge(wo_loaded, 16)
            split(wo_raw[:, :], [x[:, :] for x in wo], 0 if own_kv else 3, wo_split)
            value_parts(0, 0)
            value_parts(0, 1)
            with pool.Fori(1, KC) as g:
                if not own_kv:
                    pool.wait_ge(wq_loaded, g * 16 + 16)
                    pool.wait_ge(m_free, tile(g - 1, "q1") + 3)
                    split(wq_raw, whole(wq), g * 2 + 2, wq_split)
                pool.wait_ge(wo_loaded, g * 16 + 16)
                pool.wait_ge(m_free, tile(g - 1, f"o{B - 1}") + 3)
                split(wo_raw[:, :], [x[:, :] for x in wo], g if own_kv else g * 2 + 3, wo_split)
                if own_kv:
                    value_parts(g, 0)
                    value_parts(g, 1)

        @block.tensor
        def _(pe):
            def take(g, name):
                pe.wait_ge(m_free, tile(g, name) + 1)
                return bank_of(name)

            def transposed(g, name, w, rhs, half):
                bank = take(g, name)
                for k in range(KC):
                    ins = split_passes(nc, bank[:, :], [x[:, k, :] for x in w],
                                       [x[:, k, half * HALF:(half + 1) * HALF] for x in rhs], k == 0, k == KC - 1)
                ins.then_inc(m_full, 1)

            def keys(g):
                for half in range(2):
                    transposed(g, f"k{half}", wk, c.ctxT, half)

            def values(g):
                for half in range(2):
                    bank = take(g, f"v{half}")
                    for u in range(HB):
                        cols = slice((half * HB + u) * P, (half * HB + u + 1) * P)
                        for k in range(KC):
                            ins = split_passes(nc, bank[:, u * P:(u + 1) * P], [x[:, k, cols] for x in c.ctxT],
                                               [x[:, k, :] for x in wv], k == 0, k == KC - 1)
                    ins.then_inc(m_full, 1)

            if not own_kv:
                pe.wait_ge(kv_split, 2)
                keys(0)
                values(0)
            with pe.Fori(0, KC) as g:
                if own_kv:
                    pe.wait_ge(folded, g + 1)
                    pe.wait_ge(wq_loaded, g * 16 + 16)
                    for n, name in enumerate(("fq", "fk", "fv")):
                        bank = take(g, name)
                        for k in range(KC):
                            ins = nc.tensor.matmul(bank[:, k * P:(k + 1) * P], w_nat[:, n, k * P:(k + 1) * P], fold[:, :],
                                                   start=True, stop=True)
                        ins.then_inc(m_full, 1)
                    bank = take(g, "fb")
                    pe.wait_ge(once_loaded, 48)
                    nc.tensor.matmul(bank[:, 0:3], fold[:, :], bias_raw[:, bass.ds(g, 1), :].rearrange("p a n -> p (a n)"),
                                     start=True, stop=True).then_inc(m_full, 1)
                    pe.wait_ge(m_free, tile(g, "fq") + 3)
                else:
                    pe.wait_ge(wq_split, g + 1)
                transposed(g, "q0", wq, xnT, 0)
                transposed(g, "q1", wq, xnT, 1)
                if own_kv:
                    pe.wait_ge(m_free, tile(g, "fk") + 3)
                    keys(g)
                    pe.wait_ge(m_free, tile(g, "fv") + 3)
                    values(g)
                for n in range(TICKS):
                    if 0 <= n - 2 < N:
                        i = n - 2
                        pe.wait_ge(p_ready, g * N + (i + 3))
                        pe.wait_ge(pT_low, g * N + (i + 1))
                        for h in range(4):
                            ins = nc.tensor.transpose(PT[i % 2][:, h * P:(h + 1) * P], prob[:, i % 3, h * P:(h + 1) * P], c.ident)
                        ins.then_inc(pT_full, 1)
                    if n < N:
                        b, s = n // SG, n % SG
                        if n == 0:
                            tiles = g * 4 + 4 if own_kv else 2
                            pe.wait_ge(mask_high, tiles)
                            pe.wait_ge(mask_low, tiles)
                            pe.wait_ge(m_free, tile(g, "q1") + 3)
                        pe.wait_ge(p_ready, g * N + (n + 1))
                        tok = slice(b * P, (b + 1) * P)
                        keys_of = slice(0, 4) if own_kv else slice(4 * s, 4 * s + 4)
                        split_passes(nc, S[n % 2][:, :].rearrange("p (a t) -> p a t", a=4),
                                     [x[:, s if own_kv else 0, tok] for x in qT], [x[:, keys_of, tok] for x in kTm],
                                     True, True).then_inc(s_full, 1)
                    if 0 <= n - 3 < N:
                        i = n - 3
                        b, s = i // SG, i % SG
                        pe.wait_ge(pT_low, g * N + (i + 3))
                        if s == 0:
                            pe.wait_ge(o_free, g * B + (b + 1))
                        if i == 0:
                            pe.wait_ge(v3_ready, g * B + B if own_kv else B)
                            pe.wait_ge(ones_set, 1)
                        for h in range(4):
                            head = 4 * s + h
                            out = OB[b % 2][:, head * VW:(head + 1) * VW]
                            nc.tensor.matmul(out, pT[0][:, i % 2, h * P:(h + 1) * P], v_aug[:, b, head, :], start=True, stop=False)
                            ins = nc.tensor.matmul(out, pT[1][:, i % 2, h * P:(h + 1) * P], v_aug[:, b, head, :],
                                                   start=False, stop=True)
                        ins.then_inc(pv_done, 1)
                    if ends(n - 5) is not None:
                        b = ends(n - 5)
                        bank = take(g, f"t{b}")
                        pe.wait_ge(o_free, g * B + (b + 3))
                        nc.tensor.transpose(bank[:, 0:P], o_sb[:, b % 2, :], c.ident).then_inc(m_full, 1)
                    if ends(n - 6) is not None:
                        b = ends(n - 6)
                        bank = take(g, f"o{b}")
                        if b == 0:
                            pe.wait_ge(wo_split, g + 1)
                        pe.wait_ge(m_free, tile(g, f"t{b}") + 3)
                        split_passes(nc, bank[:, :], [x[:, b % 2, :] for x in oT], [x[:, :] for x in wo],
                                     True, True).then_inc(m_full, 1)

        @block.scalar
        def _(act):
            def masked(g, name, out, masks, col):
                r, half = temp_of(name), int(name[1])
                act.wait_ge(m_full, tile(g, name) + 1)
                if own_kv:
                    act.wait_ge(m_free, tile(g, "fb") + 3)
                    act.wait_ge(bias_scaled, g + 1)
                    nc.scalar.activation(temp[0][:, r, :], bank_of(name)[:, :], ACT.Identity,
                                         bias=bias[:, col:col + 1]).then_inc(m_high, 1)
                else:
                    nc.scalar.copy(temp[0][:, r, :], bank_of(name)[:, :]).then_inc(m_high, 1)
                act.wait_ge(m_high, high(g, name) + 1)
                for m in range(out[0].shape[1]):
                    ins = nc.scalar.activation(out[0][:, m, half * HALF:(half + 1) * HALF], fp(temp[0][:, r, :]), ACT.Copy,
                                               scale=c.consts[:, masks + m:masks + m + 1])
                ins.then_inc(mask_high, 1)

            def values(g, half):
                act.wait_ge(m_full, tile(g, f"v{half}") + 1)
                for u in range(HB):
                    src = bank_of(f"v{half}")[:, u * P:(u + 1) * P]
                    out = v_aug[:, half * HB + u, :, 0:DV]
                    if own_kv:
                        src = src.rearrange("p (h e m) -> p h m e", h=4, m=4)
                        out = out.rearrange("p (h m) e -> p h m e", h=4)
                    else:
                        src = src.rearrange("p (h e) -> p h e", h=HEADS)
                    ins = nc.scalar.copy(out, src)
                ins.then_inc(m_high, 1)

            if not own_kv:
                masked(0, "k0", kTm, MASK16, None)
                masked(0, "k1", kTm, MASK16, None)
                values(0, 0)
                values(0, 1)
            act.sem_inc(p_ready, 2)
            with act.Fori(0, KC) as g:
                if own_kv:
                    for name, w in (("fq", wq), ("fk", wk), ("fv", wv)):
                        act.wait_ge(m_full, tile(g, name) + 1)
                        nc.scalar.activation(w[0][:, :, :], bank_of(name)[:, :].rearrange("p (k n) -> p k n", k=KC), ACT.Copy,
                                             scale=SCALE if name == "fq" else 1.0).then_inc(m_high, 1)
                    masked(g, "q0", qT, MASKG, 0)
                    masked(g, "q1", qT, MASKG, 0)
                    masked(g, "k0", kTm, MASKM, 1)
                    masked(g, "k1", kTm, MASKM, 1)
                    values(g, 0)
                    values(g, 1)
                else:
                    for half in range(2):
                        act.wait_ge(m_full, tile(g, f"q{half}") + 1)
                        nc.scalar.activation(qT[0][:, 0, half * HALF:(half + 1) * HALF], bank_of(f"q{half}")[:, :], ACT.Copy,
                                             scale=SCALE).then_inc(m_high, 1)
                for n in range(TICKS):
                    if 0 <= n - 2 < N:
                        act.wait_ge(pT_full, g * N + (n - 1))
                        nc.scalar.copy(pT[0][:, n % 2, :], PT[n % 2][:, :]).then_inc(pT_high, 1)
                    if n < N:
                        act.wait_ge(max_ready, g * N + (n + 1))
                        for h in range(4):
                            ins = nc.scalar.activation(prob[:, n % 3, h * P:(h + 1) * P], S[n % 2][:, h * P:(h + 1) * P], ACT.Exp,
                                                       bias=minus_max[:, n % 3, h:h + 1])
                        ins.then_inc(p_ready, 1)
                    if ends(n - 5) is not None:
                        b = ends(n - 5)
                        act.wait_ge(m_full, tile(g, f"t{b}") + 1)
                        src = bank_of(f"t{b}")[:, 0:P]
                        if own_kv:
                            nc.scalar.activation(oT[0][:, b % 2, :], src, ACT.Identity, bias=bias[:, 2:3]).then_inc(m_high, 1)
                        else:
                            nc.scalar.copy(oT[0][:, b % 2, :], src).then_inc(m_high, 1)

        @block.vector
        def _(dve):
            def masked(g, name, out, masks, col):
                r, half = temp_of(name), int(name[1])
                dve.wait_ge(m_high, high(g, name) + 1)
                if own_kv:
                    nc.vector.scalar_tensor_tensor(temp[1][:, r, :], bank_of(name)[:, :], bias[:, col:col + 1],
                                                   fp(temp[0][:, r, :]), ALU.add, ALU.subtract).then_inc(m_free, 1)
                else:
                    nc.vector.tensor_tensor(temp[1][:, r, :], bank_of(name)[:, :], fp(temp[0][:, r, :]), ALU.subtract).then_inc(m_free, 1)
                dve.wait_ge(m_free, tile(g, name) + 3)
                for m in range(out[1].shape[1]):
                    ins = nc.vector.tensor_scalar(out[1][:, m, half * HALF:(half + 1) * HALF], fp(temp[1][:, r, :]),
                                                  c.consts[:, masks + m:masks + m + 1], None, ALU.mult)
                ins.then_inc(mask_low, 1)

            def values(g, half):
                dve.wait_ge(m_high, high(g, f"v{half}") + 1)
                for u in range(HB):
                    b = half * HB + u
                    src = bank_of(f"v{half}")[:, u * P:(u + 1) * P]
                    first, out = v_aug[:, b, :, 0:DV], v_rest[:, b, :]
                    if own_kv:
                        src = src.rearrange("p (h e m) -> p h m e", h=4, m=4)
                        first = first.rearrange("p (h m) e -> p h m e", h=4)
                        out = out.rearrange("p (h m e) -> p h m e", h=4, m=4)
                    else:
                        src = src.rearrange("p (h e) -> p h e", h=HEADS)
                        out = out.rearrange("p (h e) -> p h e", h=HEADS)
                    ins = nc.vector.tensor_tensor(out, src, first, ALU.subtract)
                ins.then_inc(m_free, 1)

            dve.sem_inc(m_free, 2)
            dve.sem_inc(pT_low, 2)
            dve.sem_inc(o_free, 2)
            if own_kv:
                dve.wait_ge(once_loaded, 48)
                nc.vector.tensor_scalar(inter[:, :, :], inter_raw[:, :, :], amp[:, 0:1], 0.1, ALU.mult, ALU.mult).then_inc(inter_ready, 1)
                dve.wait_ge(inter_ready, 1)
            else:
                masked(0, "k0", kTm, MASK16, None)
                masked(0, "k1", kTm, MASK16, None)
                values(0, 0)
                values(0, 1)
            with dve.Fori(0, KC) as g:
                if own_kv:
                    nc.vector.tensor_tensor(fold[:, :].rearrange("p (e j) -> p e j", j=4),
                                            c.consts[:, BLOCK4:BLOCK4 + P].rearrange("p (e j) -> p e j", j=4),
                                            inter[:, bass.ds(g, 1), :].broadcast_to([P, P // 4, 4]), ALU.mult).then_inc(fold_step, 1)
                    dve.wait_ge(fold_step, g + 1)
                    nc.vector.tensor_tensor(fold[:, :], fold[:, :], c.ident, ALU.add).then_inc(folded, 1)
                    for name, w in (("fq", wq), ("fk", wk), ("fv", wv)):
                        dve.wait_ge(m_high, high(g, name) + 1)
                        nc.vector.scalar_tensor_tensor(w[1][:, :, :], bank_of(name)[:, :].rearrange("p (k n) -> p k n", k=KC),
                                                       SCALE if name == "fq" else 1.0, fp(w[0][:, :, :]),
                                                       ALU.mult, ALU.subtract).then_inc(m_free, 1)
                    dve.wait_ge(m_full, tile(g, "fb") + 1)
                    nc.vector.tensor_scalar(bias[:, 0:1], bank_of("fb")[:, 0:1], SCALE, None, ALU.mult).then_inc(bias_scaled, 1)
                    nc.vector.tensor_copy(bias[:, 1:3], bank_of("fb")[:, 1:3]).then_inc(m_free, 1)
                    dve.wait_ge(bias_scaled, g + 1)
                    dve.wait_ge(m_free, tile(g, "fb") + 3)
                    masked(g, "q0", qT, MASKG, 0)
                    masked(g, "q1", qT, MASKG, 0)
                    masked(g, "k0", kTm, MASKM, 1)
                    masked(g, "k1", kTm, MASKM, 1)
                    values(g, 0)
                    values(g, 1)
                else:
                    for half in range(2):
                        dve.wait_ge(m_high, high(g, f"q{half}") + 1)
                        cols = slice(half * HALF, (half + 1) * HALF)
                        nc.vector.scalar_tensor_tensor(qT[1][:, 0, cols], bank_of(f"q{half}")[:, :], SCALE, fp(qT[0][:, 0, cols]),
                                                       ALU.mult, ALU.subtract).then_inc(m_free, 1)
                for n in range(TICKS):
                    if n < N:
                        dve.wait_ge(s_full, g * N + (n + 1))
                        scores = S[n % 2][:, :].rearrange("p (a t) -> p a t", a=4)
                        nc.vector.tensor_reduce(minus_max[:, n % 3, :], scores, AX.X, ALU.max, negate=True).then_inc(max_ready, 1)
                    if 0 <= n - 2 < N:
                        i = n - 2
                        dve.wait_ge(pT_high, g * N + (i + 1))
                        nc.vector.tensor_tensor(pT[1][:, i % 2, :], PT[i % 2][:, :], pT[0][:, i % 2, :], ALU.subtract).then_inc(pT_low, 1)
                    if ends(n - 4) is not None:
                        b = ends(n - 4)
                        r = b % 2
                        dve.wait_ge(pv_done, g * N + (n - 3))
                        sums = OB[r][:, 0:HEADS * VW].rearrange("p (h w) -> p h w", w=VW)
                        nc.vector.tensor_reduce(o_raw[:, r, :].rearrange("p (h e) -> p h e", h=HEADS),
                                                sums[:, :, 0:3 * DV].rearrange("p h (s e) -> p h e s", s=3), AX.X, ALU.add).then_inc(o_step, 1)
                        nc.vector.reciprocal(o_inv[:, r, :].unsqueeze(2), sums[:, :, 3 * DV:VW]).then_inc(o_step, 1)
                        dve.wait_ge(o_step, g * 2 * B + (2 * b + 2))
                        if own_kv:
                            out = o_sb[:, r, :].rearrange("p (h e m) -> p h m e", h=4, m=4)
                            raw = o_raw[:, r, :].rearrange("p (h m e) -> p h m e", h=4, m=4)
                            inv = o_inv[:, r, :].rearrange("p (h m) -> p h m", h=4).unsqueeze(3).broadcast_to([P, 4, 4, DV])
                        else:
                            out = o_sb[:, r, :].rearrange("p (h e) -> p h e", h=HEADS)
                            raw = o_raw[:, r, :].rearrange("p (h e) -> p h e", h=HEADS)
                            inv = o_inv[:, r, :].unsqueeze(2).broadcast_to([P, HEADS, DV])
                        nc.vector.tensor_tensor(out, raw, inv, ALU.mult).then_inc(o_free, 1)
                    if ends(n - 5) is not None:
                        b = ends(n - 5)
                        dve.wait_ge(m_high, high(g, f"t{b}") + 1)
                        src, hi, lo = bank_of(f"t{b}")[:, 0:P], fp(oT[0][:, b % 2, :]), oT[1][:, b % 2, :]
                        if own_kv:
                            nc.vector.scalar_tensor_tensor(lo, src, bias[:, 2:3], hi, ALU.add, ALU.subtract).then_inc(m_free, 1)
                        else:
                            nc.vector.tensor_tensor(lo, src, hi, ALU.subtract).then_inc(m_free, 1)
                    if ends(n - 6) is not None:
                        b = ends(n - 6)
                        dve.wait_ge(m_full, tile(g, f"o{b}") + 1)
                        nc.vector.tensor_tensor(c.x[:, b, :], bank_of(f"o{b}")[:, :], c.x[:, b, :], ALU.add).then_inc(m_free, 1)

class Chain:

    def __init__(self, eng, sem, base):
        self.eng, self.sem, self.base, self.n = eng, sem, base, 0

    def __call__(self, ins):
        ins.then_inc(self.sem, 1)
        self.n += 1
        self.eng.wait_ge(self.sem, self.base + self.n)


def moe_ffn(nc, c, d, layer):
    W = HB
    base = layer != 3
    t = f"f{layer}_"
    NA = LR + EXPERTS
    STEPS = {0: 12, 1: 9, 3: 6}[layer]
    with ExitStack() as ctx:
        def sb(name, shape, dt=F32):
            return ctx.enter_context(nc.sbuf_tensor(t + name, shape, dt))

        def pair(name, shape, dt=F32R):
            return sb(name + "_hi", shape, dt), sb(name + "_lo", shape, dt)

        def sem(name):
            return c.sem(t + name)

        n = layernorm_steps(nc, c, t, ctx, W)
        xnT = pair("xnT", [P, W, KC, P])
        wa_raw, wb_raw = sb("wa_raw", [P, KC, NA]), sb("wb_raw", [P, D])
        wa, wb = pair("wa", [P, KC, NA]), pair("wb", [P, D])
        raws, parts = [wa_raw[:, :, :], wb_raw[:, :]], [[x[:, :, :] for x in wa], [x[:, :] for x in wb]]
        if base:
            w0_raw, w0 = sb("w0_raw", [P, KC, D]), pair("w0", [P, KC, D])
            raws.append(w0_raw[:, :, :])
            parts.append([x[:, :, :] for x in w0])
            bias = sb("bias", [P, D])
        router_bias = sb("router_bias", [P, EXPERTS])
        logits, top, comb = sb("logits", [P, W, EXPERTS]), sb("top", [P, W, EXPERTS]), sb("comb", [P, W, EXPERTS])
        index, index_f = sb("index", [P, W, EXPERTS], U32), sb("index_f", [P, W, EXPERTS])
        chosen = sb("chosen", [P, W, EXPERTS])
        cum_terms, cum = sb("cum_terms", [P, W, EXPERTS, EXPERTS]), sb("cum", [P, W, EXPERTS])
        small = sb("small", [P, 5, W])
        hs = sb("hs", [P, W, LR])
        hT = pair("hT", [P, W, P])

        w_loaded = [sem(f"w{i}_loaded") for i in range(len(raws))]
        bias_loaded = sem("bias_loaded")
        w_high, w_low = sem("w_high"), sem("w_low")
        bias_added = sem("bias_added")
        h_full = sem("h_full")
        logits_done = sem("logits_done")
        step = sem("step")
        gap_ready, exp_ready = sem("gap_ready"), sem("exp_ready")
        hs_ready = sem("hs_ready")
        hT_full, hT_high, hT_low = sem("hT_full"), sem("hT_high"), sem("hT_low")
        out_full = sem("out_full")
        added = sem("added")

        block = ctx.enter_context(nc.Block())

        @block.sync
        def _(sp):
            sp.dma_start(wa_raw[:, :, :], d[f"L{layer}_wa"]).then_inc(w_loaded[0], 16)
            sp.dma_start(wb_raw[:, :], d[f"L{layer}_wb"]).then_inc(w_loaded[1], 16)
            if base:
                sp.dma_start(w0_raw[:, :, :], d[f"L{layer}_w0"]).then_inc(w_loaded[2], 16)
                sp.dma_start(bias[:, :], d[f"L{layer}_b0"].partition_broadcast(P).rearrange("p a n -> p (a n)")).then_inc(bias_loaded, 16)
            if layer == 1:
                sp.dma_start(router_bias[:, :], d["L1_br"].partition_broadcast(P).rearrange("p a n -> p (a n)")).then_inc(bias_loaded, 16)

        @block.gpsimd
        def _(pool):
            if base:
                pool.wait_ge(bias_loaded, 32 if layer == 1 else 16)
            with pool.Fori(0, B // W) as it:
                rstd_on_pool(nc, pool, n, c, it, W)
                if base:
                    for u in range(W):
                        pool.wait_ge(n.xn_ready, it * W + (u + 1))
                        xb = c.x[:, bass.ds(it * W + u, 1), :].rearrange("p a n -> p (a n)")
                        nc.gpsimd.tensor_tensor(xb, xb, bias[:, :], ALU.add).then_inc(bias_added, 1)

        @block.tensor
        def _(pe):
            with pe.Fori(0, B // W) as it:
                for u in range(W):
                    pe.wait_ge(n.xn_ready, it * W + (u + 1))
                    for k in range(KC):
                        ins = nc.tensor.transpose(c.bank[u][:, k * P:(k + 1) * P], n.xn[:, u, k * P:(k + 1) * P], c.ident)
                    ins.then_inc(n.xnT_full, 1)
                pe.wait_ge(w_low, len(raws))
                for u in range(W):
                    pe.wait_ge(n.xnT_low, it * W + (u + 1))
                    for k in range(KC):
                        ins = split_passes(nc, c.bank[u][:, 0:NA], [x[:, u, k, :] for x in xnT], [x[:, k, :] for x in wa],
                                           k == 0, k == KC - 1)
                    ins.then_inc(h_full, 1)
                if base:
                    for u in range(W):
                        for k in range(KC):
                            split_passes(nc, c.bank[4 + u][:, :], [x[:, u, k, :] for x in xnT], [x[:, k, :] for x in w0],
                                         k == 0, False)
                for u in range(W):
                    pe.wait_ge(hs_ready, it * W + (u + 1))
                    nc.tensor.transpose(c.bank[u][:, 0:P], hs[:, u, :], c.ident).then_inc(hT_full, 1)
                for u in range(W):
                    pe.wait_ge(hT_low, it * W + (u + 1))
                    split_passes(nc, c.bank[4 + u][:, :], [x[:, u, :] for x in hT], [x[:, :] for x in wb],
                                 not base, True).then_inc(out_full, 1)

        @block.scalar
        def _(act):
            for i, (raw, part) in enumerate(zip(raws, parts)):
                act.wait_ge(w_loaded[i], 16)
                nc.scalar.copy(part[0], raw).then_inc(w_high, 1)
            with act.Fori(0, B // W) as it:
                for u in range(W):
                    act.wait_ge(n.xnT_full, it * W + (u + 1))
                    nc.scalar.copy(xnT[0][:, u, :, :], c.bank[u][:, :].rearrange("p (k t) -> p k t", k=KC)).then_inc(n.xnT_high, 1)
                if layer == 0:
                    act.wait_ge(gap_ready, it + 1)
                    nc.scalar.activation(small[:, 1, :], small[:, 0, :], ACT.Exp).then_inc(exp_ready, 1)
                for u in range(W):
                    act.wait_ge(hT_full, it * W + (u + 1))
                    nc.scalar.copy(hT[0][:, u, :], c.bank[u][:, 0:P]).then_inc(hT_high, 1)

        @block.vector
        def _(dve):
            def each(x):
                return x.unsqueeze(2).broadcast_to([P, W, EXPERTS])

            def hot(i):
                return nc.vector.tensor_tensor(chosen[:, :, :], iota, each(index_f[:, :, i]), ALU.is_equal)

            iota = c.consts[:, IOTA:IOTA + EXPERTS].unsqueeze(1).broadcast_to([P, W, EXPERTS])
            for i, (raw, part) in enumerate(zip(raws, parts)):
                dve.wait_ge(w_high, i + 1)
                nc.vector.tensor_tensor(part[1], raw, fp(part[0]), ALU.subtract).then_inc(w_low, 1)
            if layer == 1:
                dve.wait_ge(bias_loaded, 32)
            with dve.Fori(0, B // W) as it:
                link = Chain(dve, step, it * STEPS)
                norm_on_vector(nc, dve, n, c, it, W, lambda u: c.x[:, bass.ds(it * W + u, 1), :].rearrange("p a n -> p (a n)"))
                for u in range(W):
                    dve.wait_ge(n.xnT_high, it * W + (u + 1))
                    nc.vector.tensor_tensor(xnT[1][:, u, :, :], c.bank[u][:, :].rearrange("p (k t) -> p k t", k=KC),
                                            fp(xnT[0][:, u, :, :]), ALU.subtract).then_inc(n.xnT_low, 1)
                for u in range(W):
                    dve.wait_ge(h_full, it * W + (u + 1))
                    if layer == 1:
                        ins = nc.vector.tensor_tensor(logits[:, u, :], c.bank[u][:, LR:NA], router_bias[:, :], ALU.add)
                    else:
                        ins = nc.vector.tensor_copy(logits[:, u, :], c.bank[u][:, LR:NA])
                link(ins)
                nc.vector.tensor_copy(c.scratch[:, :], c.ones[:, 0:1])
                for u in range(W):
                    ins = nc.vector.max(top[:, u, :], logits[:, u, :])
                link(ins)
                if layer == 1:
                    link(nc.vector.tensor_tensor(cum_terms[:, :, :, :], top[:, :, :].unsqueeze(2).broadcast_to([P, W, EXPERTS, EXPERTS]),
                                                 c.consts[:, TRI:TRI + 64].rearrange("p (k j) -> p k j", k=8).unsqueeze(1)
                                                 .broadcast_to([P, W, EXPERTS, EXPERTS]), ALU.mult))
                    link(nc.vector.tensor_reduce(cum[:, :, :], cum_terms[:, :, :, :], AX.X, ALU.add))
                    link(nc.vector.tensor_scalar(cum[:, :, :], cum[:, :, :], 1.0, None, ALU.subtract))
                    link(nc.vector.tensor_tensor(cum[:, :, :], cum[:, :, :], c.consts[:, RECK:RECK + 8].unsqueeze(1)
                                                 .broadcast_to([P, W, EXPERTS]), ALU.mult))
                    link(nc.vector.tensor_reduce(small[:, 0, :], cum[:, :, :], AX.X, ALU.max))
                    link(nc.vector.tensor_tensor(comb[:, :, :], logits[:, :, :], each(small[:, 0, :]), ALU.subtract))
                    link(nc.vector.tensor_scalar(comb[:, :, :], comb[:, :, :], 0.0, None, ALU.max))
                else:
                    nc.vector.tensor_copy(c.scratch[:, :], c.ones[:, 0:1])
                    for u in range(W):
                        ins = nc.vector.max_index(index[:, u, :], top[:, u, :], logits[:, u, :])
                    link(ins)
                    link(nc.vector.tensor_copy(index_f[:, :, :], index[:, :, :]))
                    if layer == 0:
                        nc.vector.tensor_tensor(small[:, 0, :], top[:, :, 1], top[:, :, 0], ALU.subtract).then_inc(gap_ready, 1)
                        link(hot(0))
                        dve.wait_ge(exp_ready, it + 1)
                        link(nc.vector.tensor_scalar(small[:, 2, :], small[:, 1, :], 1.0, 0.5, ALU.add, ALU.mult))
                        link(nc.vector.reciprocal(small[:, 3, :], small[:, 2, :]))
                        link(nc.vector.tensor_tensor(small[:, 4, :], small[:, 1, :], small[:, 3, :], ALU.mult))
                        link(nc.vector.tensor_tensor(comb[:, :, :], chosen[:, :, :], each(small[:, 3, :]), ALU.mult))
                        link(hot(1))
                        link(nc.vector.tensor_tensor(cum[:, :, :], chosen[:, :, :], each(small[:, 4, :]), ALU.mult))
                        link(nc.vector.tensor_tensor(comb[:, :, :], comb[:, :, :], cum[:, :, :], ALU.add))
                    else:
                        link(hot(0))
                        link(nc.vector.tensor_tensor(comb[:, :, :], chosen[:, :, :], each(top[:, :, 0]), ALU.mult))
                for u in range(W):
                    ins = nc.vector.tensor_tensor(hs[:, u, :].rearrange("p (e r) -> p e r", e=EXPERTS),
                                                  c.bank[u][:, 0:LR].rearrange("p (e r) -> p e r", e=EXPERTS),
                                                  comb[:, u, :].unsqueeze(2).broadcast_to([P, EXPERTS, RANK]), ALU.mult)
                    ins.then_inc(hs_ready, 1)
                for u in range(W):
                    dve.wait_ge(hT_high, it * W + (u + 1))
                    nc.vector.tensor_tensor(hT[1][:, u, :], c.bank[u][:, 0:P], fp(hT[0][:, u, :]), ALU.subtract).then_inc(hT_low, 1)
                for u in range(W):
                    dve.wait_ge(out_full, it * W + (u + 1))
                    if base:
                        dve.wait_ge(bias_added, it * W + (u + 1))
                    xb = c.x[:, bass.ds(it * W + u, 1), :].rearrange("p a n -> p (a n)")
                    nc.vector.tensor_tensor(xb, c.bank[4 + u][:, :], xb, ALU.add).then_inc(added, 1)
                assert link.n == STEPS, link.n


def context_attention(nc, c, d):
    W = HB
    t = "a2_"
    with ExitStack() as ctx:
        def sb(name, shape, dt=F32):
            return ctx.enter_context(nc.sbuf_tensor(t + name, shape, dt))

        def pair(name, shape, dt=F32R):
            return sb(name + "_hi", shape, dt), sb(name + "_lo", shape, dt)

        def sem(name):
            return c.sem(t + name)

        n = layernorm_steps(nc, c, t, ctx, W)
        xnT = pair("xnT", [P, W, KC, P])
        raw = sb("raw", [P, W, D])
        cx = pair("cx", [P, W, D])
        minus_max, sums, inv = sb("minus_max", [P, W]), sb("sums", [P, W]), sb("inv", [P, W])
        prob = sb("prob", [P, W, P])
        pT = pair("pT", [P, W, P])
        loaded = [sem(f"loaded{u}") for u in range(W)]
        cx_high, cx_low = sem("cx_high"), sem("cx_low")
        s_full, max_ready, p_ready, inv_ready = sem("s_full"), sem("max_ready"), sem("p_ready"), sem("inv_ready")
        pT_full, pT_high, pT_low = sem("pT_full"), sem("pT_high"), sem("pT_low")
        out_full, added = sem("out_full"), sem("added")
        block = ctx.enter_context(nc.Block())

        @block.sync
        def _(sp):
            for u in range(W):
                sp.dma_start(raw[:, u, :], d["ctx"][u]).then_inc(loaded[u], 16)
            for u in range(W):
                sp.wait_ge(cx_low, u + 1)
                sp.dma_start(raw[:, u, :], d["ctx"][W + u]).then_inc(loaded[u], 16)

        @block.gpsimd
        def _(pool):
            with pool.Fori(0, B // W) as it:
                rstd_on_pool(nc, pool, n, c, it, W)

        @block.tensor
        def _(pe):
            with pe.Fori(0, B // W) as it:
                for u in range(W):
                    pe.wait_ge(n.xn_ready, it * W + (u + 1))
                    for k in range(KC):
                        ins = nc.tensor.transpose(c.bank[u][:, k * P:(k + 1) * P], n.xn[:, u, k * P:(k + 1) * P], c.ident)
                    ins.then_inc(n.xnT_full, 1)
                for u in range(W):
                    pe.wait_ge(n.xnT_low, it * W + (u + 1))
                    for k in range(KC):
                        ins = split_passes(nc, c.bank[4 + u][:, 0:P], [x[:, u, k, :] for x in xnT],
                                           [x[:, k, bass.ds((it * W + u) * P, P)] for x in c.ctxT], k == 0, k == KC - 1)
                    ins.then_inc(s_full, 1)
                for u in range(W):
                    pe.wait_ge(p_ready, it * W + (u + 1))
                    nc.tensor.transpose(c.bank[4 + u][:, P:2 * P], prob[:, u, :], c.ident).then_inc(pT_full, 1)
                for u in range(W):
                    pe.wait_ge(pT_low, it * W + (u + 1))
                    pe.wait_ge(cx_low, it * W + (u + 1))
                    split_passes(nc, c.bank[u][:, :], [x[:, u, :] for x in pT], [x[:, u, :] for x in cx],
                                 True, True).then_inc(out_full, 1)

        @block.scalar
        def _(act):
            with act.Fori(0, B // W) as it:
                for u in range(W):
                    act.wait_ge(loaded[u], it * 16 + 16)
                    act.wait_ge(added, it * W + (u + 1))
                    nc.scalar.copy(cx[0][:, u, :], raw[:, u, :]).then_inc(cx_high, 1)
                for u in range(W):
                    act.wait_ge(n.xnT_full, it * W + (u + 1))
                    nc.scalar.copy(xnT[0][:, u, :, :], c.bank[u][:, :].rearrange("p (k t) -> p k t", k=KC)).then_inc(n.xnT_high, 1)
                for u in range(W):
                    act.wait_ge(max_ready, it * W + (u + 1))
                    nc.scalar.activation(prob[:, u, :], c.bank[4 + u][:, 0:P], ACT.Exp, bias=minus_max[:, u:u + 1],
                                         accum_out=sums[:, u:u + 1]).then_inc(p_ready, 1)
                for u in range(W):
                    act.wait_ge(pT_full, it * W + (u + 1))
                    nc.scalar.copy(pT[0][:, u, :], c.bank[4 + u][:, P:2 * P]).then_inc(pT_high, 1)

        @block.vector
        def _(dve):
            dve.sem_inc(added, W)
            with dve.Fori(0, B // W) as it:
                for u in range(W):
                    dve.wait_ge(cx_high, it * W + (u + 1))
                    nc.vector.tensor_tensor(cx[1][:, u, :], raw[:, u, :], fp(cx[0][:, u, :]), ALU.subtract).then_inc(cx_low, 1)
                norm_on_vector(nc, dve, n, c, it, W, lambda u: c.x[:, bass.ds(it * W + u, 1), :].rearrange("p a n -> p (a n)"))
                for u in range(W):
                    dve.wait_ge(n.xnT_high, it * W + (u + 1))
                    nc.vector.tensor_tensor(xnT[1][:, u, :, :], c.bank[u][:, :].rearrange("p (k t) -> p k t", k=KC),
                                            fp(xnT[0][:, u, :, :]), ALU.subtract).then_inc(n.xnT_low, 1)
                for u in range(W):
                    dve.wait_ge(s_full, it * W + (u + 1))
                    nc.vector.tensor_reduce(minus_max[:, u:u + 1], c.bank[4 + u][:, 0:P], AX.X, ALU.max, negate=True).then_inc(max_ready, 1)
                for u in range(W):
                    dve.wait_ge(p_ready, it * W + (u + 1))
                    nc.vector.reciprocal(inv[:, u:u + 1], sums[:, u:u + 1]).then_inc(inv_ready, 1)
                for u in range(W):
                    dve.wait_ge(pT_high, it * W + (u + 1))
                    nc.vector.tensor_tensor(pT[1][:, u, :], c.bank[4 + u][:, P:2 * P], fp(pT[0][:, u, :]), ALU.subtract).then_inc(pT_low, 1)
                dve.wait_ge(inv_ready, it * W + W)
                for u in range(W):
                    dve.wait_ge(out_full, it * W + (u + 1))
                    xb = c.x[:, bass.ds(it * W + u, 1), :].rearrange("p a n -> p (a n)")
                    nc.vector.scalar_tensor_tensor(xb, c.bank[u][:, :], inv[:, u:u + 1], xb, ALU.mult, ALU.add).then_inc(added, 1)


def gated_ffn(nc, c, d, xnT):
    t = "f2_"
    with ExitStack() as ctx:
        def sb(name, shape, dt=F32):
            return ctx.enter_context(nc.sbuf_tensor(t + name, shape, dt))

        def pair(name, shape, dt=F32R):
            return sb(name + "_hi", shape, dt), sb(name + "_lo", shape, dt)

        def sem(name):
            return c.sem(t + name)

        packed = sb("packed", [P, 3, D], I32)
        scales = sb("scales", [P, 3, D])
        shifts = sb("shifts", [P, 1 + D], I32)
        weight = sb("weight", [P, 3, D])
        parts = [pair(f"w{i}", [P, D]) for i in (1, 3, 2)]
        gate, hidden = sb("gate", [P, 2, HALF]), sb("hidden", [P, 2, HALF])
        hT = pair("hT", [P, TOK])
        shifts_loaded = sem("shifts_loaded")
        packed_loaded, scales_loaded = sem("packed_loaded"), sem("scales_loaded")
        shifted, unpacked = sem("shifted"), sem("unpacked")
        as_float = sem("as_float")
        weight_ready = sem("weight_ready")
        w_high, w_low = sem("w_high"), sem("w_low")
        w2_high, w2_low = sem("w2_high"), sem("w2_low")
        up_full = sem("up_full")
        gate_ready, hidden_ready, h_high, h_low = sem("gate_ready"), sem("hidden_ready"), sem("h_high"), sem("h_low")
        out_full, added = sem("out_full"), sem("added")
        UP, OUT = c.bank[0:4], c.bank[4:8]
        LAST = HCH - 1
        block = ctx.enter_context(nc.Block())

        @block.sync
        def _(sp):
            sp.dma_start(shifts[:, :], d["shifts"]).then_inc(shifts_loaded, 16)

            def load_packed(ch):
                sp.dma_start(packed[:, :, :], d["L2_packed"][bass.ds(ch, 1)].rearrange("a p w n -> (a p) w n")).then_inc(packed_loaded, 16)

            def load_scales(ch):
                for half in range(2):
                    src = d["L2_s13"][bass.ds(ch, 1), half:half + 1].rearrange("a h w n -> (a h) w n")
                    sp.dma_start(scales[64 * half:64 * half + 64, 0:2, :],
                                 src.partition_broadcast(64).rearrange("p a w n -> p (a w) n")).then_inc(scales_loaded, 16)
                for q in range(4):
                    src = d["L2_s2"][bass.ds(ch, 1), q:q + 1].rearrange("a q n -> (a q) n")
                    sp.dma_start(scales[32 * q:32 * q + 32, 2, :],
                                 src.partition_broadcast(32).rearrange("p a n -> p (a n)")).then_inc(scales_loaded, 16)

            load_packed(0)
            load_scales(0)
            with sp.Fori(1, HCH) as ch:
                sp.wait_ge(weight_ready, ch * 3)
                load_packed(ch)
                load_scales(ch)

        @block.gpsimd
        def _(pool):
            def scale(ch):
                pool.wait_ge(scales_loaded, ch * 96 + 96)
                for w in range(3):
                    pool.wait_ge(as_float, ch * 3 + (w + 1))
                    nc.gpsimd.tensor_tensor(weight[:, w, :], weight[:, w, :], scales[:, w, :], ALU.mult).then_inc(weight_ready, 1)

            def low(ch):
                for w in range(3):
                    if w < 2:
                        pool.wait_ge(w_high, ch * 2 + (w + 1))
                    else:
                        pool.wait_ge(w2_high, ch + 1)
                    nc.gpsimd.tensor_tensor(parts[w][1][:, :], weight[:, w, :], fp(parts[w][0][:, :]),
                                            ALU.subtract).then_inc(w_low if w < 2 else w2_low, 1)

            with pool.Fori(0, HCH) as ch:
                scale(ch)
                low(ch)

        @block.tensor
        def _(pe):
            def chunk(ch):
                pe.wait_ge(w_low, ch * 2 + 2)
                for half in range(2):
                    pe.wait_ge(hidden_ready, ch * 2 + (half + 1))
                    for w in range(2):
                        for k in range(KC):
                            ins = split_passes(nc, UP[2 * half + w][:, :], [x[:, k * P:(k + 1) * P] for x in parts[w]],
                                               [x[:, k, half * HALF:(half + 1) * HALF] for x in xnT], k == 0, k == KC - 1)
                        ins.then_inc(up_full, 1)
                pe.wait_ge(w2_low, ch + 1)
                for b in range(B):
                    if b % HB == 0:
                        pe.wait_ge(h_low, ch * 2 + (b // HB + 1))
                    pe.wait_ge(added, ch * B + (b + 1))
                    split_passes(nc, OUT[b % 4][:, :], [x[:, b * P:(b + 1) * P] for x in hT], [x[:, :] for x in parts[2]],
                                 True, True).then_inc(out_full, 1)

            with pe.Fori(0, HCH) as ch:
                chunk(ch)

        @block.scalar
        def _(act):
            def high(ch, w):
                act.wait_ge(weight_ready, ch * 3 + (w + 1))
                nc.scalar.copy(parts[w][0][:, :], weight[:, w, :]).then_inc(w_high if w < 2 else w2_high, 1)

            def to_float(ch):
                for w in range(3):
                    act.wait_ge(unpacked, ch * 3 + (w + 1))
                    nc.scalar.copy(weight[:, w, :], packed[:, w, :]).then_inc(as_float, 1)

            def chunk(ch, more):
                if more:
                    act.wait_ge(w_low, ch * 2 + 2)
                    act.wait_ge(w2_low, ch + 1)
                    to_float(ch + 1)
                for half in range(2):
                    act.wait_ge(up_full, ch * 4 + (2 * half + 1))
                    nc.scalar.activation(gate[:, half, :], UP[2 * half][:, :], ACT.Silu).then_inc(gate_ready, 1)
                    act.wait_ge(hidden_ready, ch * 2 + (half + 3))
                    nc.scalar.copy(hT[0][:, half * HALF:(half + 1) * HALF], hidden[:, half, :]).then_inc(h_high, 1)
                if more:
                    act.wait_ge(up_full, ch * 4 + 4)
                    high(ch + 1, 0)
                    high(ch + 1, 1)
                    act.wait_ge(out_full, ch * B + B)
                    high(ch + 1, 2)

            to_float(0)
            high(0, 0)
            high(0, 1)
            high(0, 2)
            with act.Fori(0, LAST) as ch:
                chunk(ch, True)
            chunk(LAST, False)

        @block.vector
        def _(dve):
            def unpack(ch):
                dve.wait_ge(packed_loaded, ch * 16 + 16)
                for w in range(3):
                    by = shifts[:, 0:1].broadcast_to([P, D]) if w < 2 else shifts[:, 1:1 + D]
                    nc.vector.tensor_tensor(packed[:, w, :], packed[:, w, :], by, ALU.logical_shift_left).then_inc(shifted, 1)
                for w in range(3):
                    dve.wait_ge(shifted, ch * 3 + (w + 1))
                    nc.vector.tensor_scalar(packed[:, w, :], packed[:, w, :], 28, None, ALU.arith_shift_right).then_inc(unpacked, 1)

            def chunk(ch, more):
                if more:
                    unpack(ch + 1)
                for half in range(2):
                    dve.wait_ge(up_full, ch * 4 + (2 * half + 2))
                    dve.wait_ge(gate_ready, ch * 2 + (half + 1))
                    nc.vector.tensor_tensor(hidden[:, half, :], UP[2 * half + 1][:, :], gate[:, half, :], ALU.mult).then_inc(hidden_ready, 1)
                    dve.wait_ge(h_high, ch * 2 + (half + 1))
                    cols = slice(half * HALF, (half + 1) * HALF)
                    nc.vector.tensor_tensor(hT[1][:, cols], hidden[:, half, :], fp(hT[0][:, cols]), ALU.subtract).then_inc(h_low, 1)
                for b in range(B):
                    dve.wait_ge(out_full, ch * B + (b + 1))
                    nc.vector.tensor_tensor(c.x[:, b, :], OUT[b % 4][:, :], c.x[:, b, :], ALU.add).then_inc(added, 1)
            dve.sem_inc(hidden_ready, 2)
            dve.sem_inc(added, 4)
            dve.wait_ge(shifts_loaded, 16)
            unpack(0)
            with dve.Fori(0, LAST) as ch:
                chunk(ch, True)
            chunk(LAST, False)


class Place:

    def __init__(self, base, names):
        self.base, self.names = base, names

    def __call__(self, name):
        return self.base + self.names.index(name)


def wide_head_attention(nc, c, d, xnT):
    G, H = 8, 4
    t = "a3_"
    N = B
    TICKS = N + 5
    LATE = {0: ["q10"], 1: ["q11"], 2: ["q12", "s10"], 3: ["q13", "s11"]}
    EARLY = {8: ["k0", "k1"], 9: ["sk0", "v0", "sk1", "v1"], 10: ["q00", "w0", "q01"],
             11: ["r0", "q02", "s00"], 12: ["r1", "q03", "w1", "s01"]}
    early = [x for n in sorted(EARLY) for x in EARLY[n]]
    body = []
    for n in range(TICKS):
        body += [f"o{n - 4}"] if 0 <= n - 4 < N else []
        body += LATE.get(n, []) + EARLY.get(n, [])
    assert len(early) % 2 == 0 and len(body) % 2 == 0

    def by_act(names):
        return [x for x in names if x[0] in "kqw"]

    def squares(names):
        return [x for x in names if x[0] in "kq"]

    class Where:

        def __init__(self, g, last=False):
            first = g is None
            names = early if first else body
            if last:
                names = [x for x in body if x not in early]

            def base(f):
                return 0 if first else g * len(f(body)) + len(f(early))

            self.tile = Place(base(list), names)
            self.high = Place(base(by_act), by_act(names))
            self.names = names

        def bank(self, name):
            return M[self.names.index(name) % 2]

        def ring(self, name):
            return squares(self.names).index(name) % 2

    M = c.bank[6:8]
    with ExitStack() as ctx:
        def sb(name, shape, dt=F32):
            return ctx.enter_context(nc.sbuf_tensor(t + name, shape, dt))

        def pair(name, shape, dt=F32R):
            return sb(name + "_hi", shape, dt), sb(name + "_lo", shape, dt)

        def sem(name):
            return c.sem(t + name)

        raw = sb("raw", [P, 4 * D])
        wq, wo = pair("wq", [P, KC * H * P]), pair("wo", [P, H * D])
        wkv = pair("wkv", [P, 2 * KC * P])
        norms = sb("norms", [P, 2])
        mask = sb("mask", [P, P])
        square = sb("square", [P, 2, HALF])
        qT = pair("qT", [P, H, TOK])
        kT = pair("kT", [P, TOK])
        v = pair("v", [P, B, P])
        held_k, held_v = sb("held_k", [P, TOK]), sb("held_v", [P, TOK])
        diag = sb("diag", [P, HB, P])
        var_q, rq = sb("var_q", [P, B, H]), sb("rq", [P, B, H])
        var_k, rk = sb("var_k", [P, B]), sb("rk", [P, B])
        minus_max, sums, inv = sb("minus_max", [P, 3, H]), sb("sums", [P, 3, H]), sb("inv", [P, 3, H])
        prob = sb("prob", [P, 3, H, P])
        pT = pair("pT", [P, HALF])
        oT = pair("oT", [P, H, P])

        once_loaded = sem("once_loaded")
        raw_loaded = sem("raw_loaded")
        raw_high = sem("raw_high")
        raw_split = sem("raw_split")
        m_full = sem("m_full")
        m_high = sem("m_high")
        m_free = sem("m_free")
        rk_ready, rq_ready = sem("rk_ready"), sem("rq_ready")
        diag_ready = sem("diag_ready")
        k_high, k_low = sem("k_high"), sem("k_low")
        s_full = sem("s_full")
        s_free = sem("s_free")
        max_ready, exp_ready, inv_ready = sem("max_ready"), sem("exp_ready"), sem("inv_ready")
        p_ready = sem("p_ready")
        pT_full, pT_high, pT_low = sem("pT_full"), sem("pT_high"), sem("pT_low")
        o_full, o_high, o_low = sem("o_full"), sem("o_high"), sem("o_low")
        S, PT, OB = c.bank[0:2], c.bank[2:4], c.bank[4:6]

        block = ctx.enter_context(nc.Block())

        @block.sync
        def _(sp):
            sp.dma_start(norms[:, :], d["L3_norms"]).then_inc(once_loaded, 16)
            sp.dma_start(mask[:, :], d["mask"]).then_inc(once_loaded, 16)

            def load(g, name, width):
                sp.dma_start(raw[:, 0:width], d[name][bass.ds(g, 1)].rearrange("a p n -> (a p) n")).then_inc(raw_loaded, 16)

            load(0, "L3_wkv", 2 * D)
            sp.wait_ge(raw_split, 1)
            load(0, "L3_wq", 4 * D)
            sp.wait_ge(raw_split, 2)
            load(0, "L3_wo", 4 * D)
            with sp.Fori(1, G) as g:
                sp.wait_ge(raw_split, g * 3)
                load(g, "L3_wkv", 2 * D)
                sp.wait_ge(raw_split, g * 3 + 1)
                load(g, "L3_wq", 4 * D)
                sp.wait_ge(raw_split, g * 3 + 2)
                load(g, "L3_wo", 4 * D)

        @block.gpsimd
        def _(pool):
            def split(g, slab, piece):
                w, first, pieces = ((wkv, 0, 2), (wq, 2, 4), (wo, 6, 4))[slab]
                cols = slice(piece * D, (piece + 1) * D)
                if piece == 0:
                    pool.wait_ge(raw_loaded, g * 48 + (slab * 16 + 16))
                nc.gpsimd.tensor_tensor(w[0][:, cols], raw[:, cols], c.ones[:, 0:1].broadcast_to([P, D]), ALU.mult).then_inc(raw_high, 1)
                pool.wait_ge(raw_high, g * 10 + (first + piece + 1))
                ins = nc.gpsimd.tensor_tensor(w[1][:, cols], raw[:, cols], fp(w[0][:, cols]), ALU.subtract)
                if piece == pieces - 1:
                    ins.then_inc(raw_split, 1)

            def factors(g, w, name):
                if name[:2] == "sk":
                    half = int(name[2])
                    cols = slice(half * HB, (half + 1) * HB)
                    pool.wait_ge(m_free, w.tile(name) + 3)
                    nc.gpsimd.tensor_tensor(rk[:, cols], var_k[:, cols], c.minus_half[:, 0:HB], ALU.pow).then_inc(rk_ready, 1)
                elif name[0] == "s":
                    half, j = int(name[1]), int(name[2])
                    part = slice(half * HB, (half + 1) * HB), slice(2 * j, 2 * j + 2)
                    pool.wait_ge(m_free, w.tile(name) + 3)
                    nc.gpsimd.tensor_tensor(rq[:, part[0], part[1]], var_q[:, part[0], part[1]],
                                            c.minus_half[:, 0:2 * HB].rearrange("p (b a) -> p b a", b=HB), ALU.pow).then_inc(rq_ready, 1)

            def attention(g, w, more):
                work = {0: [(2, 0), (2, 1)], 1: [(2, 2)], 2: [(2, 3)]}
                if more:
                    work |= {5: [(0, 0), (0, 1)], 6: [(1, 0)], 7: [(1, 1)], 8: [(1, 2)], 9: [(1, 3)]}
                for n in range(TICKS):
                    if 0 <= n - 1 < N:
                        b = n - 1
                        pool.wait_ge(inv_ready, g * N + (b + 1))
                        nc.gpsimd.tensor_tensor(prob[:, b % 3, :, :], prob[:, b % 3, :, :],
                                                inv[:, b % 3, :].unsqueeze(2).broadcast_to([P, H, P]), ALU.mult).then_inc(p_ready, 1)
                    for name in LATE.get(n, []):
                        factors(g, w, name)
                    for slab, piece in work.get(n, []):
                        if (slab, piece) == (2, 0):
                            pool.wait_ge(m_free, w.tile.base + 2)
                        if (slab, piece) == (1, 0):
                            pool.wait_ge(m_free, w.tile("q13") + 3)
                        split(g if slab == 2 else g + 1, slab, piece)
                    if more:
                        for name in EARLY.get(n, []):
                            factors(g + 1, w, name)

            for piece in range(2):
                split(0, 0, piece)
            for piece in range(4):
                split(0, 1, piece)
            for name in early:
                factors(0, Where(None), name)
            with pool.Fori(0, G - 1) as g:
                attention(g, Where(g), True)
            attention(G - 1, Where(G - 1, True), False)

        @block.tensor
        def _(pe):
            def project(w, name, weights, rhs, half):
                bank = w.bank(name)
                for k in range(KC):
                    ins = split_passes(nc, bank[:, :], [x[k] for x in weights], [x[:, k, half * HALF:(half + 1) * HALF] for x in rhs],
                                       k == 0, k == KC - 1)
                ins.then_inc(m_full, 1)

            def tile(g, w, name):
                pe.wait_ge(m_free, w.tile(name) + 1)
                bank = w.bank(name)
                kind, half = name[0], int(name[-1] if name[:2] == "sk" else name[1])
                if kind in "kv":
                    if name == "k0":
                        pe.wait_ge(raw_split, g * 3 + 1)
                    o = 0 if kind == "k" else KC
                    project(w, name, [[x[:, (o + k) * P:(o + k + 1) * P] for k in range(KC)] for x in wkv], c.ctxT, half)
                elif kind == "q":
                    if name == "q00":
                        pe.wait_ge(raw_split, g * 3 + 2)
                    a = int(name[2])
                    project(w, name, [[x[:, (k * H + a) * P:(k * H + a + 1) * P] for k in range(KC)] for x in wq], xnT, half)
                elif kind == "w":
                    pe.wait_ge(m_free, w.tile(f"v{half}") + 3)
                    for u in range(HB):
                        b = half * HB + u
                        ins = nc.tensor.transpose(bank[:, u * P:(u + 1) * P], held_v[:, b * P:(b + 1) * P], c.ident)
                    ins.then_inc(m_full, 1)
                elif kind == "r":
                    pe.wait_ge(diag_ready, g * 2 + (half + 1))
                    nc.tensor.matmul(bank[:, :], c.ones[:, :], diag[:, :, :].rearrange("p a n -> p (a n)"),
                                     start=True, stop=True).then_inc(m_full, 1)
                else:
                    of = [f"k{half}"] if name[:2] == "sk" else [f"q{half}{2 * int(name[2]) + i}" for i in range(2)]
                    pe.wait_ge(m_high, w.high(of[-1]) + 1)
                    for i, q in enumerate(of):
                        for u in range(HB):
                            col = u * len(of) + i
                            ins = nc.tensor.matmul(bank[:, col:col + 1], square[:, w.ring(q), u * P:(u + 1) * P], c.ones[:, 0:1],
                                                   start=True, stop=True)
                    ins.then_inc(m_full, 1)

            def attention(g, w, more):
                for n in range(TICKS):
                    if n < N:
                        b = n
                        if b == 0:
                            pe.wait_ge(k_low, g * 2 + 2)
                            pe.wait_ge(m_free, w.tile.base + 2)
                        if b == HB:
                            pe.wait_ge(m_free, w.tile("q13") + 3)
                        pe.wait_ge(s_free, g * N + (n + 1))
                        tok = slice(b * P, (b + 1) * P)
                        for h in range(H):
                            ins = split_passes(nc, S[n % 2][:, h * P:(h + 1) * P], [x[:, h, tok] for x in qT], [x[:, tok] for x in kT],
                                               True, True)
                        ins.then_inc(s_full, 1)
                    if 0 <= n - 4 < N:
                        b = n - 4
                        if b == 0:
                            pe.wait_ge(raw_split, g * 3 + 3)
                        pe.wait_ge(m_free, w.tile(f"o{b}") + 1)
                        pe.wait_ge(o_low, g * N + (b + 1))
                        for h in range(H):
                            ins = split_passes(nc, w.bank(f"o{b}")[:, :], [x[:, h, :] for x in oT],
                                               [x[:, h * D:(h + 1) * D] for x in wo], h == 0, h == H - 1)
                        ins.then_inc(m_full, 1)
                    if 0 <= n - 3 < N:
                        b = n - 3
                        pe.wait_ge(pT_low, g * N + (b + 1))
                        split_passes(nc, OB[b % 2][:, :], [x[:, b, :] for x in v], [x[:, :] for x in pT], True, True).then_inc(o_full, 1)
                    if 0 <= n - 2 < N:
                        b = n - 2
                        pe.wait_ge(p_ready, g * N + (b + 1))
                        for h in range(H):
                            ins = nc.tensor.transpose(PT[b % 2][:, h * P:(h + 1) * P], prob[:, b % 3, h, :], c.ident)
                        ins.then_inc(pT_full, 1)
                    for name in LATE.get(n, []):
                        tile(g, w, name)
                    if more:
                        for name in EARLY.get(n, []):
                            tile(g + 1, w, name)

            pe.wait_ge(once_loaded, 32)
            for name in early:
                tile(0, Where(None), name)
            with pe.Fori(0, G - 1) as g:
                attention(g, Where(g), True)
            attention(G - 1, Where(G - 1, True), False)

        @block.scalar
        def _(act):
            def tile(g, w, name):
                kind, half = name[0], int(name[1]) if name[:2] != "sk" else 0
                bank = w.bank(name)
                if kind == "w":
                    act.wait_ge(m_full, w.tile(name) + 1)
                    nc.scalar.copy(v[0][:, half * HB:(half + 1) * HB, :], bank[:, :].rearrange("p (b n) -> p b n", b=HB)).then_inc(m_high, 1)
                elif kind in "kq":
                    act.wait_ge(m_full, w.tile(name) + 1)
                    if kind == "q":
                        nc.scalar.activation(qT[0][:, int(name[2]), half * HALF:(half + 1) * HALF], bank[:, :], ACT.Copy, scale=norms[:, 0:1])
                    before = {"k0": "s11", "q00": "sk1", "q02": "s00", "q12": "s10"}.get(name)
                    if name == "q10":
                        act.wait_ge(m_full, w.tile.base)
                    elif before in w.names:
                        act.wait_ge(m_full, w.tile(before) + 1)
                    nc.scalar.activation(square[:, w.ring(name), :], bank[:, :], ACT.Square).then_inc(m_high, 1)
                elif kind == "r":
                    act.wait_ge(m_free, w.tile(name) + 3)
                    cols = slice(half * HALF, (half + 1) * HALF)
                    nc.scalar.copy(kT[0][:, cols], held_k[:, cols]).then_inc(k_high, 1)

            def attention(g, w, more):
                for n in range(TICKS):
                    if n < N:
                        act.wait_ge(max_ready, g * N + (n + 1))
                        for h in range(H):
                            ins = nc.scalar.activation(prob[:, n % 3, h, :], prob[:, n % 3, h, :], ACT.Exp,
                                                       bias=minus_max[:, n % 3, h:h + 1], accum_out=sums[:, n % 3, h:h + 1])
                        ins.then_inc(exp_ready, 1)
                    if 0 <= n - 3 < N:
                        b = n - 3
                        act.wait_ge(o_full, g * N + (b + 1))
                        nc.scalar.copy(oT[0][:, :, :], OB[b % 2][:, :].rearrange("p (h t) -> p h t", h=H)).then_inc(o_high, 1)
                    if 0 <= n - 2 < N:
                        b = n - 2
                        act.wait_ge(pT_full, g * N + (b + 1))
                        nc.scalar.copy(pT[0][:, :], PT[b % 2][:, :]).then_inc(pT_high, 1)
                    for name in LATE.get(n, []):
                        tile(g, w, name)
                    if more:
                        for name in EARLY.get(n, []):
                            tile(g + 1, w, name)

            act.wait_ge(once_loaded, 32)
            for name in early:
                tile(0, Where(None), name)
            with act.Fori(0, G - 1) as g:
                attention(g, Where(g), True)
            attention(G - 1, Where(G - 1, True), False)

        @block.vector
        def _(dve):
            def diagonal(half):
                nc.vector.tensor_tensor(diag[:, :, :], c.ident.unsqueeze(1).broadcast_to([P, HB, P]),
                                        rk[:, half * HB:(half + 1) * HB].unsqueeze(2).broadcast_to([P, HB, P]),
                                        ALU.mult).then_inc(diag_ready, 1)

            def key_low(g, half):
                cols = slice(half * HALF, (half + 1) * HALF)
                dve.wait_ge(k_high, g * 2 + (half + 1))
                nc.vector.tensor_tensor(kT[1][:, cols], held_k[:, cols], fp(kT[0][:, cols]), ALU.subtract).then_inc(k_low, 1)

            def tile(g, w, name):
                bank = w.bank(name)
                if name[:2] == "sk":
                    half = int(name[2])
                    dve.wait_ge(m_full, w.tile(name) + 1)
                    nc.vector.tensor_scalar(var_k[:, half * HB:(half + 1) * HB], bank[:, 0:HB], 1.0 / P, EPS,
                                            ALU.mult, ALU.add).then_inc(m_free, 1)
                    return
                kind, half = name[0], int(name[1])
                cols = slice(half * HALF, (half + 1) * HALF)
                if kind == "s":
                    j = int(name[2])
                    dve.wait_ge(m_full, w.tile(name) + 1)
                    nc.vector.tensor_scalar(var_q[:, half * HB:(half + 1) * HB, 2 * j:2 * j + 2],
                                            bank[:, 0:2 * HB].rearrange("p (b a) -> p b a", a=2), P * EPS, None,
                                            ALU.add).then_inc(m_free, 1)
                    if half == 0:
                        key_low(g, j)
                elif kind == "v":
                    dve.wait_ge(m_full, w.tile(name) + 1)
                    nc.vector.tensor_copy(held_v[:, cols], bank[:, :]).then_inc(m_free, 1)
                elif kind == "w":
                    part = slice(half * HB, (half + 1) * HB)
                    dve.wait_ge(m_high, w.high(name) + 1)
                    nc.vector.tensor_tensor(v[1][:, part, :], bank[:, :].rearrange("p (b n) -> p b n", b=HB), fp(v[0][:, part, :]),
                                            ALU.subtract).then_inc(m_free, 1)
                elif kind == "k":
                    dve.wait_ge(m_high, w.high(name) + 1)
                    nc.vector.tensor_scalar(held_k[:, cols], bank[:, :], norms[:, 1:2], None, ALU.mult).then_inc(m_free, 1)
                elif kind == "q":
                    a = int(name[2])
                    dve.wait_ge(m_high, w.high(name) + 1)
                    nc.vector.scalar_tensor_tensor(qT[1][:, a, cols], bank[:, :], norms[:, 0:1], fp(qT[0][:, a, cols]),
                                                   ALU.mult, ALU.subtract).then_inc(m_free, 1)
                    if name == "q00":
                        dve.wait_ge(rk_ready, g * 2 + 1)
                        diagonal(0)
                elif kind == "r":
                    dve.wait_ge(m_full, w.tile(name) + 1)
                    if half == 0:
                        dve.wait_ge(rk_ready, g * 2 + 2)
                        diagonal(1)
                    nc.vector.tensor_tensor(held_k[:, cols], bank[:, :], held_k[:, cols], ALU.mult).then_inc(m_free, 1)

            def attention(g, w, more):
                for n in range(TICKS):
                    if n < N:
                        r = n % 3
                        if n % HB == 0:
                            dve.wait_ge(rq_ready, g * 4 + (2 * (n // HB) + 2))
                        dve.wait_ge(s_full, g * N + (n + 1))
                        for h in range(H):
                            ins = nc.vector.scalar_tensor_tensor(prob[:, r, h, :], S[n % 2][:, h * P:(h + 1) * P], rq[:, n, h:h + 1],
                                                                 mask[:, :], ALU.mult, ALU.add)
                        ins.then_inc(s_free, 1)
                        dve.wait_ge(s_free, g * N + (n + 3))
                        nc.vector.tensor_reduce(minus_max[:, r, :], prob[:, r, :, :], AX.X, ALU.max, negate=True).then_inc(max_ready, 1)
                    if 0 <= n - 3 < N:
                        b = n - 3
                        dve.wait_ge(o_high, g * N + (b + 1))
                        nc.vector.tensor_tensor(oT[1][:, :, :], OB[b % 2][:, :].rearrange("p (h t) -> p h t", h=H),
                                                fp(oT[0][:, :, :]), ALU.subtract).then_inc(o_low, 1)
                    if 0 <= n - 2 < N:
                        b = n - 2
                        dve.wait_ge(pT_high, g * N + (b + 1))
                        nc.vector.tensor_tensor(pT[1][:, :], PT[b % 2][:, :], fp(pT[0][:, :]), ALU.subtract).then_inc(pT_low, 1)
                    if 0 <= n - 4 < N:
                        b = n - 4
                        dve.wait_ge(m_full, w.tile(f"o{b}") + 1)
                        nc.vector.tensor_tensor(c.x[:, b, :], w.bank(f"o{b}")[:, :], c.x[:, b, :], ALU.add).then_inc(m_free, 1)
                    if n < N:
                        dve.wait_ge(exp_ready, g * N + (n + 1))
                        nc.vector.reciprocal(inv[:, n % 3, :], sums[:, n % 3, :]).then_inc(inv_ready, 1)
                    for name in LATE.get(n, []):
                        tile(g, w, name)
                    if more:
                        for name in EARLY.get(n, []):
                            tile(g + 1, w, name)

            dve.sem_inc(m_free, 2)
            dve.sem_inc(s_free, 2)
            dve.wait_ge(once_loaded, 32)
            for name in early:
                tile(0, Where(None), name)
            with dve.Fori(0, G - 1) as g:
                attention(g, Where(g), True)
            attention(G - 1, Where(G - 1, True), False)


def build(nc, d, upto=range(8)):
    with ExitStack() as ctx:
        c = Chip()
        in_use = []

        def new_semaphore(name):
            in_use.append(nc.alloc_semaphore(name))
            return in_use[-1]

        def clear_semaphores():
            nc.clear_and_free_semaphores(in_use)
            in_use.clear()
            nc.all_engine_barrier()

        c.sem = new_semaphore
        c.x = ctx.enter_context(nc.sbuf_tensor("x", [P, B, D], F32))
        c.ctxT = [ctx.enter_context(nc.sbuf_tensor(f"ctxT_{n}", [P, KC, TOK], F32R)) for n in ("hi", "lo")]
        c.consts = ctx.enter_context(nc.sbuf_tensor("consts_sb", [P, CONSTS], F32))
        c.ones = ctx.enter_context(nc.sbuf_tensor("ones", [P, P], F32))
        c.scratch = ctx.enter_context(nc.sbuf_tensor("scratch", [P, 1], F32))
        c.minus_half = ctx.enter_context(nc.sbuf_tensor("minus_half", [P, 40], F32))
        c.ident = c.consts[:, IDENT:IDENT + P]
        c.bank = [ctx.enter_context(nc.psum_tensor(f"bank{n}", [P, HALF], F32)) for n in range(8)]
        load_inputs(nc, c, d)

        def with_xnT(t, body, bias=None):
            with ExitStack() as inner:
                xnT = [inner.enter_context(nc.sbuf_tensor(f"{t}_{n}", [P, KC, TOK], F32R)) for n in ("xnT_hi", "xnT_lo")]
                norm_transpose(nc, c, d, t + "_", xnT, bias)
                body(xnT)

        steps = [
            lambda: with_xnT("n0", lambda xnT: small_head_attention(nc, c, d, 0, xnT)),
            lambda: moe_ffn(nc, c, d, 0),
            lambda: with_xnT("n1", lambda xnT: small_head_attention(nc, c, d, 1, xnT), "L1_bo"),
            lambda: moe_ffn(nc, c, d, 1),
            lambda: context_attention(nc, c, d),
            lambda: with_xnT("n2", lambda xnT: gated_ffn(nc, c, d, xnT)),
            lambda: with_xnT("n3", lambda xnT: wide_head_attention(nc, c, d, xnT)),
            lambda: moe_ffn(nc, c, d, 3),
        ]
        for n, step in enumerate(steps):
            if n in upto:
                step()
                clear_semaphores()
        store_output(nc, c, d)


def layouts(a):
    f = {n: np.asarray(v) for n, v in a.items()}
    o = {"x": f["x"], "consts": constants()}

    def rows(w, n=KC):
        return w.reshape(n, P, -1).transpose(1, 0, 2)

    ctx = f["ctx_4096"]
    o["ctxT"] = rows(ctx.transpose(2, 0, 1).reshape(D, TOK))
    o["ctx"] = ctx
    o["mask"] = f["mask_1x1xSxS2_ff0"].reshape(P, P)
    o["L0_wq"] = f["L0_xattn_Wq"].reshape(KC, P, 8, 4, 16).transpose(3, 1, 0, 2, 4).reshape(4, P, KC, P)
    o["L0_wkv"] = np.concatenate([rows(f["L0_xattn_Wk"]), rows(f["L0_xattn_Wv"])], 1)
    o["L0_wo"] = f["L0_xattn_Wo"].reshape(8, 4, 16, D).transpose(1, 0, 2, 3).reshape(4, P, D)
    o["L1_wqkv"] = np.stack([f[f"L1_xattn_W{n}"].reshape(KC, P, D) for n in "qkv"], 2)
    o["L1_wo"] = f["L1_xattn_Wo"].T.reshape(KC, P, D)
    o["L1_bias"] = np.stack([f[f"L1_xattn_b{n}"].reshape(KC, P).T for n in "qkv"], 2)
    o["L1_bo"] = f["L1_xattn_bo"].reshape(1, D)
    inter = np.broadcast_to(f["L1_xattn_interference"].reshape(KC, 4, 1, 4, 4), (KC, 4, 8, 4, 4))
    o["L1_inter"] = inter.reshape(KC, P, 4).transpose(1, 0, 2)
    o["L1_amp"] = np.broadcast_to(f["L1_xattn_amp"].reshape(1, 1), (P, 1))
    for n, a, r, bb in ((0, f["L0_ffn_A_stack"], "L0_ffn_W_router", f["L0_ffn_B_stack"].transpose(0, 2, 1)),
                        (1, f["L1_ffn_lora_A"].transpose(0, 2, 1), "L1_ffn_W_router", f["L1_ffn_lora_B"]),
                        (3, f["L3_ffn_A"], "L3_ffn_route_w", f["L3_ffn_Bw"].transpose(0, 2, 1))):
        o[f"L{n}_wa"] = rows(np.concatenate([a.reshape(LR, D), f[r]]).T)
        o[f"L{n}_wb"] = bb.reshape(LR, D)
        if n != 3:
            o[f"L{n}_w0"] = rows(f[f"L{n}_ffn_W_base"].T)
            o[f"L{n}_b0"] = f[f"L{n}_ffn_b_base"].reshape(1, D)
    o["L1_br"] = f["L1_ffn_b_router"].reshape(1, EXPERTS)

    pad = HCH * P - HIDDEN
    w13 = []
    for n in (1, 3):
        w = f[f"L2_ffn_w{n}"].reshape(HIDDEN, KC, 64).transpose(2, 1, 0)
        w = np.concatenate([w, w])
        w13.append(np.pad(w, ((0, 0), (0, 0), (0, pad))).reshape(P, KC, HCH, P).transpose(2, 0, 1, 3).reshape(HCH, P, D))
    blocks = HIDDEN // 32
    u = blocks * np.arange(D)[None, :] + np.arange(blocks)[:, None]
    w2 = f["L2_ffn_w2"].reshape(-1, 2, 32)[u // 4, u % 2]
    w2 = np.pad(w2.transpose(0, 2, 1).reshape(HIDDEN, D), ((0, pad), (0, 0))).reshape(HCH, P, D)
    o["L2_packed"] = np.stack([*w13, w2], 2)
    s13 = []
    for n in (1, 3):
        s = np.pad(f[f"L2_ffn_s{n}"].reshape(HIDDEN, KC, 2), ((0, pad), (0, 0), (0, 0)))
        s13.append(s.reshape(HCH, P, KC, 2).transpose(0, 3, 2, 1).reshape(HCH, 2, D))
    o["L2_s13"] = np.stack(s13, 2)
    o["L2_s2"] = np.pad(f["L2_ffn_s2"][u // 2], ((0, pad // 32), (0, 0))).reshape(HCH, 4, D)
    upper13 = np.arange(P)[:, None] < 64
    upper2 = (blocks * np.arange(D)[None, :] + np.arange(P)[:, None] // 32) % 4 < 2
    o["shifts"] = np.where(np.concatenate([upper13, upper2], 1), 24, 28).astype(np.int32)

    wq = f["L3_xattn_q_proj_w"].reshape(8, 4 * P, KC, P).transpose(0, 3, 2, 1)
    o["L3_wq"] = wq.reshape(8, P, 4 * D)
    wkv = [f[f"L3_xattn_{n}_proj_w"].reshape(8, P, KC, P).transpose(0, 3, 2, 1).reshape(8, P, D) for n in "kv"]
    o["L3_wkv"] = np.concatenate(wkv, 2)
    o["L3_wo"] = f["L3_xattn_o_proj_w"].reshape(D, 8, 4, P).transpose(1, 3, 2, 0).reshape(8, P, 4 * D)
    o["L3_norms"] = np.stack([f["L3_xattn_q_norm_w"], f["L3_xattn_k_norm_w"]], 1)
    return {n: np.ascontiguousarray(v) for n, v in o.items()}


def kernel(**inputs):
    import concourse.bacc as bacc
    from concourse.bass_utils import run_bass_kernel_spmd

    arrays = layouts(inputs)
    nc = bacc.Bacc("TRN2", target_bir_lowering=False, num_devices=1)
    d = {n: nc.dram_tensor(f"in_{n}", v.shape, mybir.dt.from_np(v.dtype), kind="ExternalInput").ap() for n, v in arrays.items()}
    d["out"] = nc.dram_tensor("out_x", (B, P, D), F32, kind="ExternalOutput").ap()
    build(nc, d)
    r = run_bass_kernel_spmd(nc, [{f"in_{n}": v for n, v in arrays.items()}], core_ids=[0])
    return r.results[0]["out_x"]
```

```python
from contextlib import ExitStack

import numpy as np

import concourse.bass as bass
from concourse import mybir
from concourse.alu_op_type import AluOpType as ALU

ACT = mybir.ActivationFunctionType
AX = mybir.AxisListType
F32 = mybir.dt.float32
F32R = mybir.dt.float32r
F16 = mybir.dt.float16
BF16 = mybir.dt.bfloat16
I32 = mybir.dt.int32
U32 = mybir.dt.uint32

P = 128
B = 8
D = 512
KC = D // P
TOK = B * P
HALF = TOK // 2
HB = B // 2
EPS = 1e-5
EXPERTS, RANK = 8, 16
LR = EXPERTS * RANK
HIDDEN = 1376
HCH = -(-HIDDEN // P)
PASSES = ((0, 0), (0, 1), (1, 0))


class Chip:
    pass


def split_passes(nc, out, stationary, moving, first, last):
    for n, (s, m) in enumerate(PASSES):
        ins = nc.tensor.matmul(out, stationary[s], moving[m], start=first and n == 0, stop=last and n == 2)
    return ins


def fp(ap):
    return ap.bitcast(F32)


def take_stats(nc, c, b):
    nc.vector.bn_stats(c.stats[:, b, :], c.x[:, b, :])


class NormTransposed:

    def __init__(self, nc, c, t, ctx, xnT, ring):
        def sb(name, shape):
            return ctx.enter_context(nc.sbuf_tensor(t + name, shape, F32))

        self.nc, self.c, self.xnT, self.ring = nc, c, xnT, ring
        self.mv = sb("mv", [P, B, 2])
        self.var, self.rstd, self.shift = sb("var", [P, B]), sb("rstd", [P, B]), sb("shift", [P, B])
        self.stats_done, self.mv_done, self.var_ready = c.sem(t + "stats_done"), c.sem(t + "mv_done"), c.sem(t + "var_ready")
        self.rstd_ready = c.sem(t + "rstd_ready")
        self.shift_ready = c.sem(t + "shift_ready")
        self.even_ready, self.odd_ready = c.sem(t + "even_ready"), c.sem(t + "odd_ready")
        self.full = c.sem(t + "xnT_full")
        self.high, self.low = c.sem(t + "xnT_high"), c.sem(t + "xnT_low")

    def turned(self, b):
        return self.c.bank[b % 4][:, :].rearrange("p (k t) -> p k t", k=KC)

    def stats_on_vector(self, dve, x_loaded=None):
        nc, c = self.nc, self.c
        for half in range(2):
            part = slice(half * HB, (half + 1) * HB)
            if x_loaded:
                dve.wait_ge(x_loaded[half], 16)
                for b in range(half * HB, (half + 1) * HB):
                    nc.vector.bn_stats(c.stats[:, b, :], c.x[:, b, :]).then_inc(self.stats_done, 1)
                if half == 1:
                    self.shift_on_vector(dve, 0)
                dve.wait_ge(self.stats_done, (half + 1) * HB)
            for b in range(half * HB, (half + 1) * HB):
                nc.vector.bn_aggr(self.mv[:, b, :], c.stats[:, b, :]).then_inc(self.mv_done, 1)
            dve.wait_ge(self.mv_done, (half + 1) * HB)
            nc.vector.tensor_scalar(self.var[:, part], self.mv[:, part, 1], EPS, None, ALU.add).then_inc(self.var_ready, 1)
        if not x_loaded:
            self.shift_on_vector(dve, 0)
        self.shift_on_vector(dve, 1)

    def shift_on_vector(self, dve, half):
        part = slice(half * HB, (half + 1) * HB)
        dve.wait_ge(self.rstd_ready, half + 1)
        self.nc.vector.scalar_tensor_tensor(self.shift[:, part], self.mv[:, part, 0], -1.0, self.rstd[:, part],
                                            ALU.mult, ALU.mult).then_inc(self.shift_ready, 1)

    def parts_on_vector(self, dve, between=None):
        nc = self.nc

        def normalised(b):
            if b >= 3:
                dve.wait_ge(self.full, b - 2)
            nc.vector.tensor_scalar(self.ring[b % 3], self.c.x[:, b, :], self.mv[:, b, 0:1], self.rstd[:, b:b + 1],
                                    ALU.subtract, ALU.mult).then_inc(self.odd_ready, 1)

        normalised(1)
        for b in range(B):
            if b % 2 == 1 and b + 2 < B:
                normalised(b + 2)
            dve.wait_ge(self.high, b + 1)
            nc.vector.tensor_tensor(self.xnT[1][:, :, b * P:(b + 1) * P], self.turned(b), fp(self.xnT[0][:, :, b * P:(b + 1) * P]),
                                    ALU.subtract).then_inc(self.low, 1)
            if between and b == 1:
                between()

    def on_scalar(self, act, between=None):
        nc = self.nc

        def normalised(b):
            act.wait_ge(self.shift_ready, b // HB + 1)
            if b >= 3:
                act.wait_ge(self.full, b - 2)
            nc.scalar.activation(self.ring[b % 3], self.c.x[:, b, :], ACT.Identity, scale=self.rstd[:, b:b + 1],
                                 bias=self.shift[:, b:b + 1]).then_inc(self.even_ready, 1)

        normalised(0)
        for b in range(B):
            if b % 2 == 0 and b + 2 < B:
                normalised(b + 2)
            act.wait_ge(self.full, b + 1)
            nc.scalar.copy(self.xnT[0][:, :, b * P:(b + 1) * P], self.turned(b)).then_inc(self.high, 1)
            if between and b == 3:
                between()

    def on_gpsimd(self, pool):
        for half in range(2):
            part = slice(half * HB, (half + 1) * HB)
            pool.wait_ge(self.var_ready, half + 1)
            self.nc.gpsimd.tensor_tensor(self.rstd[:, part], self.var[:, part], self.c.minus_half[:, 0:HB], ALU.pow).then_inc(self.rstd_ready, 1)

    def on_tensor(self, pe):
        for b in range(B):
            pe.wait_ge(self.odd_ready if b % 2 else self.even_ready, b // 2 + 1)
            if b >= 4:
                pe.wait_ge(self.low, b - 3)
            for k in range(KC):
                ins = self.nc.tensor.transpose(self.c.bank[b % 4][:, k * P:(k + 1) * P], self.ring[b % 3][:, k * P:(k + 1) * P],
                                               self.c.ident)
            ins.then_inc(self.full, 1)


def store_output(nc, c, d):
    with ExitStack() as ctx:
        stored = c.sem("out_stored")
        block = ctx.enter_context(nc.Block())

        @block.sync
        def _(sp):
            sp.dma_start(d["out"].rearrange("b p n -> p b n"), c.x[:, :, :]).then_inc(stored, 16)
            sp.wait_ge(stored, 16)


IDENT, MASK16, MASKM, MASKG, BLOCK4, IOTA, TRI, RECK = 0, 128, 136, 140, 144, 272, 280, 344
CONSTS = 352


def constants():
    p = np.arange(P)
    a = np.zeros((P, CONSTS), np.float32)
    a[:, IDENT:IDENT + P] = np.eye(P)
    a[:, MASK16:MASK16 + 8] = p[:, None] // 16 == np.arange(8)
    a[:, MASKM:MASKM + 4] = p[:, None] % 4 == np.arange(4)
    a[:, MASKG:MASKG + 4] = p[:, None] // 32 == np.arange(4)
    a[:, BLOCK4:BLOCK4 + P] = p[:, None] // 4 == p // 4
    a[:, IOTA:IOTA + 8] = np.arange(8)
    a[:, TRI:TRI + 64] = np.tril(np.ones((8, 8))).reshape(-1)
    a[:, RECK:RECK + 8] = 1.0 / np.arange(1, 9)
    return a



class Place:

    def __init__(self, base, names):
        self.base, self.names = base, names

    def __call__(self, name):
        return self.base + self.names.index(name)


class Tiles:

    def __init__(self, banks, ahead, body, g, first=False, last=False, carried=(), tail=()):
        self.banks, self.ahead, self.body, self.carried = banks, ahead, body, carried
        self.g, self.first = g, first
        self.names = body
        if g is None:
            self.names = ahead
        if first:
            self.names = [x for x in body if x not in carried]
        if last:
            self.names = [x for x in body if x not in ahead] + list(tail)
        self.tile = self.place(lambda name: True)

    def counts(self, kind):
        names, ahead, body, carried = ([x for x in y if kind(x)] for y in (self.names, self.ahead, self.body, self.carried))
        return names, len(body), 0 if self.g is None else len(ahead) if self.first else len(ahead) - len(carried)

    def place(self, kind):
        names, each, base = self.counts(kind)
        return Place(base if self.g is None else self.g * each + base, names)

    def slot(self, name, ring, kind=lambda name: True):
        names, each, base = self.counts(kind)
        assert each % ring == 0
        return (base + names.index(name)) % ring

    def bank(self, name):
        return self.banks[self.slot(name, len(self.banks))]


def small_head_attention(nc, c, d, layer):
    own_kv = layer == 1
    SG = 4 if own_kv else 2
    HEADS = 4 * SG
    DV = P // HEADS
    VW = 3 * DV + 1
    MASKS = 4 if own_kv else 8
    SCALE = (8 if own_kv else 16) ** -0.5
    N = B * SG
    NORM_LAG, TURN_LAG, OUT_LAG = (5, 6, 8) if own_kv else (4, 6, 8)
    TICKS = N + OUT_LAG + 1
    t = f"a{layer}_"
    with ExitStack() as ctx:
        def sb(name, shape, dt=F32):
            return ctx.enter_context(nc.sbuf_tensor(t + name, shape, dt))

        def pair(name, shape, dt=F32R):
            return sb(name + "_hi", shape, dt), sb(name + "_lo", shape, dt)

        def sem(name):
            return c.sem(t + name)

        xnT = pair("xnT", [P, KC, TOK])
        if not own_kv:
            with nc.sbuf_tensor(t + "ctx_raw", [P, KC, TOK], F32) as ctx_raw:
                pass
        kTm = pair("kTm", [P, MASKS, TOK])
        qT = pair("qT", [P, 4 if own_kv else 1, TOK])
        wq, wk, wv, wo = pair("wq", [P, KC, P]), pair("wk", [P, KC, P]), pair("wv", [P, KC, P]), pair("wo", [P, D])
        if own_kv:
            temp = pair("temp", [P, 2, HALF])
        if own_kv:
            bias_o = sb("bias_o", [P, 1])
            out_bias = sb("out_bias", [P, D])
            wo_raw = sb("wo_raw", [P, D])
            w_nat = sb("w_nat", [P, 3, D])
            inter_raw, inter = sb("inter_raw", [P, KC, 4]), sb("inter", [P, KC, 4])
            amp = sb("amp", [P, 1])
            bias_raw, bias = sb("bias_raw", [P, KC, 3]), sb("bias", [P, 3])
            fold = sb("fold", [P, P])
        else:
            wkv_raw = sb("wkv_raw", [P, 2 * KC, P])
            temp = qT[0], qT[1]
            wq_raw, wo_raw = wkv_raw[:, 0:KC, :], wkv_raw[:, KC:2 * KC, :].rearrange("p k n -> p (k n)")
        v_aug = sb("v_aug", [P, B, HEADS, VW], BF16)
        v_rest = sb("v_rest", [P, B, P])
        minus_max = sb("minus_max", [P, 4, 4])
        prob = sb("prob", [P, 4, HALF])
        pT = pair("pT", [P, 2, HALF], F16)
        o_raw, o_inv, o_sb = sb("o_raw", [P, 2, P]), sb("o_inv", [P, 2, HEADS]), sb("o_sb", [P, 2, P])
        oT = pair("oT", [P, 2, P])

        once_loaded = sem("once_loaded")
        wq_loaded = sem("wq_loaded")
        wo_loaded = sem("wo_loaded")
        split_high = sem("split_high")
        kv_split = sem("kv_split")
        wq_split, wo_split = sem("wq_split"), sem("wo_split")
        ones_set = sem("ones_set")
        inter_ready = sem("inter_ready")
        fold_step, folded = sem("fold_step"), sem("folded")
        bias_scaled = sem("bias_scaled")
        m_full = sem("m_full")
        m_high = sem("m_high")
        m_free = sem("m_free")
        bias_taken = sem("bias_taken")
        mask_high, mask_low = sem("mask_high"), sem("mask_low")
        masking = sem("masking")
        masked = sem("masked")
        v2_ready, v3_ready = sem("v2_ready"), sem("v3_ready")
        s_full = sem("s_full")
        max_ready = sem("max_ready")
        p_ready = sem("p_ready")
        pT_full = sem("pT_full")
        pT_high = sem("pT_high")
        pT_low = sem("pT_low")
        pv_done = sem("pv_done")
        o_step = sem("o_step")
        o_free = sem("o_free")

        S, PT, OB, M = c.bank[0:2], c.bank[2:4], c.bank[4:6], c.bank[6:8]

        def ends(n):
            return n % SG == SG - 1

        def under_way(n, g):
            return n < N and (n >= 0 or g is not FIRST)

        def name_of(kind, b):
            return f"{kind}{b}" if b >= 0 else f"{kind}{b + B} before"

        if own_kv:
            early_at = {17: ["fq"], 18: ["fk"], 19: ["fv"], 20: ["fb"], 21: ["q0"], 24: ["k0"], 28: ["v0"]}
            late_at = {0: ["q1"], 2: ["k1"], 4: ["v1"]}
        else:
            early_at, late_at = {10: ["q0"]}, {0: ["q1"]}
        FOLD_AT, BIAS_AT = 16, 7
        once = [] if own_kv else ["k0", "k1", "v0", "v1"]
        early = [x for n in sorted(early_at) for x in early_at[n]]
        body, tail = [], []
        for n in range(TICKS):
            for kind, lag in (("t", TURN_LAG), ("o", OUT_LAG)):
                if n < N and ends(n - lag):
                    body.append(name_of(kind, (n - lag) // SG))
                if n >= N and n - lag < N and ends(n - lag):
                    tail.append(name_of(kind, (n - lag) // SG))
            body += late_at.get(n, []) + early_at.get(n, [])
        carried = [x for x in body if x.endswith("before")]
        FIRST = 0

        class Turn(Tiles):
            def __init__(self, g, first=False, last=False):
                super().__init__(M, once + early, body, g, first, last, carried, tail)
                self.high = self.place(lambda x: x[0] != "o" and x != "fb")
                self.masks = self.place(lambda x: x[0] in "qk")

        def passes(eng, one):
            one(FIRST, Turn(0, first=True), Turn(None), True)
            one(1, Turn(1), Turn(0, first=True), True)
            with eng.Fori(2, KC - 1) as g:
                one(g, Turn(g), Turn(g - 1), True)
            one(KC - 1, Turn(KC - 1, last=True), Turn(KC - 2), False)

        x_loaded = [sem("x0_loaded"), sem("x1_loaded")]
        consts_loaded, ctx_loaded = sem("consts_loaded"), sem("ctx_loaded")
        constants_set = sem("constants_set")
        ctx_high, ctx_low = sem("ctx_high"), sem("ctx_low")
        bias_loaded, bias_added = sem("bias_loaded"), sem("bias_added")
        norm = NormTransposed(nc, c, t + "norm_", ctx, xnT, [prob[:, i, :] for i in range(3)])
        block = ctx.enter_context(nc.Block())

        @block.sync
        def _(sp):
            def load_wq(g):
                if own_kv:
                    sp.dma_start(w_nat[:, :, :], d["L1_wqkv"][bass.ds(g, 1)].rearrange("a p w n -> (a p) w n")).then_inc(wq_loaded, 16)
                else:
                    sp.dma_start(wq_raw, d["L0_wq"][bass.ds(g, 1)].rearrange("a p k n -> (a p) k n")).then_inc(wq_loaded, 16)

            def load_wo(g):
                sp.dma_start(wo_raw[:, :], d[f"L{layer}_wo"][bass.ds(g, 1)].rearrange("a p n -> (a p) n")).then_inc(wo_loaded, 16)

            if own_kv:
                sp.dma_start(inter_raw[:, :, :], d["L1_inter"]).then_inc(once_loaded, 16)
                sp.dma_start(amp[:, :], d["L1_amp"]).then_inc(once_loaded, 16)
                sp.dma_start(bias_raw[:, :, :], d["L1_bias"]).then_inc(once_loaded, 16)
                sp.dma_start(out_bias[:, :], d["L1_bo"].partition_broadcast(P).rearrange("p a n -> p (a n)")).then_inc(bias_loaded, 16)
            else:
                for half in range(2):
                    part = slice(half * HB, (half + 1) * HB)
                    sp.dma_start(c.x[:, part, :], d["x"][part].rearrange("b p n -> p b n")).then_inc(x_loaded[half], 16)
                sp.dma_start(c.consts[:, :], d["consts"]).then_inc(consts_loaded, 16)
                sp.dma_start(wkv_raw[:, :, :], d["L0_wkv"]).then_inc(once_loaded, 16)
                for k in range(KC):
                    sp.dma_start(ctx_raw[:, k, :], d["ctxT"][:, k, :]).then_inc(ctx_loaded, 16)
                sp.wait_ge(kv_split, 1)
            load_wq(0)
            if not own_kv:
                sp.wait_ge(kv_split, 2)
            load_wo(0)

            def load_next(g, turn):
                if own_kv:
                    sp.wait_ge(m_free, turn.tile("fb") + 3)
                else:
                    sp.wait_ge(wq_split, g)
                load_wq(g)
                sp.wait_ge(wo_split, g)
                load_wo(g)

            load_next(1, Turn(None))
            load_next(2, Turn(0, first=True))
            with sp.Fori(3, KC) as g:
                load_next(g, Turn(g - 2))

        @block.gpsimd
        def _(pool):
            def split(raw, parts, highs, done):
                one = c.ones[:, 0:1].broadcast_to([P, raw.shape[1]]) if raw.ndim == 2 else \
                    c.ones[:, 0:1].unsqueeze(2).broadcast_to([P, raw.shape[1], raw.shape[2]])
                nc.gpsimd.tensor_tensor(parts[0], raw, one, ALU.mult).then_inc(split_high, 1)
                pool.wait_ge(split_high, highs + 1)
                nc.gpsimd.tensor_tensor(parts[1], raw, fp(parts[0]), ALU.subtract).then_inc(done, 1)

            def value_parts(g, turn, half):
                pool.wait_ge(m_free, turn.tile(f"v{half}") + 3)
                for u in range(HB):
                    b = half * HB + u
                    rest = v_rest[:, b, :].rearrange("p (h e) -> p h e", h=HEADS)
                    one = c.ones[:, 0:1].unsqueeze(2).broadcast_to([P, HEADS, DV])
                    nc.gpsimd.tensor_tensor(v_aug[:, b, :, DV:2 * DV], rest, one, ALU.mult).then_inc(v2_ready, 1)
                for u in range(HB):
                    b = half * HB + u
                    rest = v_rest[:, b, :].rearrange("p (h e) -> p h e", h=HEADS)
                    pool.wait_ge(v2_ready, (g if own_kv else 0) * B + (b + 1))
                    nc.gpsimd.tensor_tensor(v_aug[:, b, :, 2 * DV:3 * DV], rest, v_aug[:, b, :, DV:2 * DV],
                                            ALU.subtract).then_inc(v3_ready, 1)

            def masked_copies(g, turn, name, items):
                out, masks = (qT, MASKG) if name[0] == "q" else (kTm, MASKM)
                r, cols = int(name[0] == "k"), slice(int(name[1]) * HALF, (int(name[1]) + 1) * HALF)
                pool.wait_ge(m_free, turn.tile(name) + 3)
                pool.wait_ge(s_full, items)
                each = c.consts[:, masks:masks + 4].unsqueeze(2).broadcast_to([P, 4, HALF])
                for part, done in ((0, masking), (1, masked)):
                    nc.gpsimd.tensor_tensor(out[part][:, :, cols], fp(temp[part][:, r, :]).unsqueeze(1).broadcast_to([P, 4, HALF]), each,
                                            ALU.mult).then_inc(done, 1)

            def whole(w):
                return [x[:, :, :] for x in w]

            def split_wo(g, turn, highs):
                pool.wait_ge(wo_loaded, g * 16 + 16)
                if g is not FIRST:
                    pool.wait_ge(m_free, turn.tile(name_of("o", -1)) + 3)
                split(wo_raw[:, :], [x[:, :] for x in wo], highs, wo_split)

            def one_pass(g, turn, before, more):
                if own_kv:
                    masked_copies(g, turn, "q1", g * N + 1)
                    split_wo(g, turn, g)
                    masked_copies(g, turn, "k1", g * N + 1)
                    value_parts(g, turn, 1)
                    if more:
                        masked_copies(g + 1, turn, "q0", g * N + N // 2)
                        masked_copies(g + 1, turn, "k0", g * N + N // 2)
                        value_parts(g + 1, turn, 0)
                else:
                    if more:
                        pool.wait_ge(wq_loaded, g * 16 + 32)
                        pool.wait_ge(m_free, turn.tile("q1") + 3)
                        split(wq_raw, whole(wq), g * 2 + 3, wq_split)
                    split_wo(g, turn, g * 2 + (4 if more else 3))

            if not own_kv:
                nc.gpsimd.memset(c.minus_half[:, :], -0.5).then_inc(constants_set, 1)
                nc.gpsimd.memset(c.ones[:, :], 1.0).then_inc(constants_set, 1)
                pool.wait_ge(constants_set, 2)
            nc.gpsimd.memset(v_aug[:, :, :, VW - 1:VW], 1.0).then_inc(ones_set, 1)
            norm.on_gpsimd(pool)
            pool.sem_inc(masked, 4)
            if own_kv:
                value_parts(0, Turn(None), 0)
                pool.wait_ge(bias_loaded, 16)
                pool.wait_ge(norm.low, B)
                for b in range(B):
                    nc.gpsimd.tensor_tensor(c.x[:, b, :], c.x[:, b, :], out_bias[:, :], ALU.add).then_inc(bias_added, 1)
            else:
                pool.wait_ge(once_loaded, 16)
                split(wkv_raw[:, 0:KC, :], whole(wk), 0, kv_split)
                split(wkv_raw[:, KC:2 * KC, :], whole(wv), 1, kv_split)
                pool.wait_ge(wq_loaded, 16)
                split(wq_raw, whole(wq), 2, wq_split)
                value_parts(0, Turn(None), 0)
                value_parts(0, Turn(None), 1)
            passes(pool, one_pass)

        @block.tensor
        def _(pe):
            def take(turn, name):
                pe.wait_ge(m_free, turn.tile(name) + 1)
                return turn.bank(name)

            def tile(g, turn, name):
                if name in ("fq", "fk", "fv"):
                    nth = ("fq", "fk", "fv").index(name)
                    if nth == 0:
                        pe.wait_ge(folded, g + 1)
                        pe.wait_ge(wq_loaded, g * 16 + 16)
                    bank = take(turn, name)
                    for k in range(KC):
                        ins = nc.tensor.matmul(bank[:, k * P:(k + 1) * P], w_nat[:, nth, k * P:(k + 1) * P], fold[:, :],
                                               start=True, stop=True)
                elif name == "fb":
                    bank = take(turn, name)
                    pe.wait_ge(once_loaded, 48)
                    ins = nc.tensor.matmul(bank[:, 0:3], fold[:, :], bias_raw[:, bass.ds(g, 1), :].rearrange("p a n -> p (a n)"),
                                           start=True, stop=True)
                elif name[0] in "qk":
                    w, rhs, half = (wq, xnT, int(name[1])) if name[0] == "q" else (wk, c.ctxT, int(name[1]))
                    if name[0] == "q":
                        pe.wait_ge(norm.low, B)
                    if own_kv and half == 0:
                        pe.wait_ge(m_free, turn.tile("f" + name[0]) + 3)
                    elif name == "q0":
                        pe.wait_ge(wq_split, g + 1)
                    elif name == "k0":
                        pe.wait_ge(kv_split, 1)
                    bank = take(turn, name)
                    for k in range(KC):
                        if name == "k0" and not own_kv:
                            pe.wait_ge(ctx_low, k + 1)
                        ins = split_passes(nc, bank[:, :], [x[:, k, :] for x in w],
                                           [x[:, k, half * HALF:(half + 1) * HALF] for x in rhs], k == 0, k == KC - 1)
                else:
                    half = int(name[1])
                    if own_kv and half == 0:
                        pe.wait_ge(m_free, turn.tile("fv") + 3)
                    elif half == 0:
                        pe.wait_ge(kv_split, 2)
                    bank = take(turn, name)
                    for u in range(HB):
                        cols = slice((half * HB + u) * P, (half * HB + u + 1) * P)
                        for k in range(KC):
                            ins = split_passes(nc, bank[:, u * P:(u + 1) * P], [x[:, k, cols] for x in c.ctxT],
                                               [x[:, k, :] for x in wv], k == 0, k == KC - 1)
                ins.then_inc(m_full, 1)

            def items(g, turn, before, more):
                for n in range(N if more else TICKS):
                    if n < N:
                        b, s = n // SG, n % SG
                        if n in (0, N // 2):
                            half = n // (N // 2)
                            if g is FIRST and half == 0:
                                pe.wait_ge(mask_high, 2)
                                pe.wait_ge(mask_low, 2)
                            if own_kv:
                                pe.wait_ge(masked, g * 4 + (2 * half + 4))
                            elif half == 0:
                                pe.wait_ge(m_free, before.tile("q0") + 3)
                            else:
                                pe.wait_ge(m_free, turn.tile("q1") + 3)
                        pe.wait_ge(p_ready, g * N + (n + 1))
                        tok = slice(b * P, (b + 1) * P)
                        keys_of = slice(0, 4) if own_kv else slice(4 * s, 4 * s + 4)
                        split_passes(nc, S[n % 2][:, :].rearrange("p (a t) -> p a t", a=4),
                                     [x[:, s if own_kv else 0, tok] for x in qT], [x[:, keys_of, tok] for x in kTm],
                                     True, True).then_inc(s_full, 1)
                    if under_way(n - 2, g):
                        i = n - 2
                        pe.wait_ge(p_ready, g * N + (i + 3))
                        pe.wait_ge(pT_low, g * N + (i + 1))
                        for h in range(4):
                            ins = nc.tensor.transpose(PT[i % 2][:, h * P:(h + 1) * P], prob[:, i % 4, h * P:(h + 1) * P], c.ident)
                        ins.then_inc(pT_full, 1)
                    if under_way(n - 3, g):
                        i = n - 3
                        b, s = i // SG, i % SG
                        pe.wait_ge(pT_low, g * N + (i + 3))
                        if s == 0:
                            pe.wait_ge(o_free, g * B + (b + 1))
                        if i == 0:
                            pe.wait_ge(ones_set, 1)
                        if i in (0, N // 2):
                            half = i // (N // 2)
                            pe.wait_ge(v3_ready, g * B + (half + 1) * HB if own_kv else B)
                        for h in range(4):
                            head = 4 * s + h
                            out = OB[b % 2][:, head * VW:(head + 1) * VW]
                            nc.tensor.matmul(out, pT[0][:, i % 2, h * P:(h + 1) * P], v_aug[:, b % B, head, :], start=True, stop=False)
                            ins = nc.tensor.matmul(out, pT[1][:, i % 2, h * P:(h + 1) * P], v_aug[:, b % B, head, :],
                                                   start=False, stop=True)
                        ins.then_inc(pv_done, 1)
                    if under_way(n - TURN_LAG, g) and ends(n - TURN_LAG):
                        b = (n - TURN_LAG) // SG
                        bank = take(turn, name_of("t", b))
                        pe.wait_ge(o_free, g * B + (b + 3))
                        nc.tensor.transpose(bank[:, 0:P], o_sb[:, b % 2, :], c.ident).then_inc(m_full, 1)
                    if under_way(n - OUT_LAG, g) and ends(n - OUT_LAG):
                        b = (n - OUT_LAG) // SG
                        bank = take(turn, name_of("o", b))
                        if b == 0:
                            pe.wait_ge(wo_split, g + 1)
                        turned = name_of("t", b)
                        pe.wait_ge(m_free, (turn.tile(turned) if turned in turn.names else before.tile(f"t{b % B}")) + 3)
                        split_passes(nc, bank[:, :], [x[:, b % 2, :] for x in oT], [x[:, :] for x in wo],
                                     True, True).then_inc(m_full, 1)
                    for name in late_at.get(n, []):
                        tile(g, turn, name)
                    if more:
                        for name in early_at.get(n, []):
                            tile(g + 1, turn, name)

            if not own_kv:
                pe.wait_ge(consts_loaded, 16)
            norm.on_tensor(pe)
            for name in once + early:
                tile(0, Turn(None), name)
            passes(pe, items)

        @block.scalar
        def _(act):
            def once_keys(name):
                half = int(name[1])
                cols = slice(half * HALF, (half + 1) * HALF)
                act.wait_ge(m_full, Turn(None).tile(name) + 1)
                nc.scalar.copy(temp[0][:, 0, cols], Turn(None).bank(name)[:, :]).then_inc(m_high, 1)
                act.wait_ge(m_high, half + 1)
                for m in range(MASKS):
                    ins = nc.scalar.activation(kTm[0][:, m, half * HALF:(half + 1) * HALF], fp(temp[0][:, 0, cols]), ACT.Copy,
                                               scale=c.consts[:, MASK16 + m:MASK16 + m + 1])
                ins.then_inc(mask_high, 1)

            def tile(g, turn, name):
                bank = turn.bank(name)
                if name == "fb":
                    return
                act.wait_ge(m_full, turn.tile(name) + 1)
                if name[0] == "f":
                    w = {"fq": wq, "fk": wk, "fv": wv}[name]
                    nc.scalar.activation(w[0][:, :, :], bank[:, :].rearrange("p (k n) -> p k n", k=KC), ACT.Copy,
                                         scale=SCALE if name == "fq" else 1.0).then_inc(m_high, 1)
                elif name[0] in "qk" and own_kv:
                    if name == "q0":
                        act.wait_ge(m_free, turn.tile("fb") + 3)
                        act.wait_ge(bias_scaled, g + 1)
                    act.wait_ge(masked, turn.masks(name) + 1)
                    col = "qk".index(name[0])
                    nc.scalar.activation(temp[0][:, col, :], bank[:, :], ACT.Identity, bias=bias[:, col:col + 1]).then_inc(m_high, 1)
                elif name[0] == "q":
                    half = int(name[1])
                    nc.scalar.activation(qT[0][:, 0, half * HALF:(half + 1) * HALF], bank[:, :], ACT.Copy, scale=SCALE).then_inc(m_high, 1)
                else:
                    for u in range(HB):
                        src = bank[:, u * P:(u + 1) * P]
                        out = v_aug[:, int(name[1]) * HB + u, :, 0:DV]
                        if own_kv:
                            src = src.rearrange("p (h e m) -> p h m e", h=4, m=4)
                            out = out.rearrange("p (h m) e -> p h m e", h=4)
                        else:
                            src = src.rearrange("p (h e) -> p h e", h=HEADS)
                        ins = nc.scalar.copy(out, src)
                    ins.then_inc(m_high, 1)

            def items(g, turn, before, more):
                for n in range(N if more else TICKS):
                    if under_way(n - 2, g):
                        act.wait_ge(pT_full, g * N + (n - 1))
                        nc.scalar.copy(pT[0][:, n % 2, :], PT[n % 2][:, :]).then_inc(pT_high, 1)
                    if n < N:
                        act.wait_ge(max_ready, g * N + (n + 1))
                        for h in range(4):
                            ins = nc.scalar.activation(prob[:, n % 4, h * P:(h + 1) * P], S[n % 2][:, h * P:(h + 1) * P], ACT.Exp,
                                                       bias=minus_max[:, n % 4, h:h + 1])
                        ins.then_inc(p_ready, 1)
                    if under_way(n - TURN_LAG, g) and ends(n - TURN_LAG):
                        b = (n - TURN_LAG) // SG
                        act.wait_ge(m_full, turn.tile(name_of("t", b)) + 1)
                        src = turn.bank(name_of("t", b))[:, 0:P]
                        if own_kv:
                            act.wait_ge(bias_taken, g + (1 if b >= 0 else 0))
                            nc.scalar.activation(oT[0][:, b % 2, :], src, ACT.Identity, bias=bias_o[:, 0:1]).then_inc(m_high, 1)
                        else:
                            nc.scalar.copy(oT[0][:, b % 2, :], src).then_inc(m_high, 1)
                    for name in late_at.get(n, []):
                        tile(g, turn, name)
                    if more:
                        for name in early_at.get(n, []):
                            tile(g + 1, turn, name)

            def first_copies(name):
                out, masks = (qT, MASKG) if name[0] == "q" else (kTm, MASKM)
                act.wait_ge(m_high, Turn(None).high(name) + 1)
                for m in range(4):
                    ins = nc.scalar.activation(out[0][:, m, 0:HALF], fp(temp[0][:, "qk".index(name[0]), :]), ACT.Copy,
                                               scale=c.consts[:, masks + m:masks + m + 1])
                ins.then_inc(mask_high, 1)

            act.sem_inc(p_ready, 2)
            norm.on_scalar(act)
            if not own_kv:
                act.wait_ge(ctx_loaded, 16 * KC)
                for k in range(KC):
                    nc.scalar.copy(c.ctxT[0][:, k, :], ctx_raw[:, k, :]).then_inc(ctx_high, 1)
                act.wait_ge(consts_loaded, 16)
            for name in once + early:
                if name in once and name[0] == "k":
                    once_keys(name)
                else:
                    tile(0, Turn(None), name)
                    if own_kv and name[0] in "qk":
                        first_copies(name)
            passes(act, items)

        @block.vector
        def _(dve):
            def once_keys(name):
                half = int(name[1])
                cols = slice(half * HALF, (half + 1) * HALF)
                dve.wait_ge(m_high, half + 1)
                nc.vector.tensor_tensor(temp[1][:, 0, cols], Turn(None).bank(name)[:, :], fp(temp[0][:, 0, cols]), ALU.subtract).then_inc(m_free, 1)
                dve.wait_ge(m_free, Turn(None).tile(name) + 3)
                for m in range(MASKS):
                    ins = nc.vector.tensor_scalar(kTm[1][:, m, half * HALF:(half + 1) * HALF], fp(temp[1][:, 0, cols]),
                                                  c.consts[:, MASK16 + m:MASK16 + m + 1], None, ALU.mult)
                ins.then_inc(mask_low, 1)

            def interference(g):
                nc.vector.tensor_tensor(fold[:, :].rearrange("p (e j) -> p e j", j=4),
                                        c.consts[:, BLOCK4:BLOCK4 + P].rearrange("p (e j) -> p e j", j=4),
                                        inter[:, bass.ds(g, 1), :].broadcast_to([P, P // 4, 4]), ALU.mult).then_inc(fold_step, 1)
                dve.wait_ge(fold_step, g + 1)
                nc.vector.tensor_tensor(fold[:, :], fold[:, :], c.ident, ALU.add).then_inc(folded, 1)

            def tile(g, turn, name):
                bank = turn.bank(name)
                if name == "fb":
                    dve.wait_ge(m_full, turn.tile(name) + 1)
                    nc.vector.tensor_scalar(bias[:, 0:1], bank[:, 0:1], SCALE, None, ALU.mult).then_inc(bias_scaled, 1)
                    nc.vector.tensor_copy(bias[:, 1:3], bank[:, 1:3]).then_inc(m_free, 1)
                    return
                dve.wait_ge(m_high, turn.high(name) + 1)
                if name[0] == "f":
                    w = {"fq": wq, "fk": wk, "fv": wv}[name]
                    nc.vector.scalar_tensor_tensor(w[1][:, :, :], bank[:, :].rearrange("p (k n) -> p k n", k=KC),
                                                   SCALE if name == "fq" else 1.0, fp(w[0][:, :, :]),
                                                   ALU.mult, ALU.subtract).then_inc(m_free, 1)
                elif name[0] in "qk" and own_kv:
                    col = "qk".index(name[0])
                    if name == "q0":
                        dve.wait_ge(m_free, turn.tile("fb") + 3)
                        dve.wait_ge(bias_scaled, g + 1)
                    nc.vector.scalar_tensor_tensor(temp[1][:, col, :], bank[:, :], bias[:, col:col + 1],
                                                   fp(temp[0][:, col, :]), ALU.add, ALU.subtract).then_inc(m_free, 1)
                elif name[0] == "q":
                    cols = slice(int(name[1]) * HALF, (int(name[1]) + 1) * HALF)
                    nc.vector.scalar_tensor_tensor(qT[1][:, 0, cols], bank[:, :], SCALE, fp(qT[0][:, 0, cols]),
                                                   ALU.mult, ALU.subtract).then_inc(m_free, 1)
                else:
                    for u in range(HB):
                        b = int(name[1]) * HB + u
                        src = bank[:, u * P:(u + 1) * P]
                        first, out = v_aug[:, b, :, 0:DV], v_rest[:, b, :]
                        if own_kv:
                            src = src.rearrange("p (h e m) -> p h m e", h=4, m=4)
                            first = first.rearrange("p (h m) e -> p h m e", h=4)
                            out = out.rearrange("p (h m e) -> p h m e", h=4, m=4)
                        else:
                            src = src.rearrange("p (h e) -> p h e", h=HEADS)
                            out = out.rearrange("p (h e) -> p h e", h=HEADS)
                        ins = nc.vector.tensor_tensor(out, src, first, ALU.subtract)
                    ins.then_inc(m_free, 1)

            def items(g, turn, before, more):
                late = []
                for n in range(N if more else TICKS):
                    if n < N:
                        dve.wait_ge(s_full, g * N + (n + 1))
                        scores = S[n % 2][:, :].rearrange("p (a t) -> p a t", a=4)
                        nc.vector.tensor_reduce(minus_max[:, n % 4, :], scores, AX.X, ALU.max, negate=True).then_inc(max_ready, 1)
                    for chunk, name in late:
                        tile(chunk, turn, name)
                    if own_kv and n == BIAS_AT:
                        if g is not FIRST:
                            dve.wait_ge(m_free, turn.tile(name_of("t", -1)) + 3)
                        nc.vector.tensor_copy(bias_o[:, 0:1], bias[:, 2:3]).then_inc(bias_taken, 1)
                    late = [(g, x) for x in late_at.get(n, [])]
                    if more:
                        if own_kv and n == FOLD_AT:
                            interference(g + 1)
                        late += [(g + 1, x) for x in early_at.get(n, [])]
                    if under_way(n - 2, g):
                        i = n - 2
                        dve.wait_ge(pT_high, g * N + (i + 1))
                        nc.vector.tensor_tensor(pT[1][:, i % 2, :], PT[i % 2][:, :], pT[0][:, i % 2, :], ALU.subtract).then_inc(pT_low, 1)
                    if under_way(n - NORM_LAG, g) and ends(n - NORM_LAG):
                        b = (n - NORM_LAG) // SG
                        r = b % 2
                        dve.wait_ge(pv_done, g * N + (n - NORM_LAG + 1))
                        sums = OB[r][:, 0:HEADS * VW].rearrange("p (h w) -> p h w", w=VW)
                        nc.vector.tensor_reduce(o_raw[:, r, :].rearrange("p (h e) -> p h e", h=HEADS),
                                                sums[:, :, 0:3 * DV].rearrange("p h (s e) -> p h e s", s=3), AX.X, ALU.add).then_inc(o_step, 1)
                        nc.vector.reciprocal(o_inv[:, r, :].unsqueeze(2), sums[:, :, 3 * DV:VW]).then_inc(o_step, 1)
                        dve.wait_ge(o_step, g * 2 * B + (2 * b + 2))
                        if own_kv:
                            out = o_sb[:, r, :].rearrange("p (h e m) -> p h m e", h=4, m=4)
                            raw = o_raw[:, r, :].rearrange("p (h m e) -> p h m e", h=4, m=4)
                            inv = o_inv[:, r, :].rearrange("p (h m) -> p h m", h=4).unsqueeze(3).broadcast_to([P, 4, 4, DV])
                        else:
                            out = o_sb[:, r, :].rearrange("p (h e) -> p h e", h=HEADS)
                            raw = o_raw[:, r, :].rearrange("p (h e) -> p h e", h=HEADS)
                            inv = o_inv[:, r, :].unsqueeze(2).broadcast_to([P, HEADS, DV])
                        nc.vector.tensor_tensor(out, raw, inv, ALU.mult).then_inc(o_free, 1)
                    if under_way(n - TURN_LAG, g) and ends(n - TURN_LAG):
                        b = (n - TURN_LAG) // SG
                        dve.wait_ge(m_high, turn.high(name_of("t", b)) + 1)
                        if own_kv and b >= 0:
                            dve.wait_ge(bias_taken, g + 1)
                        src, hi, lo = turn.bank(name_of("t", b))[:, 0:P], fp(oT[0][:, b % 2, :]), oT[1][:, b % 2, :]
                        if own_kv:
                            nc.vector.scalar_tensor_tensor(lo, src, bias_o[:, 0:1], hi, ALU.add, ALU.subtract).then_inc(m_free, 1)
                        else:
                            nc.vector.tensor_tensor(lo, src, hi, ALU.subtract).then_inc(m_free, 1)
                    if under_way(n - OUT_LAG, g) and ends(n - OUT_LAG):
                        b = (n - OUT_LAG) // SG
                        if own_kv:
                            dve.wait_ge(bias_added, B)
                        dve.wait_ge(m_full, turn.tile(name_of("o", b)) + 1)
                        nc.vector.tensor_tensor(c.x[:, b % B, :], turn.bank(name_of("o", b))[:, :], c.x[:, b % B, :], ALU.add).then_inc(m_free, 1)
                        if not more and b >= 0:
                            dve.wait_ge(m_free, turn.tile(name_of("o", b)) + 3)
                            take_stats(nc, c, b)

            dve.sem_inc(m_free, 2)
            dve.sem_inc(pT_low, 2)
            dve.sem_inc(o_free, 2)
            def first_copies(name):
                out, masks = (qT, MASKG) if name[0] == "q" else (kTm, MASKM)
                dve.wait_ge(m_free, Turn(None).tile(name) + 3)
                for m in range(4):
                    ins = nc.vector.tensor_scalar(out[1][:, m, 0:HALF], fp(temp[1][:, "qk".index(name[0]), :]),
                                                  c.consts[:, masks + m:masks + m + 1], None, ALU.mult)
                ins.then_inc(mask_low, 1)

            norm.stats_on_vector(dve, None if own_kv else x_loaded)
            if not own_kv:
                norm.parts_on_vector(dve)
                for k in range(KC):
                    dve.wait_ge(ctx_high, k + 1)
                    nc.vector.tensor_tensor(c.ctxT[1][:, k, :], ctx_raw[:, k, :], fp(c.ctxT[0][:, k, :]), ALU.subtract).then_inc(ctx_low, 1)
                dve.wait_ge(consts_loaded, 16)
            if own_kv:
                dve.wait_ge(once_loaded, 48)
                nc.vector.tensor_scalar(inter[:, :, :], inter_raw[:, :, :], amp[:, 0:1], 0.1, ALU.mult, ALU.mult).then_inc(inter_ready, 1)
                dve.wait_ge(inter_ready, 1)
                interference(0)
                norm.parts_on_vector(dve)
            for name in once + early:
                if name in once and name[0] == "k":
                    once_keys(name)
                else:
                    tile(0, Turn(None), name)
                    if own_kv and name[0] in "qk":
                        first_copies(name)
            passes(dve, items)

class Chain:

    def __init__(self, eng, sem, base):
        self.eng, self.sem, self.base, self.n = eng, sem, base, 0

    def __call__(self, ins):
        ins.then_inc(self.sem, 1)
        self.n += 1
        self.eng.wait_ge(self.sem, self.base + self.n)


def moe_ffn(nc, c, d, layer):
    W = HB
    base = layer != 3
    t = f"f{layer}_"
    NA = LR + EXPERTS
    STEPS = {0: 12, 1: 9, 3: 6}[layer]
    with ExitStack() as ctx:
        def sb(name, shape, dt=F32):
            return ctx.enter_context(nc.sbuf_tensor(t + name, shape, dt))

        def pair(name, shape, dt=F32R):
            return sb(name + "_hi", shape, dt), sb(name + "_lo", shape, dt)

        def sem(name):
            return c.sem(t + name)

        xnT = pair("xnT", [P, KC, TOK])
        ring = sb("ring", [P, 3, D])
        norm = NormTransposed(nc, c, t + "norm_", ctx, xnT, [ring[:, i, :] for i in range(3)])
        wa_raw, wb_raw = sb("wa_raw", [P, KC, NA]), sb("wb_raw", [P, D])
        wa, wb = pair("wa", [P, KC, NA]), pair("wb", [P, D])
        raws, parts = [wa_raw[:, :, :], wb_raw[:, :]], [[x[:, :, :] for x in wa], [x[:, :] for x in wb]]
        if base:
            w0_raw, w0 = sb("w0_raw", [P, KC, D]), pair("w0", [P, KC, D])
            raws.append(w0_raw[:, :, :])
            parts.append([x[:, :, :] for x in w0])
            bias = sb("bias", [P, D])
        router_bias = sb("router_bias", [P, EXPERTS])
        logits, top, comb = sb("logits", [P, W, EXPERTS]), sb("top", [P, W, EXPERTS]), sb("comb", [P, W, EXPERTS])
        index, index_f = sb("index", [P, W, EXPERTS], U32), sb("index_f", [P, W, EXPERTS])
        chosen = sb("chosen", [P, W, EXPERTS])
        cum_terms, cum = sb("cum_terms", [P, W, EXPERTS, EXPERTS]), sb("cum", [P, W, EXPERTS])
        small = sb("small", [P, 5, W])
        hs = sb("hs", [P, W, LR])
        hT = pair("hT", [P, W, P])

        w_loaded = [sem(f"w{i}_loaded") for i in range(len(raws))]
        bias_loaded = sem("bias_loaded")
        ab_high, ab_low = sem("ab_high"), sem("ab_low")
        w0_high, w0_low = sem("w0_high"), sem("w0_low")
        bias_added = sem("bias_added")
        h_full = sem("h_full")
        logits_done = sem("logits_done")
        step = sem("step")
        gap_ready, exp_ready = sem("gap_ready"), sem("exp_ready")
        hs_ready = sem("hs_ready")
        hT_full, hT_high, hT_low = sem("hT_full"), sem("hT_high"), sem("hT_low")
        out_full = sem("out_full")
        added = sem("added")

        block = ctx.enter_context(nc.Block())

        @block.sync
        def _(sp):
            sp.dma_start(wa_raw[:, :, :], d[f"L{layer}_wa"]).then_inc(w_loaded[0], 16)
            sp.dma_start(wb_raw[:, :], d[f"L{layer}_wb"]).then_inc(w_loaded[1], 16)
            if base:
                sp.dma_start(w0_raw[:, :, :], d[f"L{layer}_w0"]).then_inc(w_loaded[2], 16)
                sp.dma_start(bias[:, :], d[f"L{layer}_b0"].partition_broadcast(P).rearrange("p a n -> p (a n)")).then_inc(bias_loaded, 16)
            if layer == 1:
                sp.dma_start(router_bias[:, :], d["L1_br"].partition_broadcast(P).rearrange("p a n -> p (a n)")).then_inc(bias_loaded, 16)

        @block.gpsimd
        def _(pool):
            norm.on_gpsimd(pool)
            for i in range(2):
                pool.wait_ge(w_loaded[i], 16)
                one = c.ones[:, 0:1].unsqueeze(2).broadcast_to([P, KC, NA]) if i == 0 else c.ones[:, 0:1].broadcast_to([P, D])
                nc.gpsimd.tensor_tensor(parts[i][0], raws[i], one, ALU.mult).then_inc(ab_high, 1)
                pool.wait_ge(ab_high, i + 1)
                nc.gpsimd.tensor_tensor(parts[i][1], raws[i], fp(parts[i][0]), ALU.subtract).then_inc(ab_low, 1)
            if base:
                pool.wait_ge(bias_loaded, 32 if layer == 1 else 16)
                for b in range(B):
                    pool.wait_ge(norm.low, b + 1)
                    nc.gpsimd.tensor_tensor(c.x[:, b, :], c.x[:, b, :], bias[:, :], ALU.add).then_inc(bias_added, 1)

        @block.tensor
        def _(pe):
            norm.on_tensor(pe)
            for it in range(B // W):
                if it == 0:
                    pe.wait_ge(ab_low, 1)
                for u in range(W):
                    pe.wait_ge(norm.low, W + (u + 1))
                    if it:
                        pe.wait_ge(hT_low, u + 1)
                    tok = slice((it * W + u) * P, (it * W + u + 1) * P)
                    for k in range(KC):
                        ins = split_passes(nc, c.bank[u][:, 0:NA], [x[:, k, tok] for x in xnT], [x[:, k, :] for x in wa],
                                           k == 0, k == KC - 1)
                    ins.then_inc(h_full, 1)
                if base:
                    if it == 0:
                        pe.wait_ge(w0_low, 1)
                    for u in range(W):
                        if it:
                            pe.wait_ge(added, u + 1)
                        tok = slice((it * W + u) * P, (it * W + u + 1) * P)
                        for k in range(KC):
                            split_passes(nc, c.bank[4 + u][:, :], [x[:, k, tok] for x in xnT], [x[:, k, :] for x in w0],
                                         k == 0, False)
                for u in range(W):
                    pe.wait_ge(hs_ready, it * W + (u + 1))
                    nc.tensor.transpose(c.bank[u][:, 0:P], hs[:, u, :], c.ident).then_inc(hT_full, 1)
                if it == 0:
                    pe.wait_ge(ab_low, 2)
                for u in range(W):
                    if it and not base:
                        pe.wait_ge(added, u + 1)
                    pe.wait_ge(hT_low, it * W + (u + 1))
                    split_passes(nc, c.bank[4 + u][:, :], [x[:, u, :] for x in hT], [x[:, :] for x in wb],
                                 not base, True).then_inc(out_full, 1)

        @block.scalar
        def _(act):
            norm.on_scalar(act)
            if base:
                act.wait_ge(w_loaded[2], 16)
                nc.scalar.copy(parts[2][0], raws[2]).then_inc(w0_high, 1)
            for it in range(B // W):
                if layer == 0:
                    act.wait_ge(gap_ready, it + 1)
                    nc.scalar.activation(small[:, 1, :], small[:, 0, :], ACT.Exp).then_inc(exp_ready, 1)
                for u in range(W):
                    act.wait_ge(hT_full, it * W + (u + 1))
                    nc.scalar.copy(hT[0][:, u, :], c.bank[u][:, 0:P]).then_inc(hT_high, 1)

        @block.vector
        def _(dve):
            def each(x):
                return x.unsqueeze(2).broadcast_to([P, W, EXPERTS])

            def hot(i):
                return nc.vector.tensor_tensor(chosen[:, :, :], iota, each(index_f[:, :, i]), ALU.is_equal)

            iota = c.consts[:, IOTA:IOTA + EXPERTS].unsqueeze(1).broadcast_to([P, W, EXPERTS])
            norm.stats_on_vector(dve)
            norm.parts_on_vector(dve)
            if base:
                dve.wait_ge(w0_high, 1)
                nc.vector.tensor_tensor(parts[2][1], raws[2], fp(parts[2][0]), ALU.subtract).then_inc(w0_low, 1)
            if layer == 1:
                dve.wait_ge(bias_loaded, 32)
            for it in range(B // W):
                link = Chain(dve, step, it * STEPS)
                for u in range(W):
                    dve.wait_ge(h_full, it * W + (u + 1))
                    if layer == 1:
                        ins = nc.vector.tensor_tensor(logits[:, u, :], c.bank[u][:, LR:NA], router_bias[:, :], ALU.add)
                    else:
                        ins = nc.vector.tensor_copy(logits[:, u, :], c.bank[u][:, LR:NA])
                link(ins)
                for u in range(W):
                    ins = nc.vector.max(top[:, u, :], logits[:, u, :])
                link(ins)
                if layer == 1:
                    link(nc.vector.tensor_tensor(cum_terms[:, :, :, :], top[:, :, :].unsqueeze(2).broadcast_to([P, W, EXPERTS, EXPERTS]),
                                                 c.consts[:, TRI:TRI + 64].rearrange("p (k j) -> p k j", k=8).unsqueeze(1)
                                                 .broadcast_to([P, W, EXPERTS, EXPERTS]), ALU.mult))
                    link(nc.vector.tensor_reduce(cum[:, :, :], cum_terms[:, :, :, :], AX.X, ALU.add))
                    link(nc.vector.tensor_scalar(cum[:, :, :], cum[:, :, :], 1.0, None, ALU.subtract))
                    link(nc.vector.tensor_tensor(cum[:, :, :], cum[:, :, :], c.consts[:, RECK:RECK + 8].unsqueeze(1)
                                                 .broadcast_to([P, W, EXPERTS]), ALU.mult))
                    link(nc.vector.tensor_reduce(small[:, 0, :], cum[:, :, :], AX.X, ALU.max))
                    link(nc.vector.tensor_tensor(comb[:, :, :], logits[:, :, :], each(small[:, 0, :]), ALU.subtract))
                    link(nc.vector.tensor_scalar(comb[:, :, :], comb[:, :, :], 0.0, None, ALU.max))
                else:
                    for u in range(W):
                        ins = nc.vector.max_index(index[:, u, :], top[:, u, :], logits[:, u, :])
                    link(ins)
                    link(nc.vector.tensor_copy(index_f[:, :, :], index[:, :, :]))
                    if layer == 0:
                        nc.vector.tensor_tensor(small[:, 0, :], top[:, :, 1], top[:, :, 0], ALU.subtract).then_inc(gap_ready, 1)
                        link(hot(0))
                        dve.wait_ge(exp_ready, it + 1)
                        link(nc.vector.tensor_scalar(small[:, 2, :], small[:, 1, :], 1.0, 0.5, ALU.add, ALU.mult))
                        link(nc.vector.reciprocal(small[:, 3, :], small[:, 2, :]))
                        link(nc.vector.tensor_tensor(small[:, 4, :], small[:, 1, :], small[:, 3, :], ALU.mult))
                        link(nc.vector.tensor_tensor(comb[:, :, :], chosen[:, :, :], each(small[:, 3, :]), ALU.mult))
                        link(hot(1))
                        link(nc.vector.tensor_tensor(cum[:, :, :], chosen[:, :, :], each(small[:, 4, :]), ALU.mult))
                        link(nc.vector.tensor_tensor(comb[:, :, :], comb[:, :, :], cum[:, :, :], ALU.add))
                    else:
                        link(hot(0))
                        link(nc.vector.tensor_tensor(comb[:, :, :], chosen[:, :, :], each(top[:, :, 0]), ALU.mult))
                for u in range(W):
                    ins = nc.vector.tensor_tensor(hs[:, u, :].rearrange("p (e r) -> p e r", e=EXPERTS),
                                                  c.bank[u][:, 0:LR].rearrange("p (e r) -> p e r", e=EXPERTS),
                                                  comb[:, u, :].unsqueeze(2).broadcast_to([P, EXPERTS, RANK]), ALU.mult)
                    ins.then_inc(hs_ready, 1)
                for u in range(W):
                    dve.wait_ge(hT_high, it * W + (u + 1))
                    nc.vector.tensor_tensor(hT[1][:, u, :], c.bank[u][:, 0:P], fp(hT[0][:, u, :]), ALU.subtract).then_inc(hT_low, 1)
                for u in range(W):
                    dve.wait_ge(out_full, it * W + (u + 1))
                    if base:
                        dve.wait_ge(bias_added, it * W + (u + 1))
                    xb = c.x[:, it * W + u, :]
                    nc.vector.tensor_tensor(xb, c.bank[4 + u][:, :], xb, ALU.add).then_inc(added, 1)
                    if layer != 3:
                        dve.wait_ge(added, it * W + (u + 1))
                        take_stats(nc, c, it * W + u)
                assert link.n == STEPS, link.n


def context_attention(nc, c, d):
    W = HB
    t = "a2_"
    with ExitStack() as ctx:
        def sb(name, shape, dt=F32):
            return ctx.enter_context(nc.sbuf_tensor(t + name, shape, dt))

        def pair(name, shape, dt=F32R):
            return sb(name + "_hi", shape, dt), sb(name + "_lo", shape, dt)

        def sem(name):
            return c.sem(t + name)

        xnT = pair("xnT", [P, KC, TOK])
        ring = sb("ring", [P, 3, D])
        norm = NormTransposed(nc, c, t + "norm_", ctx, xnT, [ring[:, i, :] for i in range(3)])
        raw = sb("raw", [P, B, D])
        cx = pair("cx", [P, B, D])
        minus_max, sums, inv = sb("minus_max", [P, W]), sb("sums", [P, W]), sb("inv", [P, W])
        prob = sb("prob", [P, W, P])
        pT = pair("pT", [P, W, P])
        loaded = [sem(f"loaded{b}") for b in range(B)]
        cx_high, cx_low = sem("cx_high"), sem("cx_low")
        s_full, max_ready, p_ready, inv_ready = sem("s_full"), sem("max_ready"), sem("p_ready"), sem("inv_ready")
        pT_full, pT_high, pT_low = sem("pT_full"), sem("pT_high"), sem("pT_low")
        out_full, added = sem("out_full"), sem("added")
        block = ctx.enter_context(nc.Block())

        @block.sync
        def _(sp):
            for b in range(B):
                sp.dma_start(raw[:, b, :], d["ctx"][b]).then_inc(loaded[b], 16)

        @block.gpsimd
        def _(pool):
            norm.on_gpsimd(pool)
            for b in range(B):
                pool.wait_ge(loaded[b], 16)
                nc.gpsimd.tensor_tensor(cx[0][:, b, :], raw[:, b, :], c.ones[:, 0:1].broadcast_to([P, D]), ALU.mult).then_inc(cx_high, 1)
                pool.wait_ge(cx_high, b + 1)
                nc.gpsimd.tensor_tensor(cx[1][:, b, :], raw[:, b, :], fp(cx[0][:, b, :]), ALU.subtract).then_inc(cx_low, 1)

        @block.tensor
        def _(pe):
            norm.on_tensor(pe)
            for it in range(B // W):
                for u in range(W):
                    pe.wait_ge(norm.low, it * W + (u + 1))
                    if it:
                        pe.wait_ge(pT_low, u + 1)
                    tok = slice((it * W + u) * P, (it * W + u + 1) * P)
                    for k in range(KC):
                        ins = split_passes(nc, c.bank[4 + u][:, 0:P], [x[:, k, tok] for x in xnT],
                                           [x[:, k, tok] for x in c.ctxT], k == 0, k == KC - 1)
                    ins.then_inc(s_full, 1)
                for u in range(W):
                    pe.wait_ge(p_ready, it * W + (u + 1))
                    nc.tensor.transpose(c.bank[4 + u][:, P:2 * P], prob[:, u, :], c.ident).then_inc(pT_full, 1)
                for u in range(W):
                    pe.wait_ge(pT_low, it * W + (u + 1))
                    pe.wait_ge(cx_low, it * W + (u + 1))
                    if it == 0:
                        pe.wait_ge(norm.low, W + (u + 1))
                    else:
                        pe.wait_ge(added, u + 1)
                    split_passes(nc, c.bank[u][:, :], [x[:, u, :] for x in pT], [x[:, it * W + u, :] for x in cx],
                                 True, True).then_inc(out_full, 1)

        @block.scalar
        def _(act):
            norm.on_scalar(act)
            for it in range(B // W):
                for u in range(W):
                    act.wait_ge(max_ready, it * W + (u + 1))
                    nc.scalar.activation(prob[:, u, :], c.bank[4 + u][:, 0:P], ACT.Exp, bias=minus_max[:, u:u + 1],
                                         accum_out=sums[:, u:u + 1]).then_inc(p_ready, 1)
                for u in range(W):
                    act.wait_ge(pT_full, it * W + (u + 1))
                    nc.scalar.copy(pT[0][:, u, :], c.bank[4 + u][:, P:2 * P]).then_inc(pT_high, 1)

        @block.vector
        def _(dve):
            norm.stats_on_vector(dve)
            norm.parts_on_vector(dve)
            for it in range(B // W):
                for u in range(W):
                    dve.wait_ge(s_full, it * W + (u + 1))
                    nc.vector.tensor_reduce(minus_max[:, u:u + 1], c.bank[4 + u][:, 0:P], AX.X, ALU.max, negate=True).then_inc(max_ready, 1)
                for u in range(W):
                    dve.wait_ge(p_ready, it * W + (u + 1))
                    nc.vector.reciprocal(inv[:, u:u + 1], sums[:, u:u + 1]).then_inc(inv_ready, 1)
                for u in range(W):
                    dve.wait_ge(pT_high, it * W + (u + 1))
                    nc.vector.tensor_tensor(pT[1][:, u, :], c.bank[4 + u][:, P:2 * P], fp(pT[0][:, u, :]), ALU.subtract).then_inc(pT_low, 1)
                dve.wait_ge(inv_ready, it * W + W)
                for u in range(W):
                    dve.wait_ge(out_full, it * W + (u + 1))
                    xb = c.x[:, it * W + u, :]
                    nc.vector.scalar_tensor_tensor(xb, c.bank[u][:, :], inv[:, u:u + 1], xb, ALU.mult, ALU.add).then_inc(added, 1)
                    dve.wait_ge(added, it * W + (u + 1))
                    take_stats(nc, c, it * W + u)


def gated_ffn(nc, c, d):
    t = "f2_"
    with ExitStack() as ctx:
        def sb(name, shape, dt=F32):
            return ctx.enter_context(nc.sbuf_tensor(t + name, shape, dt))

        def pair(name, shape, dt=F32R):
            return sb(name + "_hi", shape, dt), sb(name + "_lo", shape, dt)

        def sem(name):
            return c.sem(t + name)

        xnT = pair("xnT", [P, KC, TOK])
        packed = sb("packed", [P, 3, D], I32)
        scales = sb("scales", [P, 3, D])
        shifts = sb("shifts", [P, 1 + D], I32)
        weight = sb("weight", [P, 3, D])
        parts = [pair(f"w{i}", [P, D]) for i in (1, 3, 2)]
        gate, hidden = sb("gate", [P, 2, HALF]), sb("hidden", [P, 2, HALF])
        hT = pair("hT", [P, TOK])
        shifts_loaded = sem("shifts_loaded")
        packed_loaded, scales_loaded = sem("packed_loaded"), sem("scales_loaded")
        shifted, unpacked = sem("shifted"), sem("unpacked")
        as_float = sem("as_float")
        weight_ready = sem("weight_ready")
        w_high, w_low = sem("w_high"), sem("w_low")
        w2_high, w2_low = sem("w2_high"), sem("w2_low")
        up_full = sem("up_full")
        gate_ready, hidden_ready, h_high, h_low = sem("gate_ready"), sem("hidden_ready"), sem("h_high"), sem("h_low")
        out_full, added = sem("out_full"), sem("added")
        norm = NormTransposed(nc, c, t + "norm_", ctx, xnT, [gate[:, 0, :], gate[:, 1, :], hidden[:, 0, :]])
        UP, OUT = c.bank[0:4], c.bank[4:8]
        LAST = HCH - 1
        block = ctx.enter_context(nc.Block())

        @block.sync
        def _(sp):
            sp.dma_start(shifts[:, :], d["shifts"]).then_inc(shifts_loaded, 16)

            def load_packed(ch):
                sp.dma_start(packed[:, :, :], d["L2_packed"][bass.ds(ch, 1)].rearrange("a p w n -> (a p) w n")).then_inc(packed_loaded, 16)

            def load_scales(ch):
                for half in range(2):
                    src = d["L2_s13"][bass.ds(ch, 1), half:half + 1].rearrange("a h w n -> (a h) w n")
                    sp.dma_start(scales[64 * half:64 * half + 64, 0:2, :],
                                 src.partition_broadcast(64).rearrange("p a w n -> p (a w) n")).then_inc(scales_loaded, 16)
                for q in range(4):
                    src = d["L2_s2"][bass.ds(ch, 1), q:q + 1].rearrange("a q n -> (a q) n")
                    sp.dma_start(scales[32 * q:32 * q + 32, 2, :],
                                 src.partition_broadcast(32).rearrange("p a n -> p (a n)")).then_inc(scales_loaded, 16)

            load_packed(0)
            load_scales(0)
            with sp.Fori(1, HCH) as ch:
                sp.wait_ge(weight_ready, ch * 3)
                load_packed(ch)
                load_scales(ch)

        @block.gpsimd
        def _(pool):
            def scale(ch):
                pool.wait_ge(scales_loaded, ch * 96 + 96)
                for w in range(3):
                    pool.wait_ge(as_float, ch * 3 + (w + 1))
                    nc.gpsimd.tensor_tensor(weight[:, w, :], weight[:, w, :], scales[:, w, :], ALU.mult).then_inc(weight_ready, 1)

            def low(ch):
                for w in range(3):
                    if w < 2:
                        pool.wait_ge(w_high, ch * 2 + (w + 1))
                    else:
                        pool.wait_ge(w2_high, ch + 1)
                    nc.gpsimd.tensor_tensor(parts[w][1][:, :], weight[:, w, :], fp(parts[w][0][:, :]),
                                            ALU.subtract).then_inc(w_low if w < 2 else w2_low, 1)

            norm.on_gpsimd(pool)
            with pool.Fori(0, HCH) as ch:
                scale(ch)
                low(ch)

        @block.tensor
        def _(pe):
            def chunk(ch):
                pe.wait_ge(w_low, ch * 2 + 2)
                for half in range(2):
                    pe.wait_ge(hidden_ready, ch * 2 + (half + 1))
                    for w in range(2):
                        for k in range(KC):
                            ins = split_passes(nc, UP[2 * half + w][:, :], [x[:, k * P:(k + 1) * P] for x in parts[w]],
                                               [x[:, k, half * HALF:(half + 1) * HALF] for x in xnT], k == 0, k == KC - 1)
                        ins.then_inc(up_full, 1)
                pe.wait_ge(w2_low, ch + 1)
                for b in range(B):
                    if b % HB == 0:
                        pe.wait_ge(h_low, ch * 2 + (b // HB + 1))
                    pe.wait_ge(added, ch * B + (b + 1))
                    split_passes(nc, OUT[b % 4][:, :], [x[:, b * P:(b + 1) * P] for x in hT], [x[:, :] for x in parts[2]],
                                 True, True).then_inc(out_full, 1)

            norm.on_tensor(pe)
            pe.wait_ge(norm.low, B)
            with pe.Fori(0, HCH) as ch:
                chunk(ch)

        @block.scalar
        def _(act):
            def high(ch, w):
                act.wait_ge(weight_ready, ch * 3 + (w + 1))
                nc.scalar.copy(parts[w][0][:, :], weight[:, w, :]).then_inc(w_high if w < 2 else w2_high, 1)

            def to_float(ch):
                for w in range(3):
                    act.wait_ge(unpacked, ch * 3 + (w + 1))
                    nc.scalar.copy(weight[:, w, :], packed[:, w, :]).then_inc(as_float, 1)

            def chunk(ch, more):
                if more:
                    act.wait_ge(w_low, ch * 2 + 2)
                    act.wait_ge(w2_low, ch + 1)
                    to_float(ch + 1)
                for half in range(2):
                    act.wait_ge(up_full, ch * 4 + (2 * half + 1))
                    nc.scalar.activation(gate[:, half, :], UP[2 * half][:, :], ACT.Silu).then_inc(gate_ready, 1)
                    act.wait_ge(hidden_ready, ch * 2 + (half + 3))
                    nc.scalar.copy(hT[0][:, half * HALF:(half + 1) * HALF], hidden[:, half, :]).then_inc(h_high, 1)
                if more:
                    act.wait_ge(up_full, ch * 4 + 4)
                    high(ch + 1, 0)
                    high(ch + 1, 1)
                    act.wait_ge(out_full, ch * B + B)
                    high(ch + 1, 2)

            norm.on_scalar(act, lambda: to_float(0))
            high(0, 0)
            high(0, 1)
            high(0, 2)
            with act.Fori(0, LAST) as ch:
                chunk(ch, True)
            chunk(LAST, False)

        @block.vector
        def _(dve):
            def unpack(ch):
                dve.wait_ge(packed_loaded, ch * 16 + 16)
                for w in range(3):
                    by = shifts[:, 0:1].broadcast_to([P, D]) if w < 2 else shifts[:, 1:1 + D]
                    nc.vector.tensor_tensor(packed[:, w, :], packed[:, w, :], by, ALU.logical_shift_left).then_inc(shifted, 1)
                for w in range(3):
                    dve.wait_ge(shifted, ch * 3 + (w + 1))
                    nc.vector.tensor_scalar(packed[:, w, :], packed[:, w, :], 28, None, ALU.arith_shift_right).then_inc(unpacked, 1)

            def chunk(ch, more):
                if more:
                    unpack(ch + 1)
                for half in range(2):
                    dve.wait_ge(up_full, ch * 4 + (2 * half + 2))
                    dve.wait_ge(gate_ready, ch * 2 + (half + 1))
                    nc.vector.tensor_tensor(hidden[:, half, :], UP[2 * half + 1][:, :], gate[:, half, :], ALU.mult).then_inc(hidden_ready, 1)
                    dve.wait_ge(h_high, ch * 2 + (half + 1))
                    cols = slice(half * HALF, (half + 1) * HALF)
                    nc.vector.tensor_tensor(hT[1][:, cols], hidden[:, half, :], fp(hT[0][:, cols]), ALU.subtract).then_inc(h_low, 1)
                for b in range(B):
                    dve.wait_ge(out_full, ch * B + (b + 1))
                    nc.vector.tensor_tensor(c.x[:, b, :], OUT[b % 4][:, :], c.x[:, b, :], ALU.add).then_inc(added, 1)
                    if not more:
                        dve.wait_ge(added, ch * B + (b + 5))
                        take_stats(nc, c, b)

            dve.sem_inc(hidden_ready, 2)
            dve.sem_inc(added, 4)
            def unpack_first():
                dve.wait_ge(shifts_loaded, 16)
                unpack(0)

            norm.stats_on_vector(dve)
            norm.parts_on_vector(dve, unpack_first)
            with dve.Fori(0, LAST) as ch:
                chunk(ch, True)
            chunk(LAST, False)


def wide_head_attention(nc, c, d):
    G, H = 8, 4
    t = "a3_"
    N = B
    TICKS = N + 5
    RING = 4
    LATE = {0: ["q4", "Q3"], 1: ["q5", "Q4"], 2: ["q6", "Q5"], 3: ["q7", "Q6"], 4: ["Q7"]}
    EARLY = {7: ["kv0"], 8: ["kv1", "kv2"], 9: ["kv3", "K0", "q0"], 10: ["K1", "K2", "q1", "Q0"],
             11: ["K3", "q2", "Q1"], 12: ["q3", "Q2"]}
    early = [x for n in sorted(EARLY) for x in EARLY[n]]
    body = []
    for n in range(TICKS):
        body += [f"o{n - 4}"] if 0 <= n - 4 < N else []
        body += LATE.get(n, []) + EARLY.get(n, [])
    assert len(body) % RING == 0

    def squared(names):
        return [x for x in names if x[0] in "kq"]

    def by_act(names):
        return [x for x in names if x[0] in "KQ"]

    assert len(squared(body)) % RING == 0

    class Where:

        def __init__(self, g, last=False):
            first = g is None
            names = early if first else [x for x in body if x not in early] if last else body

            def place(f):
                return Place(0 if first else g * len(f(body)) + len(f(early)), f(names))

            self.tile, self.high, self.squared = place(list), place(by_act), place(squared)
            self.bank_shift = RING - len(early) % RING if first else 0
            self.slot_shift = RING - len(squared(early)) % RING if first else 0
            self.names = names

        def bank(self, name):
            return M[(self.names.index(name) + self.bank_shift) % RING]

        def slot(self, name):
            return (squared(self.names).index(name) + self.slot_shift) % RING

    S, PT, OB, M = c.bank[0:2], c.bank[2], c.bank[3], c.bank[4:8]
    with ExitStack() as ctx:
        def sb(name, shape, dt=F32):
            return ctx.enter_context(nc.sbuf_tensor(t + name, shape, dt))

        def pair(name, shape, dt=F32R):
            return sb(name + "_hi", shape, dt), sb(name + "_lo", shape, dt)

        def sem(name):
            return c.sem(t + name)

        xnT = pair("xnT", [P, KC, TOK])
        raw = sb("raw", [P, 4 * D])
        wq, wo = pair("wq", [P, KC, H * P]), pair("wo", [P, H * D])
        wkv = pair("wkv", [P, KC, 2 * P])
        norms = sb("norms", [P, 2])
        mask = sb("mask", [P, P])
        sum_sq, var, factor = (sb(n, [P, RING, H]) for n in ("sum_sq", "var", "factor"))
        q_eps, k_eps = sb("q_eps", [P, H]), sb("k_eps", [P, 2])
        q_tok, k_tok = sb("q_tok", [P, 2, H, P]), sb("k_tok", [P, B, P])
        qT = pair("qT", [P, H, TOK])
        kT = pair("kT", [P, TOK])
        held_v = sb("held_v", [P, B, P])
        v = pair("v", [P, B, P])
        minus_max, sums, inv = sb("minus_max", [P, 3, H]), sb("sums", [P, 3, H]), sb("inv", [P, 3, H])
        prob = sb("prob", [P, 3, H, P])
        pT = pair("pT", [P, HALF])
        oT = pair("oT", [P, H, P])

        once_loaded = sem("once_loaded")
        raw_loaded = sem("raw_loaded")
        raw_high = sem("raw_high")
        raw_split = sem("raw_split")
        eps_set = sem("eps_set")
        m_full = sem("m_full")
        m_high = sem("m_high")
        m_free = sem("m_free")
        squares_summed = sem("squares_summed")
        var_ready, factor_ready = sem("var_ready"), sem("factor_ready")
        v_held = sem("v_held")
        v_high, v_low = sem("v_high"), sem("v_low")
        s_full = sem("s_full")
        s_free = sem("s_free")
        max_ready, exp_ready, inv_ready = sem("max_ready"), sem("exp_ready"), sem("inv_ready")
        p_ready = sem("p_ready")
        pT_full, pT_high = sem("pT_full"), sem("pT_high")
        pT_low = sem("pT_low")
        o_full, o_high = sem("o_full"), sem("o_high")
        o_low = sem("o_low")

        norm = NormTransposed(nc, c, t + "norm_", ctx, xnT, [prob[:, i, :, :].rearrange("p h n -> p (h n)") for i in range(3)])
        block = ctx.enter_context(nc.Block())

        @block.sync
        def _(sp):
            sp.dma_start(norms[:, :], d["L3_norms"]).then_inc(once_loaded, 16)
            sp.dma_start(mask[:, :], d["mask"]).then_inc(once_loaded, 16)

            def load(g, name, width):
                sp.dma_start(raw[:, 0:width], d[name][bass.ds(g, 1)].rearrange("a p n -> (a p) n")).then_inc(raw_loaded, 16)

            load(0, "L3_wkv", 2 * D)
            sp.wait_ge(raw_split, 1)
            load(0, "L3_wq", 4 * D)
            sp.wait_ge(raw_split, 2)
            load(0, "L3_wo", 4 * D)
            with sp.Fori(1, G) as g:
                sp.wait_ge(raw_split, g * 3)
                load(g, "L3_wkv", 2 * D)
                sp.wait_ge(raw_split, g * 3 + 1)
                load(g, "L3_wq", 4 * D)
                sp.wait_ge(raw_split, g * 3 + 2)
                load(g, "L3_wo", 4 * D)

        @block.gpsimd
        def _(pool):
            flat = {"wkv": [x[:, :, :].rearrange("p k n -> p (k n)") for x in wkv],
                    "wq": [x[:, :, :].rearrange("p k n -> p (k n)") for x in wq],
                    "wo": [x[:, :] for x in wo]}

            def split(g, slab, piece):
                first, pieces, nth = {"wkv": (0, 2, 1), "wq": (2, 4, 2), "wo": (6, 4, 3)}[slab]
                cols = slice(piece * D, (piece + 1) * D)
                if piece == 0:
                    pool.wait_ge(raw_loaded, g * 48 + nth * 16)
                high, low = (x[:, cols] for x in flat[slab])
                nc.gpsimd.tensor_tensor(high, raw[:, cols], c.ones[:, 0:1].broadcast_to([P, D]), ALU.mult).then_inc(raw_high, 1)
                pool.wait_ge(raw_high, g * 10 + (first + piece + 1))
                ins = nc.gpsimd.tensor_tensor(low, raw[:, cols], fp(high), ALU.subtract)
                if piece == pieces - 1:
                    ins.then_inc(raw_split, 1)

            def factors(w, name):
                if name[0] not in "kq":
                    return
                slot, eps = w.slot(name), q_eps if name[0] == "q" else k_eps
                width = eps.shape[1]
                pool.wait_ge(squares_summed, w.squared(name) + 1)
                nc.gpsimd.tensor_tensor(var[:, slot, 0:width], sum_sq[:, slot, 0:width], eps[:, :], ALU.add).then_inc(var_ready, 1)
                pool.wait_ge(var_ready, w.squared(name) + 1)
                nc.gpsimd.tensor_tensor(factor[:, slot, 0:width], var[:, slot, 0:width], c.minus_half[:, 0:width],
                                        ALU.pow).then_inc(factor_ready, 1)

            def attention(g, w, more):
                work = {0: [("wo", 0), ("wo", 1)], 1: [("wo", 2)], 2: [("wo", 3)]}
                if more:
                    work |= {4: [("wkv", 0), ("wkv", 1)], 5: [("wq", 0)], 6: [("wq", 1)], 7: [("wq", 2)], 8: [("wq", 3)]}
                for n in range(TICKS):
                    if 0 <= n - 1 < N:
                        b = n - 1
                        pool.wait_ge(inv_ready, g * N + (b + 1))
                        nc.gpsimd.tensor_tensor(prob[:, b % 3, :, :], prob[:, b % 3, :, :],
                                                inv[:, b % 3, :].unsqueeze(2).broadcast_to([P, H, P]), ALU.mult).then_inc(p_ready, 1)
                    if n > 0:
                        for name in LATE.get(n, []):
                            factors(w, name)
                    for slab, piece in work.get(n, []):
                        if (slab, piece) == ("wo", 0):
                            pool.wait_ge(m_free, w.tile.base + (RING + 1 - len(body) + body.index(f"o{N - 1}")))
                        if (slab, piece) == ("wq", 0):
                            pool.wait_ge(m_free, w.tile("q7") + (RING + 1))
                        split(g if slab == "wo" else g + 1, slab, piece)
                    if n == 0:
                        for name in LATE[0]:
                            factors(w, name)
                    if more:
                        for name in EARLY.get(n, []):
                            factors(w, name)

            nc.gpsimd.memset(q_eps[:, :], P * EPS).then_inc(eps_set, 1)
            nc.gpsimd.memset(k_eps[:, :], EPS).then_inc(eps_set, 1)
            pool.wait_ge(eps_set, 2)
            norm.on_gpsimd(pool)
            for piece in range(2):
                split(0, "wkv", piece)
            for piece in range(4):
                split(0, "wq", piece)
            for name in early:
                factors(Where(None), name)
            with pool.Fori(0, G - 1) as g:
                attention(g, Where(g), True)
            attention(G - 1, Where(G - 1, True), False)

        @block.tensor
        def _(pe):
            def tile(g, w, name):
                pe.wait_ge(m_free, w.tile(name) + 1)
                bank = w.bank(name)
                i = int(name[-1])
                if name[0] == "k":
                    if i == 0:
                        pe.wait_ge(raw_split, g * 3 + 1)
                    for u in range(2):
                        tok = slice((2 * i + u) * P, (2 * i + u + 1) * P)
                        for k in range(KC):
                            ins = split_passes(nc, bank[:, 2 * u * P:2 * (u + 1) * P], [x[:, k, tok] for x in c.ctxT],
                                               [x[:, k, :] for x in wkv], k == 0, k == KC - 1)
                elif name[0] == "q":
                    if i == 0:
                        pe.wait_ge(norm.low, B)
                        pe.wait_ge(raw_split, g * 3 + 2)
                    for k in range(KC):
                        ins = split_passes(nc, bank[:, :], [x[:, k, i * P:(i + 1) * P] for x in xnT],
                                           [x[:, k, :] for x in wq], k == 0, k == KC - 1)
                elif name[0] == "K":
                    pe.wait_ge(m_free, w.tile(f"kv{i}") + (RING + 1))
                    for u in range(2):
                        ins = nc.tensor.transpose(bank[:, u * P:(u + 1) * P], k_tok[:, 2 * i + u, :], c.ident)
                else:
                    pe.wait_ge(m_free, w.tile(f"q{i}") + (RING + 1) if i != 3 else w.tile.base + (RING - 1))
                    for h in range(H):
                        ins = nc.tensor.transpose(bank[:, h * P:(h + 1) * P], q_tok[:, i % 2, h, :], c.ident)
                ins.then_inc(m_full, 1)

            def attention(g, w, more):
                for n in range(TICKS):
                    if n < N:
                        if n < 3:
                            pe.wait_ge(m_free, w.tile.base + (RING - len(early) + 1 + early.index(f"Q{n}")))
                        else:
                            pe.wait_ge(m_free, w.tile(f"Q{n}") + (RING + 1))
                        pe.wait_ge(s_free, g * N + (n + 1))
                        tok = slice(n * P, (n + 1) * P)
                        for h in range(H):
                            ins = split_passes(nc, S[n % 2][:, h * P:(h + 1) * P], [x[:, h, tok] for x in qT], [x[:, tok] for x in kT],
                                               True, True)
                        ins.then_inc(s_full, 1)
                    if 0 <= n - 4 < N:
                        b = n - 4
                        if b == 0:
                            pe.wait_ge(raw_split, g * 3 + 3)
                        pe.wait_ge(m_free, w.tile(f"o{b}") + 1)
                        pe.wait_ge(o_low, g * N + (b + 2))
                        for h in range(H):
                            ins = split_passes(nc, w.bank(f"o{b}")[:, :], [x[:, h, :] for x in oT],
                                               [x[:, h * D:(h + 1) * D] for x in wo], h == 0, h == H - 1)
                        ins.then_inc(m_full, 1)
                    if 0 <= n - 3 < N:
                        b = n - 3
                        if b == 0:
                            pe.wait_ge(v_low, g * 2 + 2)
                        pe.wait_ge(pT_low, g * N + (b + 2))
                        pe.wait_ge(o_low, g * N + (b + 1))
                        split_passes(nc, OB[:, :], [x[:, b, :] for x in v], [x[:, :] for x in pT], True, True).then_inc(o_full, 1)
                    if 0 <= n - 2 < N:
                        b = n - 2
                        pe.wait_ge(p_ready, g * N + (b + 1))
                        pe.wait_ge(pT_low, g * N + (b + 1))
                        for h in range(H):
                            ins = nc.tensor.transpose(PT[:, h * P:(h + 1) * P], prob[:, b % 3, h, :], c.ident)
                        ins.then_inc(pT_full, 1)
                    for name in LATE.get(n, []):
                        tile(g, w, name)
                    if more:
                        for name in EARLY.get(n, []):
                            tile(g + 1, w, name)

            norm.on_tensor(pe)
            for name in early:
                tile(0, Where(None), name)
            with pe.Fori(0, G - 1) as g:
                attention(g, Where(g), True)
            attention(G - 1, Where(G - 1, True), False)

        @block.scalar
        def _(act):
            def tile(w, name):
                bank, i = w.bank(name), int(name[-1])
                act.wait_ge(m_full, w.tile(name) + 1)
                if name[0] == "q":
                    for h in range(H):
                        ins = nc.scalar.activation(q_tok[:, i % 2, h, :], bank[:, h * P:(h + 1) * P], ACT.Square,
                                                   accum_out=sum_sq[:, w.slot(name), h:h + 1])
                    ins.then_inc(squares_summed, 1)
                elif name[0] == "k":
                    for u in range(2):
                        ins = nc.scalar.activation(k_tok[:, 2 * i + u, :], bank[:, 2 * u * P:(2 * u + 1) * P], ACT.Square, scale=P ** -0.5,
                                                   accum_out=sum_sq[:, w.slot(name), u:u + 1])
                    ins.then_inc(squares_summed, 1)
                elif name[0] == "Q":
                    nc.scalar.activation(qT[0][:, :, i * P:(i + 1) * P], bank[:, :].rearrange("p (h n) -> p h n", h=H), ACT.Copy,
                                         scale=norms[:, 0:1]).then_inc(m_high, 1)
                else:
                    nc.scalar.activation(kT[0][:, 2 * i * P:2 * (i + 1) * P], bank[:, 0:2 * P], ACT.Copy,
                                         scale=norms[:, 1:2]).then_inc(m_high, 1)

            def values(w):
                act.wait_ge(m_free, w.tile("kv3") + (RING + 1))
                for half in range(2):
                    part = slice(half * HB, (half + 1) * HB)
                    nc.scalar.copy(v[0][:, part, :], held_v[:, part, :]).then_inc(v_high, 1)

            def attention(g, w, more):
                for n in range(TICKS):
                    if n < N:
                        act.wait_ge(max_ready, g * N + (n + 1))
                        for h in range(H):
                            ins = nc.scalar.activation(prob[:, n % 3, h, :], prob[:, n % 3, h, :], ACT.Exp,
                                                       bias=minus_max[:, n % 3, h:h + 1], accum_out=sums[:, n % 3, h:h + 1])
                        ins.then_inc(exp_ready, 1)
                    if 0 <= n - 3 < N:
                        b = n - 3
                        act.wait_ge(o_full, g * N + (b + 1))
                        nc.scalar.copy(oT[0][:, :, :], OB[:, :].rearrange("p (h t) -> p h t", h=H)).then_inc(o_high, 1)
                    if 0 <= n - 2 < N:
                        b = n - 2
                        act.wait_ge(pT_full, g * N + (b + 1))
                        nc.scalar.copy(pT[0][:, :], PT[:, :]).then_inc(pT_high, 1)
                    for name in LATE.get(n, []):
                        tile(w, name)
                    if more:
                        for name in EARLY.get(n, []):
                            tile(w, name)
                        if n == N + 3:
                            values(w)

            norm.on_scalar(act)
            act.wait_ge(once_loaded, 32)
            for name in early:
                tile(Where(None), name)
            values(Where(None))
            with act.Fori(0, G - 1) as g:
                attention(g, Where(g), True)
            attention(G - 1, Where(G - 1, True), False)

        @block.vector
        def _(dve):
            def tile(w, name):
                bank, i = w.bank(name), int(name[-1])
                if name[0] in "kq":
                    dve.wait_ge(factor_ready, w.squared(name) + 1)
                    slot = w.slot(name)
                if name[0] == "q":
                    nc.vector.tensor_tensor(q_tok[:, i % 2, :, :], bank[:, :].rearrange("p (h n) -> p h n", h=H),
                                            factor[:, slot, :].unsqueeze(2).broadcast_to([P, H, P]), ALU.mult).then_inc(m_free, 1)
                elif name[0] == "k":
                    both = bank[:, :].rearrange("p (b n) -> p b n", b=2)
                    nc.vector.tensor_copy(held_v[:, 2 * i:2 * i + 2, :], both[:, :, P:2 * P]).then_inc(v_held, 1)
                    nc.vector.tensor_tensor(k_tok[:, 2 * i:2 * i + 2, :], both[:, :, 0:P],
                                            factor[:, slot, 0:2].unsqueeze(2).broadcast_to([P, 2, P]), ALU.mult).then_inc(m_free, 1)
                elif name[0] == "Q":
                    tok = slice(i * P, (i + 1) * P)
                    dve.wait_ge(m_high, w.high(name) + 1)
                    nc.vector.scalar_tensor_tensor(qT[1][:, :, tok], bank[:, :].rearrange("p (h n) -> p h n", h=H), norms[:, 0:1],
                                                   fp(qT[0][:, :, tok]), ALU.mult, ALU.subtract).then_inc(m_free, 1)
                else:
                    cols = slice(2 * i * P, 2 * (i + 1) * P)
                    dve.wait_ge(m_high, w.high(name) + 1)
                    nc.vector.scalar_tensor_tensor(kT[1][:, cols], bank[:, 0:2 * P], norms[:, 1:2], fp(kT[0][:, cols]),
                                                   ALU.mult, ALU.subtract).then_inc(m_free, 1)

            def values(g):
                for half in range(2):
                    part = slice(half * HB, (half + 1) * HB)
                    dve.wait_ge(v_high, g * 2 + (half + 1))
                    nc.vector.tensor_tensor(v[1][:, part, :], held_v[:, part, :], fp(v[0][:, part, :]), ALU.subtract).then_inc(v_low, 1)

            def attention(g, w, more):
                late = []
                for n in range(TICKS):
                    if n < N:
                        r = n % 3
                        dve.wait_ge(s_full, g * N + (n + 1))
                        nc.vector.tensor_tensor(prob[:, r, :, :], S[n % 2][:, :].rearrange("p (h n) -> p h n", h=H),
                                                mask[:, :].unsqueeze(1).broadcast_to([P, H, P]), ALU.add).then_inc(s_free, 1)
                        dve.wait_ge(s_free, g * N + (n + 3))
                        nc.vector.tensor_reduce(minus_max[:, r, :], prob[:, r, :, :], AX.X, ALU.max, negate=True).then_inc(max_ready, 1)
                    for name in late:
                        tile(w, name)
                    if 0 <= n - 3 < N:
                        b = n - 3
                        dve.wait_ge(o_high, g * N + (b + 1))
                        nc.vector.tensor_tensor(oT[1][:, :, :], OB[:, :].rearrange("p (h t) -> p h t", h=H),
                                                fp(oT[0][:, :, :]), ALU.subtract).then_inc(o_low, 1)
                    if 0 <= n - 2 < N:
                        b = n - 2
                        dve.wait_ge(pT_high, g * N + (b + 1))
                        nc.vector.tensor_tensor(pT[1][:, :], PT[:, :], fp(pT[0][:, :]), ALU.subtract).then_inc(pT_low, 1)
                    if 0 <= n - 4 < N:
                        b = n - 4
                        dve.wait_ge(m_full, w.tile(f"o{b}") + 1)
                        nc.vector.tensor_tensor(c.x[:, b, :], w.bank(f"o{b}")[:, :], c.x[:, b, :], ALU.add).then_inc(m_free, 1)
                        if not more:
                            dve.wait_ge(m_free, w.tile(f"o{b}") + (RING + 1))
                            take_stats(nc, c, b)
                    if n < N:
                        dve.wait_ge(exp_ready, g * N + (n + 1))
                        nc.vector.reciprocal(inv[:, n % 3, :], sums[:, n % 3, :]).then_inc(inv_ready, 1)
                    late = LATE.get(n, []) + (EARLY.get(n, []) if more else [])
                    if more and n == N + 4:
                        values(g + 1)
                for name in late:
                    tile(w, name)

            dve.sem_inc(m_free, RING)
            dve.sem_inc(s_free, 2)
            dve.sem_inc(pT_low, 1)
            dve.sem_inc(o_low, 1)
            norm.stats_on_vector(dve)
            norm.parts_on_vector(dve)
            dve.wait_ge(once_loaded, 32)
            for name in early:
                tile(Where(None), name)
            values(0)
            with dve.Fori(0, G - 1) as g:
                attention(g, Where(g), True)
            attention(G - 1, Where(G - 1, True), False)


def build(nc, d):
    with ExitStack() as ctx:
        c = Chip()
        in_use = []

        def new_semaphore(name):
            in_use.append(nc.alloc_semaphore(name))
            return in_use[-1]

        def clear_semaphores():
            nc.clear_and_free_semaphores(in_use)
            in_use.clear()
            nc.all_engine_barrier()

        c.sem = new_semaphore
        c.x = ctx.enter_context(nc.sbuf_tensor("x", [P, B, D], F32))
        c.ctxT = [ctx.enter_context(nc.sbuf_tensor(f"ctxT_{n}", [P, KC, TOK], F32R)) for n in ("hi", "lo")]
        c.consts = ctx.enter_context(nc.sbuf_tensor("consts_sb", [P, CONSTS], F32))
        c.stats = ctx.enter_context(nc.sbuf_tensor("stats", [P, B, 6], F32))
        c.ones = ctx.enter_context(nc.sbuf_tensor("ones", [P, 1], F32))
        c.minus_half = ctx.enter_context(nc.sbuf_tensor("minus_half", [P, B], F32))
        c.ident = c.consts[:, IDENT:IDENT + P]
        c.bank = [ctx.enter_context(nc.psum_tensor(f"bank{n}", [P, HALF], F32)) for n in range(8)]
        steps = [
            lambda: small_head_attention(nc, c, d, 0),
            lambda: moe_ffn(nc, c, d, 0),
            lambda: small_head_attention(nc, c, d, 1),
            lambda: moe_ffn(nc, c, d, 1),
            lambda: context_attention(nc, c, d),
            lambda: gated_ffn(nc, c, d),
            lambda: wide_head_attention(nc, c, d),
            lambda: moe_ffn(nc, c, d, 3),
        ]
        for step in steps:
            step()
            clear_semaphores()
        store_output(nc, c, d)


def layouts(a):
    f = {n: np.asarray(v) for n, v in a.items()}
    o = {"x": f["x"], "consts": constants()}

    def rows(w, n=KC):
        return w.reshape(n, P, -1).transpose(1, 0, 2)

    ctx = f["ctx_4096"]
    o["ctxT"] = rows(ctx.transpose(2, 0, 1).reshape(D, TOK))
    o["ctx"] = ctx
    o["mask"] = f["mask_1x1xSxS2_ff0"].reshape(P, P)
    o["L0_wq"] = f["L0_xattn_Wq"].reshape(KC, P, 8, 4, 16).transpose(3, 1, 0, 2, 4).reshape(4, P, KC, P)
    o["L0_wkv"] = np.concatenate([rows(f["L0_xattn_Wk"]), rows(f["L0_xattn_Wv"])], 1)
    o["L0_wo"] = f["L0_xattn_Wo"].reshape(8, 4, 16, D).transpose(1, 0, 2, 3).reshape(4, P, D)
    o["L1_wqkv"] = np.stack([f[f"L1_xattn_W{n}"].reshape(KC, P, D) for n in "qkv"], 2)
    o["L1_wo"] = f["L1_xattn_Wo"].T.reshape(KC, P, D)
    o["L1_bias"] = np.stack([f[f"L1_xattn_b{n}"].reshape(KC, P).T for n in "qkv"], 2)
    o["L1_bo"] = f["L1_xattn_bo"].reshape(1, D)
    inter = np.broadcast_to(f["L1_xattn_interference"].reshape(KC, 4, 1, 4, 4), (KC, 4, 8, 4, 4))
    o["L1_inter"] = inter.reshape(KC, P, 4).transpose(1, 0, 2)
    o["L1_amp"] = np.broadcast_to(f["L1_xattn_amp"].reshape(1, 1), (P, 1))
    for n, a, r, bb in ((0, f["L0_ffn_A_stack"], "L0_ffn_W_router", f["L0_ffn_B_stack"].transpose(0, 2, 1)),
                        (1, f["L1_ffn_lora_A"].transpose(0, 2, 1), "L1_ffn_W_router", f["L1_ffn_lora_B"]),
                        (3, f["L3_ffn_A"], "L3_ffn_route_w", f["L3_ffn_Bw"].transpose(0, 2, 1))):
        o[f"L{n}_wa"] = rows(np.concatenate([a.reshape(LR, D), f[r]]).T)
        o[f"L{n}_wb"] = bb.reshape(LR, D)
        if n != 3:
            o[f"L{n}_w0"] = rows(f[f"L{n}_ffn_W_base"].T)
            o[f"L{n}_b0"] = f[f"L{n}_ffn_b_base"].reshape(1, D)
    o["L1_br"] = f["L1_ffn_b_router"].reshape(1, EXPERTS)

    pad = HCH * P - HIDDEN
    w13 = []
    for n in (1, 3):
        w = f[f"L2_ffn_w{n}"].reshape(HIDDEN, KC, 64).transpose(2, 1, 0)
        w = np.concatenate([w, w])
        w13.append(np.pad(w, ((0, 0), (0, 0), (0, pad))).reshape(P, KC, HCH, P).transpose(2, 0, 1, 3).reshape(HCH, P, D))
    blocks = HIDDEN // 32
    u = blocks * np.arange(D)[None, :] + np.arange(blocks)[:, None]
    w2 = f["L2_ffn_w2"].reshape(-1, 2, 32)[u // 4, u % 2]
    w2 = np.pad(w2.transpose(0, 2, 1).reshape(HIDDEN, D), ((0, pad), (0, 0))).reshape(HCH, P, D)
    o["L2_packed"] = np.stack([*w13, w2], 2)
    s13 = []
    for n in (1, 3):
        s = np.pad(f[f"L2_ffn_s{n}"].reshape(HIDDEN, KC, 2), ((0, pad), (0, 0), (0, 0)))
        s13.append(s.reshape(HCH, P, KC, 2).transpose(0, 3, 2, 1).reshape(HCH, 2, D))
    o["L2_s13"] = np.stack(s13, 2)
    o["L2_s2"] = np.pad(f["L2_ffn_s2"][u // 2], ((0, pad // 32), (0, 0))).reshape(HCH, 4, D)
    upper13 = np.arange(P)[:, None] < 64
    upper2 = (blocks * np.arange(D)[None, :] + np.arange(P)[:, None] // 32) % 4 < 2
    o["shifts"] = np.where(np.concatenate([upper13, upper2], 1), 24, 28).astype(np.int32)

    wq = f["L3_xattn_q_proj_w"].reshape(8, 4 * P, KC, P).transpose(0, 3, 2, 1)
    o["L3_wq"] = wq.reshape(8, P, 4 * D)
    wkv = [f[f"L3_xattn_{n}_proj_w"].reshape(8, P, KC, P).transpose(0, 3, 2, 1) for n in "kv"]
    o["L3_wkv"] = np.concatenate(wkv, 3).reshape(8, P, 2 * D)
    o["L3_wo"] = f["L3_xattn_o_proj_w"].reshape(D, 8, 4, P).transpose(1, 3, 2, 0).reshape(8, P, 4 * D)
    o["L3_norms"] = np.stack([f["L3_xattn_q_norm_w"], f["L3_xattn_k_norm_w"]], 1)
    return {n: np.ascontiguousarray(v) for n, v in o.items()}


def kernel(**inputs):
    import concourse.bacc as bacc
    from concourse.bass_utils import run_bass_kernel_spmd

    arrays = layouts(inputs)
    nc = bacc.Bacc("TRN2", target_bir_lowering=False, num_devices=1)
    d = {n: nc.dram_tensor(f"in_{n}", v.shape, mybir.dt.from_np(v.dtype), kind="ExternalInput").ap() for n, v in arrays.items()}
    d["out"] = nc.dram_tensor("out_x", (B, P, D), F32, kind="ExternalOutput").ap()
    build(nc, d)
    r = run_bass_kernel_spmd(nc, [{f"in_{n}": v for n, v in arrays.items()}], core_ids=[0])
    return r.results[0]["out_x"]
```
